# Optimizing a Trainium2 kernel written in Bass

```python
import numpy as np
import jax
import jax.numpy as jnp

def _softmax(x, axis=-1):
    return jax.nn.softmax(x, axis=axis)
def _gelu(x):
    return jax.nn.gelu(x, approximate=True)
def _silu(x):
    return jax.nn.silu(x)
def _sigmoid(x):
    return jax.nn.sigmoid(x)
def _layernorm(x, axis=-1, eps=1e-5):
    m = jnp.mean(x, axis=axis, keepdims=True)
    v = jnp.var(x, axis=axis, keepdims=True)
    return (x - m) / jnp.sqrt(v + eps)
def _scatter_add(tgt, idx, src, axis=0):
    return tgt.at[idx].add(src)
def _segment_sum(src, seg, n):
    return jax.ops.segment_sum(src, seg, n)

kernel_name = 'mk_adj_resnorm_d2_adj_512_e12ae5'

def setup_inputs(seed: int = 0):
    np.random.seed(seed)
    _w = jnp.asarray
    def _rec_inputs():
        import jax
        import jax.numpy as jnp
        _gk = jax.random.key(seed)
        x = -0.0005207 + 1.001 * jax.random.normal(jax.random.fold_in(_gk, 1), (4096, 512), jnp.float32)
        _w = (1.0 + jnp.arange(4096, dtype=jnp.float32)) ** -0.5
        _w = _w / _w.mean()
        _pij = jnp.clip(0.00390625 * _w[:, None] * _w[None, :], 0.0, 1.0)
        _a = jax.random.uniform(jax.random.fold_in(_gk, 2), (4096, 4096)) < _pij
        _af = _a.astype(jnp.float32)
        adj = _af
        return x, adj
    x, adj = _rec_inputs()
    def _L0_gnn_setup():
        import jax, jax.numpy as jnp
        import numpy as np
        N = 4096
        IN = 512
        D = 128
        H = 4
        SLOPE = 0.2
        NEG = -1e+30
        key = jax.random.key(seed)
        ks = jax.random.split(key, 8)
        stdv = 1.0 / np.sqrt(H * D)
        inputs = jax.random.normal(ks[0], (N, IN), jnp.float32)
        adjacency = jax.random.randint(ks[1], (N, N), 0, 2).astype(jnp.float32)
        weight = jax.random.uniform(ks[2], (IN, H * D), jnp.float32, -stdv, stdv)
        weight_u = jax.random.uniform(ks[3], (H, D, 1), jnp.float32, -1.0, 1.0)
        weight_v = jax.random.uniform(ks[4], (H, D, 1), jnp.float32, -1.0, 1.0)
        bias = jax.random.uniform(ks[5], (1, H * D), jnp.float32, -stdv, stdv)
        proj_w = jax.random.normal(ks[6], (IN, H * D), jnp.float32) * 0.02
        proj_b = jnp.zeros((H * D,), jnp.float32)
        return {'inputs': inputs, 'adjacency': adjacency, 'weight': weight, 'weight_u': weight_u, 'weight_v': weight_v, 'bias': bias, 'proj_w': proj_w, 'proj_b': proj_b}
    _L0_gnn_all = _L0_gnn_setup()
    _L0_gnn_in = {k: v for k, v in _L0_gnn_all.items() if k in ('weight', 'weight_u', 'weight_v', 'bias', 'proj_w', 'proj_b', )}
    del _L0_gnn_all

    def _L1_gnn_setup():
        import jax, jax.numpy as jnp
        import numpy as np
        N = 8192
        D_IN = 512
        D_OUT = 512
        NEG_BIG = -9000000000000000.0
        key = jax.random.key(seed)
        kx, ka, kw, kb, kn, ke = jax.random.split(key, 6)
        x = jax.random.normal(kx, (N, D_IN), dtype=jnp.float32)
        adj = (jax.random.uniform(ka, (N, N)) > 0.9).astype(jnp.float32)
        stdv = 1.0 / np.sqrt(D_OUT)
        weight = jax.random.uniform(kw, (D_IN, D_OUT), minval=-stdv, maxval=stdv, dtype=jnp.float32)
        bias = jax.random.uniform(kb, (D_OUT,), minval=-stdv, maxval=stdv, dtype=jnp.float32)
        node_w = jax.random.uniform(kn, (D_IN, 1), minval=-1.0, maxval=1.0, dtype=jnp.float32)
        stdv_e = 1.0 / np.sqrt(D_IN)
        edge_w = jax.random.uniform(ke, (D_IN, D_IN), minval=-stdv_e, maxval=stdv_e, dtype=jnp.float32)
        return {'x': x, 'adj': adj, 'weight': weight, 'bias': bias, 'node_w': node_w, 'edge_w': edge_w}
    _L1_gnn_all = _L1_gnn_setup()
    _L1_gnn_in = {k: v for k, v in _L1_gnn_all.items() if k in ('weight', 'bias', 'node_w', 'edge_w', )}
    del _L1_gnn_all

    return {
        "x": x,
        "adj": adj,
        "L0_gnn_weight": _L0_gnn_in["weight"],
        "L0_gnn_weight_u": _L0_gnn_in["weight_u"],
        "L0_gnn_weight_v": _L0_gnn_in["weight_v"],
        "L0_gnn_bias": _L0_gnn_in["bias"],
        "L0_gnn_proj_w": _L0_gnn_in["proj_w"],
        "L0_gnn_proj_b": _L0_gnn_in["proj_b"],
        "L1_gnn_weight": _L1_gnn_in["weight"],
        "L1_gnn_bias": _L1_gnn_in["bias"],
        "L1_gnn_node_w": _L1_gnn_in["node_w"],
        "L1_gnn_edge_w": _L1_gnn_in["edge_w"],
    }

def reference(x, adj, L0_gnn_weight, L0_gnn_weight_u, L0_gnn_weight_v, L0_gnn_bias, L0_gnn_proj_w, L0_gnn_proj_b, L1_gnn_weight, L1_gnn_bias, L1_gnn_node_w, L1_gnn_edge_w):
    import jax
    import jax.numpy as jnp
    def _L0_gnn_ref(inputs, adjacency, weight, weight_u, weight_v, bias, proj_w, proj_b):
        import jax, jax.numpy as jnp
        import numpy as np
        N = 4096
        IN = 512
        D = 128
        H = 4
        SLOPE = 0.2
        NEG = -1e+30
        support = (inputs @ weight).reshape(N, H, D).transpose(1, 0, 2)
        f1 = jnp.einsum('hnd,hdo->hn', support, weight_u)[:, None, :]
        f2 = jnp.einsum('hnd,hdo->hn', support, weight_v)[:, :, None]
        logits = f1 + f2
        w = jnp.where(logits >= 0, logits, SLOPE * logits)
        masked = w * adjacency[None]
        mask = masked != 0
        z = jnp.where(mask, masked, NEG)
        attn = jax.nn.softmax(z, axis=-1) * mask
        out = jnp.einsum('hij,hjd->hid', attn, support)
        out = out.transpose(1, 0, 2).reshape(N, H * D)
        out = out + bias
        out = out + inputs @ proj_w + proj_b
        return out

    def _L1_gnn_ref(x, adj, weight, bias, node_w, edge_w):
        import jax, jax.numpy as jnp
        import numpy as np
        N = 8192
        D_IN = 512
        D_OUT = 512
        NEG_BIG = -9000000000000000.0
        node_att = jax.nn.softmax(x @ node_w, axis=0)
        h = x @ edge_w
        e = h @ h.T
        e = jnp.where(adj > 0, e, NEG_BIG)
        edge_att = jax.nn.softmax(e, axis=1)
        combined_att = node_att * edge_att
        support = x @ weight
        output = adj * combined_att @ support
        return output + bias

    x = _layernorm(x + _L0_gnn_ref(x, adj, L0_gnn_weight, L0_gnn_weight_u, L0_gnn_weight_v, L0_gnn_bias, L0_gnn_proj_w, L0_gnn_proj_b), axis=-1)
    x = _layernorm(x + _L1_gnn_ref(x, adj, L1_gnn_weight, L1_gnn_bias, L1_gnn_node_w, L1_gnn_edge_w), axis=-1)
    return x


_drawn_inputs = setup_inputs


def setup_inputs(seed=0):
    import zlib

    import numpy as np

    out = dict(_drawn_inputs(seed))
    spreads = {'L0_gnn_proj_b': (0.0, 0.1)}
    factors = {}
    for name, (base, spread) in spreads.items():
        noise = np.random.default_rng([zlib.crc32(name.encode()), seed]).standard_normal(out[name].shape)
        drawn = base * np.exp(spread * noise) if base else spread * noise
        out[name] = jnp.asarray(drawn.astype(out[name].dtype))
    for name, factor in factors.items():
        out[name] = (out[name] * factor).astype(out[name].dtype)
    return out
```

```python
import numpy as np
import concourse.bass as bass
from concourse import mybir
from contextlib import ExitStack

FP32 = mybir.dt.float32
F16 = mybir.dt.float16
BF16 = mybir.dt.bfloat16
U32 = mybir.dt.uint32
ALU = mybir.AluOpType
ACT = mybir.ActivationFunctionType
AX = mybir.AxisListType
RMAX = bass.bass_isa.ReduceOp.max
RADD = bass.bass_isa.ReduceOp.add

P = 128
N = 4096
D = 512
H = 4
DH = D // H
NT = N // P
KT = D // P
IC = 512
NIC = N // IC
IT = IC // P
XW = DH + 1
XP = DH + 2
NQ = NT // 4
EPS = 1e-5
SHIFT = 40.0
DEN = 1024.0
SLOPE = 0.2
BIG = 3.0e38
PSCALE = 8.317766166719343


class Map:

    def __init__(self, nc, at):
        self.nc, self.at = nc, at

    def __call__(self, name, shape, dt, width):
        size = int(np.prod(shape[1:])) * width
        t = self.nc.alloc_sbuf_tensor_at(name, shape, dt, offset=self.at)
        self.at += (size + 31) // 32 * 32
        return t


def build(nc, x, adj, w0, wu, wv, b0, pw, pb, w1, b1, nw, ew, out):
    ctx = ExitStack()
    with ctx:
        def sem(name):
            return ctx.enter_context(nc.semaphore(name))

        y0_dram = nc.dram_tensor("y0_scratch", [N, D], FP32).ap()
        x1_dram = nc.dram_tensor("x1_scratch", [N, D], FP32).ap()
        f2_dram = nc.dram_tensor("f2_scratch", [H * NT, P], FP32).ap()

        keep = Map(nc, (nc.sbuf_base + 31) // 32 * 32)
        k = Kept()
        k.ident = keep("ident", [P, P], FP32, 4)
        k.f12 = keep("f12", [P, 2 * H, NT], FP32, 4)
        k.expo = keep("expo", [P, 4, H, NT], FP32, 4)
        k.qm = keep("qm", [P, 2, H, NT], FP32, 4)
        k.score = keep("score", [P, NT], FP32, 4)
        k.small = keep("small", [P, 32], FP32, 4)
        k.at = keep.at
        k.bank = [ctx.enter_context(nc.psum_tensor(f"bank{i}", [P, 512], FP32)) for i in range(8)]

        project0(nc, sem, k, x, w0, wu, wv, b0, pw, pb, y0_dram)
        scale_support(nc, sem, k, f2_dram)
        attend0(nc, sem, k, adj, y0_dram, f2_dram, x1_dram)
        project1(nc, sem, k, w1, nw, ew, x1_dram)
        attend1(nc, sem, k, adj, b1, x1_dram, out)


class Kept:
    pass


def wait_apart(eng, done, value, passed):
    eng.wait_ge(done, value)
    eng.sem_inc(passed, 1)


def flat(ap):
    return ap.rearrange("p a n -> p (a n)")


X_BYTES = H * NT * 2 * 2 * XP * 2


def project0(nc, sem, k, x, w0, wu, wv, b0, pw, pb, y0_dram):
    k.sup = nc.alloc_sbuf_tensor_at("sup", [P, NT, D], FP32, offset=k.at + (X_BYTES + 31) // 32 * 32)
    m = Map(nc, k.at)
    w_sb = m("w_sb", [P, KT, D], FP32, 4)
    p_sb = m("p_sb", [P, KT, D], FP32, 4)
    u_bc = m("u_bc", [P, 2, D], FP32, 4)
    bias = m("bias", [P, 2, D], FP32, 4)
    x_in = m("x_in", [P, 4, D], FP32, 4)
    xb = m("xb", [P, 4, D], FP32, 4)
    xT = m("xT", [P, 2, KT, P], FP32, 4)
    prod = m("prod", [P, 2, 2 * H, DH], FP32, 4)
    y_sb = m("y_sb", [P, 4, D], FP32, 4)
    smax = m("smax", [P, NT], FP32, 4)
    ident, bank = k.ident, k.bank

    w_in, c_in, id_done, bias_done = sem("p0_w_in"), sem("p0_c_in"), sem("p0_id_done"), sem("p0_bias_done")
    x_loaded = [sem(f"p0_x_loaded{i}") for i in range(4)]
    y_stored = [sem(f"p0_y_stored{i}") for i in range(4)]
    passed = [sem(f"p0_passed{i}") for i in range(3)]
    xb_done, xT_ps, xT_done, mm_s, mm_y = (sem("p0_" + n) for n in ("xb_done", "xT_ps", "xT_done", "mm_s", "mm_y"))
    s_done, y_done, prod_done, f_done = (sem("p0_" + n) for n in ("s_done", "y_done", "prod_done", "f_done"))

    x_t = x.rearrange("(t p) d -> p t d", p=P)
    y_t = y0_dram.rearrange("(t p) d -> p t d", p=P)

    with nc.Block() as block:

        @block.sync
        def _(sp):
            sp.dma_start(w_sb[:], w0.rearrange("(k p) d -> p k d", p=P)).then_inc(w_in, 16)
            sp.dma_start(p_sb[:], pw.rearrange("(k p) d -> p k d", p=P)).then_inc(w_in, 16)
            for u in range(4):
                sp.dma_start(x_in[:, u, :], x_t[:, u, :]).then_inc(x_loaded[u], 16)
            sp.dma_start(u_bc[:, 0, :], wu.rearrange("h d o -> (h d o)").partition_broadcast(P)).then_inc(c_in, 16)
            sp.dma_start(u_bc[:, 1, :], wv.rearrange("h d o -> (h d o)").partition_broadcast(P)).then_inc(c_in, 16)
            sp.dma_start(bias[:, 0, :], b0.rearrange("a d -> (a d)").partition_broadcast(P)).then_inc(c_in, 16)
            sp.dma_start(bias[:, 1, :], pb.partition_broadcast(P)).then_inc(c_in, 16)
            with sp.Fori(1, NT // 4) as q:
                for u in range(4):
                    wait_apart(sp, y_done, q * 4 + u + 1, passed[0])
                    sp.dma_start(y_t[:, bass.ds(q * 4 + (u - 4), 1), :], y_sb[:, u:u + 1, :]).then_inc(y_stored[u], 16)
                    sp.dma_start(x_in[:, u:u + 1, :], x_t[:, bass.ds(q * 4 + u, 1), :]).then_inc(x_loaded[u], 16)
            for u in range(4):
                sp.wait_ge(y_done, NT + u + 1)
                sp.dma_start(y_t[:, NT - 4 + u, :], y_sb[:, u, :]).then_inc(y_stored[u], 16)
            for u in range(4):
                sp.wait_ge(y_stored[u], NT // 4 * 16)

        @block.gpsimd
        def _(pool):
            nc.gpsimd.memset(ident[:], 0.0).then_inc(id_done, 1)
            pool.wait_ge(id_done, 1)
            nc.gpsimd.affine_select(out=ident[:], in_=ident[:], compare_op=ALU.not_equal, fill=1.0, base=0,
                                    pattern=[[-1, P]], channel_multiplier=1).then_inc(id_done, 1)
            pool.wait_ge(c_in, 64)
            nc.gpsimd.tensor_tensor(out=bias[:, 0, :], in0=bias[:, 0, :], in1=bias[:, 1, :],
                                    op=ALU.add).then_inc(bias_done, 1)
            pool.wait_ge(bias_done, 1)
            with pool.Fori(0, NT // 4) as q:
                for u in range(4):
                    pool.wait_ge(x_loaded[u], q * 16 + 16)
                    pool.wait_ge(y_done, q * 4 + u + 1)
                    nc.gpsimd.tensor_tensor(out=xb[:, u, :], in0=x_in[:, u, :], in1=bias[:, 0, :],
                                            op=ALU.add).then_inc(xb_done, 1)

        def transpose_tile(pe, q, u):
            pe.wait_ge(x_loaded[u], q * 16 + 16)
            pe.wait_ge(xT_done, q * 4 + u + 1)
            for j in range(KT):
                last = nc.tensor.transpose(bank[u % 2][:, j * P:(j + 1) * P], x_in[:, u, j * P:(j + 1) * P], ident[:])
            last.then_inc(xT_ps, 1)

        def project_tile(pe, q, u):
            pe.wait_ge(xT_done, q * 4 + u + 3)
            pe.wait_ge(s_done, q * 4 + u + 1)
            for j in range(KT):
                last = nc.tensor.matmul(bank[2 + u % 2][:], xT[:, u % 2, j, :], w_sb[:, j, :],
                                        start=(j == 0), stop=(j == KT - 1))
            last.then_inc(mm_s, 1)
            pe.wait_ge(y_done, q * 4 + u + 3)
            for j in range(KT):
                last = nc.tensor.matmul(bank[4 + u % 2][:], xT[:, u % 2, j, :], p_sb[:, j, :],
                                        start=(j == 0), stop=(j == KT - 1))
            last.then_inc(mm_y, 1)

        @block.tensor
        def _(pe):
            pe.wait_ge(id_done, 2)
            pe.wait_ge(w_in, 32)
            transpose_tile(pe, 0, 0)
            with pe.Fori(0, NT // 4 - 1) as q:
                for u in range(4):
                    transpose_tile(pe, q + (u + 1) // 4, (u + 1) % 4)
                    project_tile(pe, q, u)
            for u in range(4):
                if u < 3:
                    transpose_tile(pe, NT // 4 - 1, u + 1)
                project_tile(pe, NT // 4 - 1, u)

        @block.scalar
        def _(act):
            act.sem_inc(xT_done, 2)
            act.sem_inc(s_done, 2)
            act.sem_inc(mm_y, 2)

            def copy_xT(q, u):
                act.wait_ge(xT_ps, q * 4 + u + 1)
                act.wait_ge(mm_y, q * 4 + u + 1)
                nc.scalar.activation(xT[:, u % 2, :, :].rearrange("p k n -> p (k n)"), bank[u % 2][:],
                                     ACT.Copy).then_inc(xT_done, 1)

            def copy_s(q, u):
                act.wait_ge(mm_s, q * 4 + u + 1)
                nc.scalar.activation(flat(k.sup[:, bass.ds(q * 4 + u, 1), :]), bank[2 + u % 2][:],
                                     ACT.Copy).then_inc(s_done, 1)

            copy_xT(0, 0)
            with act.Fori(0, NT // 4 - 1) as q:
                for u in range(4):
                    copy_xT(q + (u + 1) // 4, (u + 1) % 4)
                    copy_s(q, u)
            for u in range(4):
                if u < 3:
                    copy_xT(NT // 4 - 1, u + 1)
                copy_s(NT // 4 - 1, u)

        @block.vector
        def _(dve):
            dve.sem_inc(y_done, 4)
            dve.wait_ge(c_in, 64)

            def tile(q, u, first):
                t = q * 4 + u
                dve.wait_ge(s_done, t + 3)
                st = flat(k.sup[:, bass.ds(t, 1), :]) if not isinstance(t, int) else k.sup[:, t, :]
                for i in range(2):
                    last = nc.vector.tensor_tensor(
                        out=prod[:, u % 2, i * H:(i + 1) * H, :].rearrange("p h d -> p (h d)"), in0=st,
                        in1=u_bc[:, i, :], op=ALU.mult)
                last.then_inc(prod_done, 1)
                nc.vector.tensor_reduce(out=smax[:, bass.ds(t, 1)], in_=st, axis=AX.X, op=ALU.max,
                                        apply_absolute_value=True).then_inc(f_done, 1)
                dve.wait_ge(prod_done, t + 1)
                nc.vector.tensor_reduce(out=k.f12[:, :, bass.ds(t, 1)], in_=prod[:, u % 2, :, :], axis=AX.X,
                                        op=ALU.add).then_inc(f_done, 1)
                dve.wait_ge(mm_y, t + 3)
                dve.wait_ge(xb_done, t + 1)
                if not first:
                    dve.wait_ge(y_stored[u], q * 16)
                nc.vector.tensor_tensor(out=y_sb[:, u, :], in0=bank[4 + u % 2][:], in1=xb[:, u, :],
                                        op=ALU.add).then_inc(y_done, 1)

            for u in range(4):
                tile(0, u, True)
            with dve.Fori(1, NT // 4) as q:
                for u in range(4):
                    tile(q, u, False)
            dve.wait_ge(f_done, 2 * NT)
            nc.vector.tensor_reduce(out=k.small[:, 4:5], in_=smax[:], axis=AX.X, op=ALU.max).then_inc(f_done, 1)
            dve.wait_ge(f_done, 2 * NT + 1)


def power_of_two(link, out, peak, room):
    link(lambda v: v.tensor_scalar(out, peak, 1e-30, None, ALU.max))
    link(lambda v: v.reciprocal(out, out))
    link(lambda v: v.tensor_scalar(out, out, room, None, ALU.mult))
    link(lambda v: v.tensor_scalar(out.bitcast(U32), out.bitcast(U32), 0x7F800000, None, ALU.bitwise_and))


def linker(nc, dve, done):
    count = [0]

    def link(step):
        step(nc.vector).then_inc(done, 1)
        count[0] += 1
        dve.wait_ge(done, count[0])
    return link


def scale_support(nc, sem, k, f2_dram):
    k.xs = nc.alloc_sbuf_tensor_at("xs", [P, H, NT, 2, 2, XP], F16, offset=k.at)
    m = Map(nc, k.at + (X_BYTES + 31) // 32 * 32 + NT * D * 4)
    t1 = m("t1", [P, 2, 2, D], FP32, 4)
    arg = m("arg", [P, 2, H, NT], FP32, 4)
    f2r = k.expo[:, 3].rearrange("p h t -> p (h t)")
    qb = k.expo[:, 2].rearrange("p h t -> p (h t)").bitcast(BF16).rearrange("p (a h t) -> p a h t", a=2, h=H)
    small, bank, ident, f12 = k.small, k.bank, k.ident, k.f12
    peak, gmax, scale, kout = small[:, 0:5], small[:, 5:10], small[:, 10:11], small[:, 11:12]

    steps, g_out, e_done, f2_ps, f2_sb, f2_out = (sem("p1_" + n) for n in
                                                  ("steps", "g_out", "e_done", "f2_ps", "f2_sb", "f2_out"))
    local_done, arg_done, cs_done, t1_dve, t1_pool, hi_done, lo_done, den_done = (sem("p1_" + n) for n in (
        "local_done", "arg_done", "cs_done", "t1_dve", "t1_pool", "hi_done", "lo_done", "den_done"))

    def fac(mm, t):
        return arg[:, mm, :, bass.ds(t, 1)].broadcast_to([P, H, DH])

    def half(t, mm, part):
        return k.xs[:, :, bass.ds(t, 1), mm, part, 0:DH].rearrange("p h a d -> p (h a) d")

    def sup(t):
        return flat(k.sup[:, bass.ds(t, 1), :]).rearrange("p (h d) -> p h d", h=H)

    with nc.Block() as block:

        @block.tensor
        def _(pe):
            nc.tensor.transpose(bank[0][:, 0:P], f12[:, H:2 * H, :].rearrange("p h t -> p (h t)"),
                                ident[:]).then_inc(f2_ps, 1)

        @block.sync
        def _(sp):
            sp.wait_ge(f2_sb, 1)
            sp.dma_start(f2_dram, f2r).then_inc(f2_out, 16)
            sp.wait_ge(f2_out, 16)

        @block.gpsimd
        def _(pool):
            pool.wait_ge(local_done, 1)
            nc.gpsimd.partition_all_reduce(gmax, peak, P, RMAX).then_inc(g_out, 1)
            pool.wait_ge(cs_done, 1)
            with pool.Fori(0, NT // 2) as i:
                for u in range(2):
                    pool.wait_ge(lo_done, i * 4 + 2 * u + 2)
                    nc.gpsimd.tensor_tensor(out=t1[:, u, 1, :].rearrange("p (h d) -> p h d", h=H),
                                            in0=sup(i * 2 + u), in1=fac(1, i * 2 + u), op=ALU.mult
                                            ).then_inc(t1_pool, 1)

        @block.scalar
        def _(act):
            act.wait_ge(f2_ps, 1)
            nc.scalar.activation(f2r, bank[0][:, 0:P], ACT.Copy).then_inc(f2_sb, 1)
            act.wait_ge(arg_done, 1)
            nc.scalar.activation(k.expo[:, 0:2].rearrange("p a h t -> p (a h t)"),
                                 arg[:].rearrange("p a h t -> p (a h t)"), ACT.Exp).then_inc(e_done, 1)
            act.wait_ge(arg_done, 2)
            act.wait_ge(f2_out, 16)
            nc.scalar.activation(k.expo[:, 2:4].rearrange("p a h t -> p (a h t)"),
                                 arg[:].rearrange("p a h t -> p (a h t)"), ACT.Exp).then_inc(e_done, 1)
            with act.Fori(0, NT // 2) as i:
                for u in range(2):
                    t = i * 2 + u
                    for mm, ready in ((0, t1_dve), (1, t1_pool)):
                        act.wait_ge(ready, t + 1)
                        nc.scalar.activation(half(t, mm, 0), t1[:, u, mm, :].rearrange("p (h d) -> p h d", h=H),
                                             ACT.Copy).then_inc(hi_done, 1)

        @block.vector
        def _(dve):
            link = linker(nc, dve, steps)
            link(lambda v: v.tensor_reduce(out=peak[:, 0:4], in_=f12[:, 0:H, :], axis=AX.X, op=ALU.max))
            dve.sem_inc(local_done, 1)
            dve.sem_inc(lo_done, 4)
            dve.wait_ge(g_out, 1)
            for h in range(H):
                c = gmax[:, h:h + 1]
                nc.vector.tensor_scalar(arg[:, 0, h, :], f12[:, h, :], c, SHIFT, ALU.subtract, ALU.add)
                link(lambda v: v.tensor_scalar(arg[:, 1, h, :], f12[:, h, :], c, SLOPE, ALU.subtract, ALU.mult))
            link(lambda v: v.tensor_scalar(arg[:, 1], arg[:, 1], SHIFT, None, ALU.add))
            dve.sem_inc(arg_done, 1)
            power_of_two(link, scale, gmax[:, 4:5], 16384.0)
            link(lambda v: v.reciprocal(kout, scale))
            link(lambda v: v.tensor_scalar(kout, kout, DEN, None, ALU.mult))
            dve.wait_ge(e_done, 1)
            key = k.expo[:, 0:2]
            link(lambda v: v.tensor_copy(qb, key))
            link(lambda v: v.tensor_copy(k.qm[:], qb))
            link(lambda v: v.tensor_scalar(arg[:], k.qm[:], 1e-37, None, ALU.max))
            link(lambda v: v.reciprocal(arg[:], arg[:]))
            link(lambda v: v.tensor_tensor(out=key, in0=key, in1=arg[:], op=ALU.mult))
            link(lambda v: v.tensor_scalar(k.qm[:, 1], k.qm[:, 1], -1.0, None, ALU.mult))
            for h in range(H):
                link(lambda v: v.tensor_scalar(arg[:, 0, h, :], f12[:, H + h, :], gmax[:, h:h + 1], 1.0 - SLOPE,
                                               ALU.add, ALU.mult))
            link(lambda v: v.tensor_scalar(arg[:, 1], arg[:, 0], -1.0, 0.0, ALU.mult, ALU.min))
            link(lambda v: v.tensor_scalar(arg[:, 0], arg[:, 0], 0.0, None, ALU.min))
            dve.sem_inc(arg_done, 1)
            dve.wait_ge(e_done, 2)
            link(lambda v: v.tensor_scalar(arg[:], key, DEN, None, ALU.mult))
            for mm in range(2):
                link(lambda v: v.tensor_copy(k.xs[:, :, :, mm, 0, DH], arg[:, mm]))
                link(lambda v: v.tensor_tensor(out=k.xs[:, :, :, mm, 1, DH], in0=arg[:, mm],
                                               in1=k.xs[:, :, :, mm, 0, DH], op=ALU.subtract))
            link(lambda v: v.tensor_scalar(arg[:], key, scale, None, ALU.mult))
            dve.sem_inc(cs_done, 1)

            def scaled(t, u):
                dve.wait_ge(lo_done, t * 2 + 1)
                nc.vector.tensor_tensor(out=t1[:, u, 0, :].rearrange("p (h d) -> p h d", h=H), in0=sup(t),
                                        in1=fac(0, t), op=ALU.mult).then_inc(t1_dve, 1)

            def low(t, u):
                for mm in range(2):
                    dve.wait_ge(hi_done, t * 2 + mm + 1)
                    nc.vector.tensor_tensor(out=half(t, mm, 1), in0=t1[:, u, mm, :].rearrange("p (h d) -> p h d", h=H),
                                            in1=half(t, mm, 0), op=ALU.subtract).then_inc(lo_done, 1)

            scaled(0, 0)
            with dve.Fori(0, NT // 2 - 1) as i:
                for u in range(2):
                    scaled(i * 2 + u + 1, (u + 1) % 2)
                    low(i * 2 + u, u)
            scaled(NT - 1, 1)
            low(NT - 2, 0)
            low(NT - 1, 1)


def attend0(nc, sem, k, adj, y0_dram, f2_dram, x1_dram):
    m = Map(nc, k.at + (X_BYTES + 31) // 32 * 32)
    aT = m("aT", [P, NT, IC], BF16, 2)
    f2b = m("f2b", [P, H, IC], FP32, 4)
    sign = m("sign", [P, 2, 2, IC], BF16, 2)
    mask = m("mask", [P, 4, 2, IC], BF16, 2)
    stage = m("stage", [P, 2, IT, 2 * P], FP32, 4)
    y = m("y", [P, IT, D], FP32, 4)
    part = m("part", [P, IT, XW], FP32, 4)
    dinv = m("dinv", [P, IT], FP32, 4)
    stats = m("stats", [P, IT, 6], FP32, 4)
    mv = m("mv", [P, IT, 2], FP32, 4)
    rstd = m("rstd", [P, IT], FP32, 4)
    assert m.at <= nc.sbuf_usable_end
    bank, ident, xs = k.bank, k.ident, k.xs
    acc = [bank[0:3], bank[3:6]]
    kout = k.small[:, 11:12]
    NP = NT // 2

    def slot(s, i):
        return acc[s][i // 3][:, i % 3 * XW:i % 3 * XW + XW]

    names = ("sign_done", "sign_free", "mask_done", "mask_free", "acc_done", "part_done", "acc_free", "aT_ps0",
             "aT_ps1", "aT_done0", "aT_done1", "stage_free", "f2_free", "y_loaded", "y_final", "y_stored",
             "b_done", "sum_done", "den_done", "stat_done", "mv_done", "std_done", "inv_done")
    s = {n: sem("a0_" + n) for n in names}
    passed = [sem(f"a0_passed{i}") for i in range(3)]
    stage_in = [sem(f"a0_stage_in{i}") for i in range(2)]
    f2_in = [sem(f"a0_f2_in{h}") for h in range(H)]
    aT_ps, aT_done = [s["aT_ps0"], s["aT_ps1"]], [s["aT_done0"], s["aT_done1"]]

    adj_r = adj.rearrange("(c i p) n -> p c i n", i=IT, p=P)
    y0_r = y0_dram.rearrange("(c i p) d -> p c i d", i=IT, p=P)
    x1_r = x1_dram.rearrange("(c i p) d -> p c i d", i=IT, p=P)
    f2_r = f2_dram.rearrange("(h c i) p -> h c (i p)", h=H, i=IT)

    with nc.Block() as block:

        @block.sync
        def _(sp):
            def load_adj(c):
                with sp.Fori(0, NP // 2) as q:
                    for u in range(2):
                        wait_apart(sp, s["stage_free"], c * NP + q * 2 + u + 1, passed[0])
                        sp.dma_start(stage[:, u, :, :],
                                     adj_r[:, bass.ds(c, 1), :, bass.ds(q * 512 + u * 256, 256)].rearrange(
                                         "p c i n -> p (c i) n")).then_inc(stage_in[u], 16)

            def load_f2(c, h):
                wait_apart(sp, s["f2_free"], c * H + h + 1, passed[0])
                sp.dma_start(f2b[:, h, :], f2_r[h, bass.ds(c, 1), :].rearrange("a n -> (a n)").partition_broadcast(P)
                             ).then_inc(f2_in[h], 16)

            def store_y(c):
                wait_apart(sp, s["y_final"], c + 1, passed[0])
                sp.dma_start(x1_r[:, bass.ds(c, 1), :, :].rearrange("p c i d -> p (c i) d"), y[:]
                             ).then_inc(s["y_stored"], 16)
                wait_apart(sp, s["y_stored"], c * 16 + 16, passed[0])

            def load_y(c):
                sp.dma_start(y[:], y0_r[:, bass.ds(c, 1), :, :].rearrange("p c i d -> p (c i) d")
                             ).then_inc(s["y_loaded"], 16)

            for h in range(H):
                load_f2(0, h)
            load_adj(0)
            load_y(0)
            for h in range(H - 1):
                load_f2(1, h)
            load_adj(1)
            load_f2(1, H - 1)
            with sp.Fori(1, NIC - 1) as c:
                store_y(c - 1)
                load_y(c)
                for h in range(H - 1):
                    load_f2(c + 1, h)
                load_adj(c + 1)
                load_f2(c + 1, H - 1)
            store_y(NIC - 2)
            load_y(NIC - 1)
            store_y(NIC - 1)

        def transpose_pair(pe, c, q, u):
            pe.wait_ge(stage_in[u], (c * (NP // 2) + q) * 16 + 16)
            for j in range(2):
                pe.wait_ge(aT_done[j], c * NP + q * 2 + u + 1)
                for i in range(IT):
                    last = nc.tensor.transpose(bank[6 + j][:, i * P:(i + 1) * P],
                                               stage[:, u, i, j * P:(j + 1) * P], ident[:])
                last.then_inc(aT_ps[j], 1)
            pe.wait_ge(aT_ps[1], c * NP + q * 2 + u + 1)
            pe.sem_inc(s["stage_free"], 1)

        @block.tensor
        def _(pe):
            pe.sem_inc(s["stage_free"], 2)

            def products(c, h, q, first=False, last_quad=False, tr=None):
                hh = c * H + h
                for t4 in range(4):
                    pe.wait_ge(s["mask_done"], hh * NT + q * 4 + t4 + 1)
                    for i in range(2 * IT):
                        br, it = i // IT, i % IT
                        for pt in range(2):
                            begin = first and t4 == 0 and pt == 0 and i % 3 == 0
                            end = last_quad and t4 == 3 and pt == 1
                            op = nc.tensor.matmul(slot(h % 2, i), mask[:, t4, br, it * P:(it + 1) * P],
                                                  xs[:, h, bass.ds(q * 4 + t4, 1), br, pt, 0:XW].rearrange(
                                                      "p a n -> p (a n)"),
                                                  start=begin, stop=end, skip_group_check=True)
                    op.then_inc(s["mask_free"], 1)
                    if end:
                        pass
                    if tr is not None and t4 % 2 == 1:
                        transpose_pair(pe, tr, q, t4 // 2)

            def chunk(c, tr):
                for h in range(H):
                    pe.wait_ge(s["acc_free"], c * H + h + 1)
                    t = tr if h == H - 1 else None
                    products(c, h, 0, first=True, tr=t)
                    with pe.Fori(1, NQ - 1) as q:
                        products(c, h, q, tr=t)
                    products(c, h, NQ - 1, last_quad=True, tr=t)

            with pe.Fori(0, NP // 2) as q:
                for u in range(2):
                    transpose_pair(pe, 0, q, u)
            chunk(0, 1)
            with pe.Fori(1, NIC - 1) as c:
                chunk(c, c + 1)
            chunk(NIC - 1, None)

        def copy_aT(eng, copy, c, q, u, j):
            eng.wait_ge(aT_ps[j], c * NP + q * 2 + u + 1)
            copy(flat(aT[:, bass.ds(q * 4 + 2 * u + j, 1), :]), bank[6 + j][:]).then_inc(aT_done[j], 1)

        @block.scalar
        def _(act):
            act.sem_inc(s["f2_free"], 4)
            act.sem_inc(aT_done[0], 1)

            def copy(c, q, u):
                copy_aT(act, lambda o, i: nc.scalar.activation(o, i, ACT.Copy), c, q, u, 0)

            def signs(c, h, q, tr=None, tr_q=None):
                for u in range(2):
                    act.wait_ge(s["sign_free"], (c * H + h) * NP + q * 2 + u + 1)
                    for j in range(2):
                        last = nc.scalar.activation(sign[:, u, j, :], f2b[:, h, :], ACT.Sign,
                                                    bias=k.f12[:, h, bass.ds(q * 4 + 2 * u + j, 1)])
                    last.then_inc(s["sign_done"], 1)
                    if tr is not None:
                        copy(tr, tr_q, u)

            def read_out(c, h, st):
                hh = c * H + h
                act.wait_ge(s["mask_free"], hh * NT + NT + 4)
                act.wait_ge(s["acc_free"], hh + 2)
                for i in range(IT):
                    last = nc.scalar.activation(part[:, i, :], slot(st, i), ACT.Copy,
                                                scale=k.expo[:, 2, h, bass.ds(c * IT + i, 1)])
                last.then_inc(s["part_done"], 1)

            def deviation(c):
                act.wait_ge(s["mv_done"], c * 2 + 2)
                nc.scalar.activation(rstd[:], mv[:, :, 1], ACT.Sqrt).then_inc(s["std_done"], 1)

            def chunk(c, tr, prev):
                for h in range(H):
                    act.wait_ge(f2_in[h], c * 16 + 16)
                    if h == 0 and prev is not None:
                        signs(c, h, 0, c, NQ - 1)
                        read_out(prev, H - 1, 1)
                    else:
                        signs(c, h, 0)
                        if h:
                            read_out(c, h - 1, (h - 1) % 2)
                    signs(c, h, 1, tr if h == H - 1 else None, 0)
                    if h == 0 and prev is not None:
                        deviation(prev)
                    with act.Fori(2, NQ) as q:
                        signs(c, h, q, tr if h == H - 1 else None, q - 1)
                    act.wait_ge(s["sign_done"], (c * H + h) * NP + NP)
                    act.sem_inc(s["f2_free"], 1)

            with act.Fori(0, NP // 2) as q:
                for u in range(2):
                    copy(0, q, u)
            chunk(0, 1, None)
            with act.Fori(1, NIC - 1) as c:
                chunk(c, c + 1, c - 1)
            chunk(NIC - 1, None, NIC - 2)
            read_out(NIC - 1, H - 1, 1)
            deviation(NIC - 1)

        @block.vector
        def _(dve):
            dve.sem_inc(s["sign_free"], 2)
            dve.sem_inc(s["mask_free"], 4)
            dve.sem_inc(s["acc_free"], 2)
            dve.sem_inc(aT_done[1], 1)

            def copy(c, q, u):
                copy_aT(dve, nc.vector.tensor_copy, c, q, u, 1)

            def masks(c, h, q, tr=None, tr_q=None):
                hh = c * H + h
                for u in range(2):
                    if h == 0:
                        for j in range(2):
                            dve.wait_ge(aT_done[j], c * NP + q * 2 + u + 2)
                    dve.wait_ge(s["sign_done"], hh * NP + q * 2 + u + 1)
                    sg = sign[:, u, :, :].rearrange("p j n -> p (j n)")
                    nc.vector.tensor_tensor(out=sg, in0=sg, in1=aT[:, bass.ds(q * 4 + 2 * u, 2), :].rearrange(
                        "p j n -> p (j n)"), op=ALU.mult).then_inc(s["b_done"], 1)
                    dve.wait_ge(s["b_done"], hh * NP + q * 2 + u + 1)
                    for j in range(2):
                        t4 = 2 * u + j
                        dve.wait_ge(s["mask_free"], hh * NT + q * 4 + t4 + 1)
                        for br, op in ((0, ALU.max), (1, ALU.min)):
                            last = nc.vector.tensor_scalar(mask[:, t4, br, :], sign[:, u, j, :], 0.0,
                                                           k.qm[:, br, h, bass.ds(q * 4 + t4, 1)], op, ALU.mult)
                        last.then_inc(s["mask_done"], 1)
                    dve.wait_ge(s["mask_done"], hh * NT + q * 4 + 2 * u + 2)
                    dve.sem_inc(s["sign_free"], 1)
                    if tr is not None:
                        copy(tr, tr_q, u)

            def read_out(c, h, st):
                hh = c * H + h
                dve.wait_ge(s["part_done"], hh + 1)
                for i in range(IT):
                    nc.vector.scalar_tensor_tensor(
                        out=part[:, i, :], in0=slot(st, IT + i), scalar=k.expo[:, 3, h, bass.ds(c * IT + i, 1)],
                        in1=part[:, i, :], op0=ALU.mult, op1=ALU.add).then_inc(s["sum_done"], 1)
                dve.wait_ge(s["sum_done"], (hh + 1) * IT)
                dve.wait_ge(s["acc_free"], hh + 2)
                nc.vector.tensor_scalar(dinv[:], part[:, :, DH], 1e-30, None, ALU.max).then_inc(s["den_done"], 1)
                dve.wait_ge(s["den_done"], hh * 3 + 1)
                nc.vector.reciprocal(dinv[:], dinv[:]).then_inc(s["den_done"], 1)
                dve.wait_ge(s["den_done"], hh * 3 + 2)
                nc.vector.tensor_scalar(dinv[:], dinv[:], kout, None, ALU.mult).then_inc(s["den_done"], 1)
                dve.wait_ge(s["den_done"], hh * 3 + 3)
                if h == 0:
                    dve.wait_ge(s["y_loaded"], c * 16 + 16)
                for i in range(IT):
                    ys = y[:, i, h * DH:(h + 1) * DH]
                    last = nc.vector.scalar_tensor_tensor(out=ys, in0=part[:, i, 0:DH], scalar=dinv[:, i:i + 1],
                                                          in1=ys, op0=ALU.mult, op1=ALU.add)
                last.then_inc(s["acc_free"], 1)

            def moments(c):
                dve.wait_ge(s["acc_free"], c * H + H + 2)
                for i in range(IT):
                    last = nc.vector.bn_stats(stats[:, i, :], y[:, i, :])
                last.then_inc(s["stat_done"], 1)
                wait_apart(dve, s["stat_done"], c + 1, passed[2])
                for i in range(IT):
                    last = nc.vector.bn_aggr(mv[:, i, :], stats[:, i, :])
                last.then_inc(s["mv_done"], 1)
                dve.wait_ge(s["mv_done"], c * 2 + 1)
                nc.vector.tensor_scalar(mv[:, :, 1], mv[:, :, 1], EPS, None, ALU.add).then_inc(s["mv_done"], 1)

            def normalize(c):
                dve.wait_ge(s["std_done"], c + 1)
                nc.vector.reciprocal(rstd[:], rstd[:]).then_inc(s["inv_done"], 1)
                dve.wait_ge(s["inv_done"], c + 1)
                for i in range(IT):
                    last = nc.vector.tensor_scalar(y[:, i, :], y[:, i, :], mv[:, i, 0:1], rstd[:, i:i + 1],
                                                   ALU.subtract, ALU.mult)
                last.then_inc(s["y_final"], 1)

            def chunk(c, tr, prev):
                for h in range(H):
                    if h == 0 and prev is not None:
                        masks(c, h, 0, c, NQ - 1)
                        read_out(prev, H - 1, 1)
                        moments(prev)
                    else:
                        masks(c, h, 0)
                        if h:
                            read_out(c, h - 1, (h - 1) % 2)
                    masks(c, h, 1, tr if h == H - 1 else None, 0)
                    if h == 0 and prev is not None:
                        normalize(prev)
                    with dve.Fori(2, NQ) as q:
                        masks(c, h, q, tr if h == H - 1 else None, q - 1)

            with dve.Fori(0, NP // 2) as q:
                for u in range(2):
                    copy(0, q, u)
            chunk(0, 1, None)
            with dve.Fori(1, NIC - 1) as c:
                chunk(c, c + 1, c - 1)
            chunk(NIC - 1, None, NIC - 2)
            read_out(NIC - 1, H - 1, 1)
            moments(NIC - 1)
            normalize(NIC - 1)


def project1(nc, sem, k, w1, nw, ew, x1_dram):
    m = Map(nc, k.at)
    k.hT = m("hT", [P, 2, KT, N], F16, 2)
    k.v = m("v", [P, 2, NT, D], F16, 2)
    k.free = m.at
    w_sb = m("w1_sb", [P, KT, D], FP32, 4)
    e_sb = m("e1_sb", [P, KT, D], FP32, 4)
    x_in = m("x1_in", [P, 2, IT, D], FP32, 4)
    xT = m("x1T", [P, 2, KT, IC], FP32, 4)
    n_bc = m("n_bc", [P, D], FP32, 4)
    prod = m("prod1", [P, IT, D], FP32, 4)
    assert m.at <= nc.sbuf_usable_end
    bank, ident, small = k.bank, k.ident, k.small
    peak, gmax = small[:, 12:14], small[:, 14:16]
    s_e, s_w, k.inv_e2, k.inv_w = small[:, 16:17], small[:, 17:18], small[:, 18:19], small[:, 19:20]

    steps, w_in, n_in, g_in, g_out, scale_done, xT_ps, xT_done, mm, hi, lo, prod_done, score_done, node_max, \
        node_exp, node_sum = (sem("p2_" + n) for n in (
            "steps", "w_in", "n_in", "g_in", "g_out", "scale_done", "xT_ps", "xT_done", "mm", "hi", "lo",
            "prod_done", "score_done", "node_max", "node_exp", "node_sum"))
    passed = [sem(f"p2_passed{i}") for i in range(3)]
    x_loaded = [sem(f"p2_x_loaded{i}") for i in range(2)]
    x1_r = x1_dram.rearrange("(c i p) d -> p c i d", i=IT, p=P)
    NJ = KT + IT

    with nc.Block() as block:

        @block.sync
        def _(sp):
            sp.dma_start(w_sb[:], w1.rearrange("(k p) d -> p k d", p=P)).then_inc(w_in, 16)
            sp.dma_start(e_sb[:], ew.rearrange("(k p) d -> p k d", p=P)).then_inc(w_in, 16)
            sp.dma_start(n_bc[:], nw.rearrange("d o -> (d o)").partition_broadcast(P)).then_inc(n_in, 16)
            with sp.Fori(0, NIC // 2) as c2:
                for u in range(2):
                    wait_apart(sp, score_done, c2 * 2 + u + 1, passed[0])
                    sp.dma_start(x_in[:, u, :, :], x1_r[:, bass.ds(c2 * 2 + u, 1), :, :].rearrange(
                        "p c i d -> p (c i) d")).then_inc(x_loaded[u], 16)

        @block.gpsimd
        def _(pool):
            pool.wait_ge(g_in, 1)
            nc.gpsimd.partition_all_reduce(gmax, peak, P, RMAX).then_inc(g_out, 1)
            pool.wait_ge(node_max, 1)
            nc.gpsimd.partition_all_reduce(small[:, 21:22], small[:, 20:21], P, RMAX).then_inc(node_max, 1)
            pool.wait_ge(node_exp, 2)
            nc.gpsimd.partition_all_reduce(small[:, 24:25], small[:, 23:24], P, RADD).then_inc(node_sum, 1)

        @block.tensor
        def _(pe):
            def transposes(c2, u):
                c = c2 * 2 + u
                pe.wait_ge(x_loaded[u], c2 * 16 + 16)
                for j in range(KT):
                    pe.wait_ge(xT_done, c * KT + j + 1)
                    for i in range(IT):
                        last = nc.tensor.transpose(bank[j % 2][:, i * P:(i + 1) * P],
                                                   x_in[:, u, i, j * P:(j + 1) * P], ident[:])
                    last.then_inc(xT_ps, 1)

            def product(c2, u, j):
                c = c2 * 2 + u
                pe.wait_ge(lo, c * NJ + j + 1)
                for i in range(KT):
                    if j < KT:
                        left, right = e_sb[:, i, j * P:(j + 1) * P], xT[:, u, i, :]
                    else:
                        left, right = xT[:, u, i, (j - KT) * P:(j - KT + 1) * P], w_sb[:, i, :]
                    last = nc.tensor.matmul(bank[2 + j % 4][:], left, right, start=(i == 0), stop=(i == KT - 1))
                last.then_inc(mm, 1)

            def chunk(c2, u, following):
                pe.wait_ge(xT_done, (c2 * 2 + u) * KT + KT + 2)
                for j in range(NJ):
                    product(c2, u, j)
                    if j == 3 and following is not None:
                        transposes(*following)

            pe.wait_ge(w_in, 32)
            transposes(0, 0)
            with pe.Fori(0, NIC // 2 - 1) as c2:
                chunk(c2, 0, (c2, 1))
                chunk(c2, 1, (c2 + 1, 0))
            chunk(NIC // 2 - 1, 0, (NIC // 2 - 1, 1))
            chunk(NIC // 2 - 1, 1, None)

        def place(c2, u, j, part):
            c = c2 * 2 + u
            if j < KT:
                return k.hT[:, part, j, bass.ds(c * IC, IC)]
            return flat(k.v[:, part, bass.ds(c * IT + (j - KT), 1), :])

        @block.scalar
        def _(act):
            act.sem_inc(xT_done, 2)

            def copies(c2, u):
                c = c2 * 2 + u
                for j in range(KT):
                    act.wait_ge(xT_ps, c * KT + j + 1)
                    nc.scalar.activation(xT[:, u, j, :], bank[j % 2][:], ACT.Copy).then_inc(xT_done, 1)

            def split(c2, u, following):
                for j in range(NJ):
                    act.wait_ge(mm, (c2 * 2 + u) * NJ + j + 1)
                    nc.scalar.activation(place(c2, u, j, 0), bank[2 + j % 4][:], ACT.Copy,
                                         scale=(s_e if j < KT else s_w)).then_inc(hi, 1)
                    if j == 3 and following is not None:
                        copies(*following)

            copies(0, 0)
            act.wait_ge(scale_done, 1)
            with act.Fori(0, NIC // 2 - 1) as c2:
                split(c2, 0, (c2, 1))
                split(c2, 1, (c2 + 1, 0))
            split(NIC // 2 - 1, 0, (NIC // 2 - 1, 1))
            split(NIC // 2 - 1, 1, None)
            act.wait_ge(node_max, 3)
            nc.scalar.activation(k.score[:], k.score[:], ACT.Exp, bias=small[:, 22:23],
                                 accum_out=small[:, 23:24]).then_inc(node_exp, 2)

        @block.vector
        def _(dve):
            dve.sem_inc(lo, 4)
            dve.sem_inc(score_done, 2)
            link = linker(nc, dve, steps)
            dve.wait_ge(w_in, 32)
            for i, w in enumerate((e_sb, w_sb)):
                link(lambda v: v.tensor_reduce(out=peak[:, i:i + 1], in_=w[:].rearrange("p k d -> p (k d)"),
                                               axis=AX.X, op=ALU.max, apply_absolute_value=True))
            dve.sem_inc(g_in, 1)
            dve.wait_ge(g_out, 1)
            power_of_two(link, small[:, 16:18], gmax, 64.0)
            link(lambda v: v.reciprocal(small[:, 18:20], small[:, 16:18]))
            link(lambda v: v.tensor_scalar(k.inv_e2, k.inv_e2, k.inv_e2, None, ALU.mult))
            dve.sem_inc(scale_done, 1)
            dve.wait_ge(n_in, 16)

            def chunk(c2, u):
                c = c2 * 2 + u
                dve.wait_ge(x_loaded[u], c2 * 16 + 16)
                for i in range(IT):
                    last = nc.vector.tensor_tensor(out=prod[:, i, :], in0=x_in[:, u, i, :], in1=n_bc[:], op=ALU.mult)
                last.then_inc(prod_done, 1)
                for j in range(NJ):
                    dve.wait_ge(hi, c * NJ + j + 1)
                    nc.vector.scalar_tensor_tensor(out=place(c2, u, j, 1), in0=bank[2 + j % 4][:],
                                                   scalar=(s_e if j < KT else s_w), in1=place(c2, u, j, 0),
                                                   op0=ALU.mult, op1=ALU.subtract).then_inc(lo, 1)
                    if j == 0:
                        dve.wait_ge(prod_done, c + 1)
                        nc.vector.tensor_reduce(out=k.score[:, bass.ds(c * IT, IT)], in_=prod[:], axis=AX.X,
                                                op=ALU.add).then_inc(score_done, 1)

            with dve.Fori(0, NIC // 2) as c2:
                for u in range(2):
                    chunk(c2, u)
            dve.wait_ge(score_done, NIC + 2)
            link(lambda v: v.tensor_reduce(out=small[:, 20:21], in_=k.score[:], axis=AX.X, op=ALU.max))
            dve.sem_inc(node_max, 1)
            dve.wait_ge(node_max, 2)
            link(lambda v: v.tensor_scalar(small[:, 22:23], small[:, 21:22], -1.0, None, ALU.mult))
            dve.sem_inc(node_max, 1)
            dve.wait_ge(node_sum, 1)
            link(lambda v: v.reciprocal(small[:, 25:26], small[:, 24:25]))
            link(lambda v: v.tensor_scalar(k.score[:], k.score[:], small[:, 25:26], k.inv_w, ALU.mult, ALU.mult))


def attend1(nc, sem, k, adj, b1, x1_dram, out):
    m = Map(nc, k.free)
    pr = m("pr", [P, 2, N], FP32, 4)
    NM = 4
    QW = N // NM
    neg = m("neg", [P, NM, QW], FP32, 4)
    pT = m("pT", [P, 2, 2, IC], F16, 2)
    xr = m("xr", [P, 2, D], FP32, 4)
    bias = m("bias1", [P, D], FP32, 4)
    cmax = m("cmax", [P, 2, 8], FP32, 4)
    st = m("st1", [P, 2, 16], FP32, 4)
    assert m.at <= nc.sbuf_usable_end
    bank, ident, hT, v = k.bank, k.ident, k.hT, k.v
    NC = N // IC
    names = ("neg_done", "neg_free", "qk", "s_done", "max_done", "bias_done", "exp_done", "coef_done",
             "pT_ps", "hi", "lo", "pv", "x_biased", "sum_done", "stat_done", "mv_done", "std_done", "inv_done",
             "norm_done", "b_in")
    s = {n: sem("a1_" + n) for n in names}
    passed = [sem(f"a1_passed{i}") for i in range(3)]
    neg_in = [sem(f"a1_neg_in{i}") for i in range(NM)]
    x_in = [sem(f"a1_x_in{i}") for i in range(2)]
    o_out = [sem(f"a1_o_out{i}") for i in range(2)]
    adj_r = adj.rearrange("(t p) n -> p t n", p=P)
    x1_r = x1_dram.rearrange("(t p) d -> p t d", p=P)
    out_r = out.rearrange("(t p) d -> p t d", p=P)

    with nc.Block() as block:

        @block.sync
        def _(sp):
            sp.dma_start(bias[:], b1.partition_broadcast(P)).then_inc(s["b_in"], 16)

            def tile(t, u, first=False):
                for i in range(NM):
                    wait_apart(sp, s["neg_free"], t * NM + i + 1, passed[0])
                    sp.dma_start(neg[:, i:i + 1, :], adj_r[:, bass.ds(t, 1), i * QW:(i + 1) * QW]
                                 ).then_inc(neg_in[i], 16)
                    if i == 1:
                        if not first:
                            wait_apart(sp, s["norm_done"], t + 1, passed[0])
                            sp.dma_start(out_r[:, bass.ds(t - 2, 1), :], xr[:, u:u + 1, :]).then_inc(o_out[u], 16)
                            wait_apart(sp, o_out[u], (t - u) * 8, passed[0])
                        sp.dma_start(xr[:, u:u + 1, :], x1_r[:, bass.ds(t, 1), :]).then_inc(x_in[u], 16)

            tile(0, 0, True)
            tile(1, 1, True)
            with sp.Fori(1, NT // 2) as i2:
                for u in range(2):
                    tile(i2 * 2 + u, u)
            for u in range(2):
                sp.wait_ge(s["norm_done"], NT + u + 1)
                sp.dma_start(out_r[:, NT - 2 + u, :], xr[:, u, :]).then_inc(o_out[u], 16)
            for u in range(2):
                sp.wait_ge(o_out[u], NT // 2 * 16)

        @block.gpsimd
        def _(pool):
            pool.wait_ge(s["b_in"], 16)
            with pool.Fori(0, NT // 2) as i2:
                for u in range(2):
                    t = i2 * 2 + u
                    for i in range(NM):
                        wait_apart(pool, neg_in[i], t * 16 + 16, passed[1])
                        nc.gpsimd.tensor_scalar(neg[:, i, :], neg[:, i, :], -1.0, BIG, ALU.add, ALU.mult
                                                ).then_inc(s["neg_done"], 1)
                    pool.wait_ge(x_in[u], i2 * 16 + 16)
                    nc.gpsimd.tensor_tensor(out=xr[:, u, :], in0=xr[:, u, :], in1=bias[:], op=ALU.add
                                            ).then_inc(s["x_biased"], 1)

        @block.tensor
        def _(pe):
            def logits(t, c):
                pe.wait_ge(s["s_done"], t * NC + c + 1)
                n = 0
                for a, b in ((0, 0), (0, 1), (1, 0)):
                    for j in range(KT):
                        last = nc.tensor.matmul(bank[c % 4][:], hT[:, a, j, bass.ds(t * P, P)],
                                                hT[:, b, j, c * IC:(c + 1) * IC], start=(n == 0), stop=(n == 11))
                        n += 1
                last.then_inc(s["qk"], 1)

            def transposes(t, u, g):
                pe.wait_ge(s["exp_done"], t + 1)
                pe.wait_ge(s["lo"], t * NC + g + 1)
                for j in range(4):
                    last = nc.tensor.transpose(bank[4 + g % 2][:, j * P:(j + 1) * P],
                                               pr[:, u, (g * 4 + j) * P:(g * 4 + j + 1) * P], ident[:])
                last.then_inc(s["pT_ps"], 1)

            def values(t, u, g):
                pe.wait_ge(s["lo"], t * NC + g + 3)
                if g == 0:
                    pe.wait_ge(s["sum_done"], t + 1)
                for j in range(4):
                    for a, b in ((0, 0), (0, 1), (1, 0)):
                        last = nc.tensor.matmul(bank[6 + u][:], pT[:, g % 2, a, j * P:(j + 1) * P],
                                                v[:, b, g * 4 + j, :], start=(g == 0 and j == 0 and a == b),
                                                stop=(g == NC - 1 and j == 3 and a == 1))
                last.then_inc(s["pv"], 1)

            def step(t, u, rows=True, prev=True):
                for c in range(NC):
                    if rows:
                        logits(t, c)
                    if prev and c >= 2:
                        transposes(t - 1, 1 - u, c - 2)
                        if c >= 3:
                            values(t - 1, 1 - u, c - 3)
                if prev:
                    transposes(t - 1, 1 - u, NC - 2)
                    values(t - 1, 1 - u, NC - 3)
                    transposes(t - 1, 1 - u, NC - 1)
                    values(t - 1, 1 - u, NC - 2)
                    values(t - 1, 1 - u, NC - 1)

            step(0, 0, prev=False)
            with pe.Fori(0, NT // 2 - 1) as i2:
                step(i2 * 2 + 1, 1)
                step(i2 * 2 + 2, 0)
            step(NT - 1, 1)
            step(NT, 0, rows=False)

        @block.scalar
        def _(act):
            def exps(t, u):
                act.wait_ge(s["bias_done"], t + 1)
                nc.scalar.activation(pr[:, u, :], pr[:, u, :], ACT.Exp, bias=st[:, u, 1:2], scale=k.inv_e2,
                                     accum_out=st[:, u, 2:3]).then_inc(s["exp_done"], 1)

            def high(t, u, g):
                act.wait_ge(s["pT_ps"], t * NC + g + 1)
                act.wait_ge(s["pv"], t * NC + g + 1)
                nc.scalar.activation(pT[:, g % 2, 0, :], bank[4 + g % 2][:], ACT.Copy).then_inc(s["hi"], 1)

            def deviation(t, u):
                act.wait_ge(s["mv_done"], t * 2 + 2)
                nc.scalar.activation(st[:, u, 13:14], st[:, u, 12:13], ACT.Sqrt).then_inc(s["std_done"], 1)

            def step(t, u, prev=True):
                exps(t, u)
                if prev:
                    deviation(t - 1, 1 - u)
                for g in range(NC):
                    high(t, u, g)

            act.sem_inc(s["pv"], 2)
            step(0, 0, prev=False)
            with act.Fori(0, NT // 2 - 1) as i2:
                step(i2 * 2 + 1, 1)
                step(i2 * 2 + 2, 0)
            step(NT - 1, 1)
            deviation(NT - 1, 1)

        @block.vector
        def _(dve):
            dve.sem_inc(s["s_done"], 4)
            dve.sem_inc(s["neg_free"], 4)
            dve.sem_inc(s["lo"], 2)
            dve.sem_inc(s["norm_done"], 2)
            dve.sem_inc(s["sum_done"], 2)

            def mask_chunk(t, u, c):
                if c % 2 == 0:
                    dve.wait_ge(s["neg_done"], t * NM + c // 2 + 1)
                wait_apart(dve, s["qk"], t * NC + c + 1, passed[2])
                nc.vector.tensor_tensor_reduce(out=pr[:, u, c * IC:(c + 1) * IC], in0=bank[c % 4][:],
                                               in1=neg[:, c // 2, c % 2 * IC:(c % 2 + 1) * IC], scale=1.0,
                                               scalar=-3.3e38, op0=ALU.add, op1=ALU.max,
                                               accum_out=cmax[:, u, c:c + 1]).then_inc(s["s_done"], 1)
                if c % 2 == 1:
                    dve.wait_ge(s["s_done"], t * NC + c + 5)
                    dve.sem_inc(s["neg_free"], 1)

            def row_max(t, u):
                nc.vector.tensor_reduce(out=st[:, u, 0:1], in_=cmax[:, u, :], axis=AX.X, op=ALU.max
                                        ).then_inc(s["max_done"], 1)
                dve.wait_ge(s["max_done"], t * 3 + 1)
                nc.vector.tensor_scalar(st[:, u, 3:4], st[:, u, 0:1], k.inv_e2, -1.0, ALU.mult, ALU.mult
                                        ).then_inc(s["max_done"], 1)
                dve.wait_ge(s["max_done"], t * 3 + 2)
                nc.vector.tensor_scalar(st[:, u, 1:2], st[:, u, 3:4], PSCALE, None, ALU.add
                                        ).then_inc(s["bias_done"], 1)
                nc.vector.tensor_scalar(st[:, u, 4:5], st[:, u, 0:1], -1.0e38, k.score[:, bass.ds(t, 1)],
                                        ALU.is_gt, ALU.mult).then_inc(s["max_done"], 1)

            def low(t, u, g):
                dve.wait_ge(s["hi"], t * NC + g + 1)
                nc.vector.tensor_tensor(out=pT[:, g % 2, 1, :], in0=bank[4 + g % 2][:], in1=pT[:, g % 2, 0, :],
                                        op=ALU.subtract).then_inc(s["lo"], 1)

            def coef(t, u):
                dve.wait_ge(s["exp_done"], t + 1)
                dve.wait_ge(s["max_done"], t * 3 + 3)
                nc.vector.reciprocal(st[:, u, 5:6], st[:, u, 2:3]).then_inc(s["coef_done"], 1)
                dve.wait_ge(s["coef_done"], t * 2 + 1)
                nc.vector.tensor_scalar(st[:, u, 5:6], st[:, u, 5:6], st[:, u, 4:5], None, ALU.mult
                                        ).then_inc(s["coef_done"], 1)

            def total(t, u):
                dve.wait_ge(s["pv"], t * NC + NC + 2)
                dve.wait_ge(s["coef_done"], t * 2 + 2)
                dve.wait_ge(s["x_biased"], t + 1)
                nc.vector.scalar_tensor_tensor(out=xr[:, u, :], in0=bank[6 + u][:], scalar=st[:, u, 5:6],
                                               in1=xr[:, u, :], op0=ALU.mult, op1=ALU.add).then_inc(s["sum_done"], 1)
                dve.wait_ge(s["sum_done"], t + 3)
                nc.vector.bn_stats(st[:, u, 6:12], xr[:, u, :]).then_inc(s["stat_done"], 1)
                wait_apart(dve, s["stat_done"], t + 1, passed[2])
                nc.vector.bn_aggr(st[:, u, 14:16], st[:, u, 6:12]).then_inc(s["mv_done"], 1)
                dve.wait_ge(s["mv_done"], t * 2 + 1)
                nc.vector.tensor_scalar(st[:, u, 12:13], st[:, u, 15:16], EPS, None, ALU.add
                                        ).then_inc(s["mv_done"], 1)

            def normalize(t, u):
                dve.wait_ge(s["std_done"], t + 1)
                nc.vector.reciprocal(st[:, u, 13:14], st[:, u, 13:14]).then_inc(s["inv_done"], 1)
                dve.wait_ge(s["inv_done"], t + 1)
                nc.vector.tensor_scalar(xr[:, u, :], xr[:, u, :], st[:, u, 14:15], st[:, u, 13:14],
                                        ALU.subtract, ALU.mult).then_inc(s["norm_done"], 1)

            def step(t, u, rows=True, prev=True, prev2=True):
                w = 1 - u
                for c in range(NC):
                    if rows:
                        mask_chunk(t, u, c)
                    if c == 0:
                        if prev:
                            coef(t - 1, w)
                        if prev2:
                            total(t - 2, u)
                    if c == 2 and prev2:
                        normalize(t - 2, u)
                    if prev and c >= 2:
                        low(t - 1, w, c - 2)
                if rows:
                    row_max(t, u)
                if prev:
                    low(t - 1, w, NC - 2)
                    low(t - 1, w, NC - 1)

            step(0, 0, prev=False, prev2=False)
            step(1, 1, prev2=False)
            with dve.Fori(1, NT // 2) as i2:
                step(i2 * 2, 0)
                step(i2 * 2 + 1, 1)
            step(NT, 0, rows=False)
            total(NT - 1, 1)
            normalize(NT - 1, 1)


_INS = ["x", "adj", "L0_gnn_weight", "L0_gnn_weight_u", "L0_gnn_weight_v", "L0_gnn_bias", "L0_gnn_proj_w",
        "L0_gnn_proj_b", "L1_gnn_weight", "L1_gnn_bias", "L1_gnn_node_w", "L1_gnn_edge_w"]


def kernel(**inputs):
    import numpy as _np
    import concourse.bacc as _bacc
    from concourse import mybir as _mybir
    from concourse.bass_utils import run_bass_kernel_spmd as _run

    nc = _bacc.Bacc("TRN2", target_bir_lowering=False, num_devices=1)
    arrays, args = {}, []
    for name in _INS:
        a = _np.ascontiguousarray(inputs[name])
        arrays[f"in_{name}_dram"] = a
        args.append(nc.dram_tensor(f"in_{name}_dram", a.shape, _mybir.dt.from_np(a.dtype), kind="ExternalInput").ap())
    args.append(nc.dram_tensor("out_0_dram", (N, D), FP32, kind="ExternalOutput").ap())
    build(nc, *args)
    r = _run(nc, [arrays], core_ids=[0])
    return r.results[0]["out_0_dram"]
```

```python
import numpy as np
import concourse.bass as bass
from concourse import mybir
from contextlib import ExitStack

FP32 = mybir.dt.float32
F16 = mybir.dt.float16
BF16 = mybir.dt.bfloat16
U32 = mybir.dt.uint32
ALU = mybir.AluOpType
ACT = mybir.ActivationFunctionType
AX = mybir.AxisListType
RMAX = bass.bass_isa.ReduceOp.max
RADD = bass.bass_isa.ReduceOp.add

P = 128
N = 4096
D = 512
H = 4
DH = D // H
NT = N // P
KT = D // P
IC = 512
NIC = N // IC
IT = IC // P
XW = DH + 1
XP = DH + 2
NQ = NT // 4
EPS = 1e-5
SHIFT = 40.0
DEN = 1024.0
SLOPE = 0.2
BIG = 3.0e38
PSCALE = 8.317766166719343


class Map:

    def __init__(self, nc, at):
        self.nc, self.at = nc, at

    def __call__(self, name, shape, dt, width):
        size = int(np.prod(shape[1:])) * width
        t = self.nc.alloc_sbuf_tensor_at(name, shape, dt, offset=self.at)
        self.at += (size + 31) // 32 * 32
        return t


def build(nc, x, adj, w0, wu, wv, b0, pw, pb, w1, b1, nw, ew, out):
    ctx = ExitStack()
    with ctx:
        def sem(name):
            return ctx.enter_context(nc.semaphore(name))

        y0_dram = nc.dram_tensor("y0_scratch", [N, D], FP32).ap()
        x1_dram = nc.dram_tensor("x1_scratch", [N, D], FP32).ap()
        f2_dram = nc.dram_tensor("f2_scratch", [H * NT, P], FP32).ap()

        keep = Map(nc, (nc.sbuf_base + 31) // 32 * 32)
        k = Kept()
        k.ident = keep("ident", [P, P], FP32, 4)
        k.f12 = keep("f12", [P, 2 * H, NT], FP32, 4)
        k.expo = keep("expo", [P, 4, H, NT], FP32, 4)
        k.qm = keep("qm", [P, 2, H, NT], FP32, 4)
        k.score = keep("score", [P, NT], FP32, 4)
        k.small = keep("small", [P, 32], FP32, 4)
        k.at = keep.at
        k.bank = [ctx.enter_context(nc.psum_tensor(f"bank{i}", [P, 512], FP32)) for i in range(8)]

        project0(nc, sem, k, x, w0, wu, wv, b0, pw, pb, y0_dram)
        scale_support(nc, sem, k, f2_dram)
        attend0(nc, sem, k, adj, y0_dram, f2_dram, x1_dram)
        project1(nc, sem, k, w1, nw, ew, x1_dram)
        attend1(nc, sem, k, adj, b1, x1_dram, out)


class Kept:
    pass


def wait_apart(eng, done, value, passed):
    eng.wait_ge(done, value)
    eng.sem_inc(passed, 1)


def flat(ap):
    return ap.rearrange("p a n -> p (a n)")


X_BYTES = H * NT * 2 * 2 * XP * 2


def project0(nc, sem, k, x, w0, wu, wv, b0, pw, pb, y0_dram):
    k.sup = nc.alloc_sbuf_tensor_at("sup", [P, NT, D], FP32, offset=k.at + (X_BYTES + 31) // 32 * 32)
    m = Map(nc, k.at)
    w_sb = m("w_sb", [P, KT, D], FP32, 4)
    p_sb = m("p_sb", [P, KT, D], FP32, 4)
    u_bc = m("u_bc", [P, 2, D], FP32, 4)
    bias = m("bias", [P, 2, D], FP32, 4)
    x_in = m("x_in", [P, 4, D], FP32, 4)
    xb = m("xb", [P, 4, D], FP32, 4)
    xT = m("xT", [P, 2, KT, P], FP32, 4)
    prod = m("prod", [P, 2, 2 * H, DH], FP32, 4)
    y_sb = m("y_sb", [P, 4, D], FP32, 4)
    smax = m("smax", [P, NT], FP32, 4)
    ident, bank = k.ident, k.bank

    w_in, c_in, id_done, bias_done = sem("p0_w_in"), sem("p0_c_in"), sem("p0_id_done"), sem("p0_bias_done")
    x_loaded = [sem(f"p0_x_loaded{i}") for i in range(4)]
    y_stored = [sem(f"p0_y_stored{i}") for i in range(4)]
    passed = [sem(f"p0_passed{i}") for i in range(3)]
    xb_done, xT_ps, xT_done, mm_s, mm_y = (sem("p0_" + n) for n in ("xb_done", "xT_ps", "xT_done", "mm_s", "mm_y"))
    s_done, y_done, prod_done, f_done = (sem("p0_" + n) for n in ("s_done", "y_done", "prod_done", "f_done"))

    x_t = x.rearrange("(t p) d -> p t d", p=P)
    y_t = y0_dram.rearrange("(t p) d -> p t d", p=P)

    with nc.Block() as block:

        @block.sync
        def _(sp):
            sp.dma_start(w_sb[:], w0.rearrange("(k p) d -> p k d", p=P)).then_inc(w_in, 16)
            sp.dma_start(p_sb[:], pw.rearrange("(k p) d -> p k d", p=P)).then_inc(w_in, 16)
            for u in range(4):
                sp.dma_start(x_in[:, u, :], x_t[:, u, :]).then_inc(x_loaded[u], 16)
            sp.dma_start(u_bc[:, 0, :], wu.rearrange("h d o -> (h d o)").partition_broadcast(P)).then_inc(c_in, 16)
            sp.dma_start(u_bc[:, 1, :], wv.rearrange("h d o -> (h d o)").partition_broadcast(P)).then_inc(c_in, 16)
            sp.dma_start(bias[:, 0, :], b0.rearrange("a d -> (a d)").partition_broadcast(P)).then_inc(c_in, 16)
            sp.dma_start(bias[:, 1, :], pb.partition_broadcast(P)).then_inc(c_in, 16)
            with sp.Fori(1, NT // 4) as q:
                for u in range(4):
                    wait_apart(sp, y_done, q * 4 + u + 1, passed[0])
                    sp.dma_start(y_t[:, bass.ds(q * 4 + (u - 4), 1), :], y_sb[:, u:u + 1, :]).then_inc(y_stored[u], 16)
                    sp.dma_start(x_in[:, u:u + 1, :], x_t[:, bass.ds(q * 4 + u, 1), :]).then_inc(x_loaded[u], 16)
            for u in range(4):
                sp.wait_ge(y_done, NT + u + 1)
                sp.dma_start(y_t[:, NT - 4 + u, :], y_sb[:, u, :]).then_inc(y_stored[u], 16)
            for u in range(4):
                sp.wait_ge(y_stored[u], NT // 4 * 16)

        @block.gpsimd
        def _(pool):
            nc.gpsimd.memset(ident[:], 0.0).then_inc(id_done, 1)
            pool.wait_ge(id_done, 1)
            nc.gpsimd.affine_select(out=ident[:], in_=ident[:], compare_op=ALU.not_equal, fill=1.0, base=0,
                                    pattern=[[-1, P]], channel_multiplier=1).then_inc(id_done, 1)
            pool.wait_ge(c_in, 64)
            nc.gpsimd.tensor_tensor(out=bias[:, 0, :], in0=bias[:, 0, :], in1=bias[:, 1, :],
                                    op=ALU.add).then_inc(bias_done, 1)
            pool.wait_ge(bias_done, 1)
            with pool.Fori(0, NT // 4) as q:
                for u in range(4):
                    pool.wait_ge(x_loaded[u], q * 16 + 16)
                    pool.wait_ge(y_done, q * 4 + u + 1)
                    nc.gpsimd.tensor_tensor(out=xb[:, u, :], in0=x_in[:, u, :], in1=bias[:, 0, :],
                                            op=ALU.add).then_inc(xb_done, 1)

        def transpose_tile(pe, q, u):
            pe.wait_ge(x_loaded[u], q * 16 + 16)
            pe.wait_ge(xT_done, q * 4 + u + 1)
            for j in range(KT):
                last = nc.tensor.transpose(bank[u % 2][:, j * P:(j + 1) * P], x_in[:, u, j * P:(j + 1) * P], ident[:])
            last.then_inc(xT_ps, 1)

        def project_tile(pe, q, u):
            pe.wait_ge(xT_done, q * 4 + u + 3)
            pe.wait_ge(s_done, q * 4 + u + 1)
            for j in range(KT):
                last = nc.tensor.matmul(bank[2 + u % 2][:], xT[:, u % 2, j, :], w_sb[:, j, :],
                                        start=(j == 0), stop=(j == KT - 1))
            last.then_inc(mm_s, 1)
            pe.wait_ge(y_done, q * 4 + u + 3)
            for j in range(KT):
                last = nc.tensor.matmul(bank[4 + u % 2][:], xT[:, u % 2, j, :], p_sb[:, j, :],
                                        start=(j == 0), stop=(j == KT - 1))
            last.then_inc(mm_y, 1)

        @block.tensor
        def _(pe):
            pe.wait_ge(id_done, 2)
            pe.wait_ge(w_in, 32)
            transpose_tile(pe, 0, 0)
            with pe.Fori(0, NT // 4 - 1) as q:
                for u in range(4):
                    transpose_tile(pe, q + (u + 1) // 4, (u + 1) % 4)
                    project_tile(pe, q, u)
            for u in range(4):
                if u < 3:
                    transpose_tile(pe, NT // 4 - 1, u + 1)
                project_tile(pe, NT // 4 - 1, u)

        @block.scalar
        def _(act):
            act.sem_inc(xT_done, 2)
            act.sem_inc(s_done, 2)
            act.sem_inc(mm_y, 2)

            def copy_xT(q, u):
                act.wait_ge(xT_ps, q * 4 + u + 1)
                act.wait_ge(mm_y, q * 4 + u + 1)
                nc.scalar.activation(xT[:, u % 2, :, :].rearrange("p k n -> p (k n)"), bank[u % 2][:],
                                     ACT.Copy).then_inc(xT_done, 1)

            def copy_s(q, u):
                act.wait_ge(mm_s, q * 4 + u + 1)
                nc.scalar.activation(flat(k.sup[:, bass.ds(q * 4 + u, 1), :]), bank[2 + u % 2][:],
                                     ACT.Copy).then_inc(s_done, 1)

            copy_xT(0, 0)
            with act.Fori(0, NT // 4 - 1) as q:
                for u in range(4):
                    copy_xT(q + (u + 1) // 4, (u + 1) % 4)
                    copy_s(q, u)
            for u in range(4):
                if u < 3:
                    copy_xT(NT // 4 - 1, u + 1)
                copy_s(NT // 4 - 1, u)

        @block.vector
        def _(dve):
            dve.sem_inc(y_done, 4)
            dve.wait_ge(c_in, 64)

            def tile(q, u, first):
                t = q * 4 + u
                dve.wait_ge(s_done, t + 3)
                st = flat(k.sup[:, bass.ds(t, 1), :]) if not isinstance(t, int) else k.sup[:, t, :]
                for i in range(2):
                    last = nc.vector.tensor_tensor(
                        out=prod[:, u % 2, i * H:(i + 1) * H, :].rearrange("p h d -> p (h d)"), in0=st,
                        in1=u_bc[:, i, :], op=ALU.mult)
                last.then_inc(prod_done, 1)
                nc.vector.tensor_reduce(out=smax[:, bass.ds(t, 1)], in_=st, axis=AX.X, op=ALU.max,
                                        apply_absolute_value=True).then_inc(f_done, 1)
                dve.wait_ge(prod_done, t + 1)
                nc.vector.tensor_reduce(out=k.f12[:, :, bass.ds(t, 1)], in_=prod[:, u % 2, :, :], axis=AX.X,
                                        op=ALU.add).then_inc(f_done, 1)
                dve.wait_ge(mm_y, t + 3)
                dve.wait_ge(xb_done, t + 1)
                if not first:
                    dve.wait_ge(y_stored[u], q * 16)
                nc.vector.tensor_tensor(out=y_sb[:, u, :], in0=bank[4 + u % 2][:], in1=xb[:, u, :],
                                        op=ALU.add).then_inc(y_done, 1)

            for u in range(4):
                tile(0, u, True)
            with dve.Fori(1, NT // 4) as q:
                for u in range(4):
                    tile(q, u, False)
            dve.wait_ge(f_done, 2 * NT)
            nc.vector.tensor_reduce(out=k.small[:, 4:5], in_=smax[:], axis=AX.X, op=ALU.max).then_inc(f_done, 1)
            dve.wait_ge(f_done, 2 * NT + 1)


def power_of_two(link, out, peak, room):
    link(lambda v: v.tensor_scalar(out, peak, 1e-30, None, ALU.max))
    link(lambda v: v.reciprocal(out, out))
    link(lambda v: v.tensor_scalar(out, out, room, None, ALU.mult))
    link(lambda v: v.tensor_scalar(out.bitcast(U32), out.bitcast(U32), 0x7F800000, None, ALU.bitwise_and))


def linker(nc, dve, done):
    count = [0]

    def link(step):
        step(nc.vector).then_inc(done, 1)
        count[0] += 1
        dve.wait_ge(done, count[0])
    return link


def scale_support(nc, sem, k, f2_dram):
    k.xs = nc.alloc_sbuf_tensor_at("xs", [P, H, NT, 2, 2, XP], F16, offset=k.at)
    m = Map(nc, k.at + (X_BYTES + 31) // 32 * 32 + NT * D * 4)
    t1 = m("t1", [P, 2, 2, D], FP32, 4)
    arg = m("arg", [P, 2, H, NT], FP32, 4)
    f2r = k.expo[:, 3].rearrange("p h t -> p (h t)")
    qb = k.expo[:, 2].rearrange("p h t -> p (h t)").bitcast(BF16).rearrange("p (a h t) -> p a h t", a=2, h=H)
    small, bank, ident, f12 = k.small, k.bank, k.ident, k.f12
    peak, gmax, scale, ratio = small[:, 0:5], small[:, 5:10], small[:, 10:11], small[:, 11:12]

    steps, g_out, e_done, f2_ps, f2_sb, f2_out = (sem("p1_" + n) for n in
                                                  ("steps", "g_out", "e_done", "f2_ps", "f2_sb", "f2_out"))
    local_done, arg_done, cs_done, t1_dve, t1_pool, hi_done, lo_done, den_done = (sem("p1_" + n) for n in (
        "local_done", "arg_done", "cs_done", "t1_dve", "t1_pool", "hi_done", "lo_done", "den_done"))

    def fac(mm, t):
        return arg[:, mm, :, bass.ds(t, 1)].broadcast_to([P, H, DH])

    def half(t, mm, part):
        return k.xs[:, :, bass.ds(t, 1), mm, part, 0:DH].rearrange("p h a d -> p (h a) d")

    def sup(t):
        return flat(k.sup[:, bass.ds(t, 1), :]).rearrange("p (h d) -> p h d", h=H)

    with nc.Block() as block:

        @block.tensor
        def _(pe):
            nc.tensor.transpose(bank[0][:, 0:P], f12[:, H:2 * H, :].rearrange("p h t -> p (h t)"),
                                ident[:]).then_inc(f2_ps, 1)

        @block.sync
        def _(sp):
            sp.wait_ge(f2_sb, 1)
            sp.dma_start(f2_dram, f2r).then_inc(f2_out, 16)
            sp.wait_ge(f2_out, 16)

        @block.gpsimd
        def _(pool):
            pool.wait_ge(local_done, 1)
            nc.gpsimd.partition_all_reduce(gmax, peak, P, RMAX).then_inc(g_out, 1)
            pool.wait_ge(cs_done, 1)
            with pool.Fori(0, NT // 2) as i:
                for u in range(2):
                    pool.wait_ge(lo_done, i * 4 + 2 * u + 2)
                    nc.gpsimd.tensor_tensor(out=t1[:, u, 1, :].rearrange("p (h d) -> p h d", h=H),
                                            in0=sup(i * 2 + u), in1=fac(1, i * 2 + u), op=ALU.mult
                                            ).then_inc(t1_pool, 1)

        @block.scalar
        def _(act):
            act.wait_ge(f2_ps, 1)
            nc.scalar.activation(f2r, bank[0][:, 0:P], ACT.Copy).then_inc(f2_sb, 1)
            act.wait_ge(arg_done, 1)
            nc.scalar.activation(k.expo[:, 0:2].rearrange("p a h t -> p (a h t)"),
                                 arg[:].rearrange("p a h t -> p (a h t)"), ACT.Exp).then_inc(e_done, 1)
            act.wait_ge(arg_done, 2)
            act.wait_ge(f2_out, 16)
            nc.scalar.activation(k.expo[:, 2:4].rearrange("p a h t -> p (a h t)"),
                                 arg[:].rearrange("p a h t -> p (a h t)"), ACT.Exp).then_inc(e_done, 1)
            with act.Fori(0, NT // 2) as i:
                for u in range(2):
                    t = i * 2 + u
                    for mm, ready in ((0, t1_dve), (1, t1_pool)):
                        act.wait_ge(ready, t + 1)
                        nc.scalar.activation(half(t, mm, 0), t1[:, u, mm, :].rearrange("p (h d) -> p h d", h=H),
                                             ACT.Copy).then_inc(hi_done, 1)

        @block.vector
        def _(dve):
            link = linker(nc, dve, steps)
            link(lambda v: v.tensor_reduce(out=peak[:, 0:4], in_=f12[:, 0:H, :], axis=AX.X, op=ALU.max))
            dve.sem_inc(local_done, 1)
            dve.sem_inc(lo_done, 4)
            dve.wait_ge(g_out, 1)
            for h in range(H):
                c = gmax[:, h:h + 1]
                nc.vector.tensor_scalar(arg[:, 0, h, :], f12[:, h, :], c, SHIFT, ALU.subtract, ALU.add)
                link(lambda v: v.tensor_scalar(arg[:, 1, h, :], f12[:, h, :], c, SLOPE, ALU.subtract, ALU.mult))
            link(lambda v: v.tensor_scalar(arg[:, 1], arg[:, 1], SHIFT, None, ALU.add))
            dve.sem_inc(arg_done, 1)
            power_of_two(link, scale, gmax[:, 4:5], 16384.0)
            link(lambda v: v.tensor_scalar(ratio, scale, 1.0 / DEN, None, ALU.mult))
            dve.wait_ge(e_done, 1)
            key = k.expo[:, 0:2]
            link(lambda v: v.tensor_copy(qb, key))
            link(lambda v: v.tensor_copy(k.qm[:], qb))
            link(lambda v: v.tensor_scalar(arg[:], k.qm[:], 1e-37, None, ALU.max))
            link(lambda v: v.reciprocal(arg[:], arg[:]))
            link(lambda v: v.tensor_tensor(out=key, in0=key, in1=arg[:], op=ALU.mult))
            link(lambda v: v.tensor_scalar(k.qm[:, 1], k.qm[:, 1], -1.0, None, ALU.mult))
            for h in range(H):
                link(lambda v: v.tensor_scalar(arg[:, 0, h, :], f12[:, H + h, :], gmax[:, h:h + 1], 1.0 - SLOPE,
                                               ALU.add, ALU.mult))
            link(lambda v: v.tensor_scalar(arg[:, 1], arg[:, 0], -1.0, 0.0, ALU.mult, ALU.min))
            link(lambda v: v.tensor_scalar(arg[:, 0], arg[:, 0], 0.0, None, ALU.min))
            dve.sem_inc(arg_done, 1)
            dve.wait_ge(e_done, 2)
            link(lambda v: v.tensor_scalar(arg[:], key, DEN, None, ALU.mult))
            for mm in range(2):
                link(lambda v: v.tensor_copy(k.xs[:, :, :, mm, 0, DH], arg[:, mm]))
                link(lambda v: v.tensor_tensor(out=k.xs[:, :, :, mm, 1, DH], in0=arg[:, mm],
                                               in1=k.xs[:, :, :, mm, 0, DH], op=ALU.subtract))
            link(lambda v: v.tensor_scalar(arg[:], key, scale, None, ALU.mult))
            dve.sem_inc(cs_done, 1)

            def scaled(t, u):
                dve.wait_ge(lo_done, t * 2 + 1)
                nc.vector.tensor_tensor(out=t1[:, u, 0, :].rearrange("p (h d) -> p h d", h=H), in0=sup(t),
                                        in1=fac(0, t), op=ALU.mult).then_inc(t1_dve, 1)

            def low(t, u):
                for mm in range(2):
                    dve.wait_ge(hi_done, t * 2 + mm + 1)
                    nc.vector.tensor_tensor(out=half(t, mm, 1), in0=t1[:, u, mm, :].rearrange("p (h d) -> p h d", h=H),
                                            in1=half(t, mm, 0), op=ALU.subtract).then_inc(lo_done, 1)

            scaled(0, 0)
            with dve.Fori(0, NT // 2 - 1) as i:
                for u in range(2):
                    scaled(i * 2 + u + 1, (u + 1) % 2)
                    low(i * 2 + u, u)
            scaled(NT - 1, 1)
            low(NT - 2, 0)
            low(NT - 1, 1)


def attend0(nc, sem, k, adj, y0_dram, f2_dram, x1_dram):
    m = Map(nc, k.at + (X_BYTES + 31) // 32 * 32)
    aT = m("aT", [P, NT, IC], BF16, 2)
    f2b = m("f2b", [P, 2, IC], FP32, 4)
    sign = m("sign", [P, 2, 2, IC], BF16, 2)
    signed = m("signed", [P, 2, 2, IC], BF16, 2)
    mask = m("mask", [P, 4, 2, IC], BF16, 2)
    stage = m("stage", [P, 2, IT, 2 * P], FP32, 4)
    y = m("y", [P, IT, D], FP32, 4)
    part = m("part", [P, IT, XW], FP32, 4)
    dinv = m("dinv", [P, IT], FP32, 4)
    stats = m("stats", [P, IT, 6], FP32, 4)
    mv = m("mv", [P, IT, 2], FP32, 4)
    rstd = m("rstd", [P, IT], FP32, 4)
    assert m.at <= nc.sbuf_usable_end, m.at
    bank, ident, xs = k.bank, k.ident, k.xs
    acc = [bank[0:3], bank[3:6]]
    ratio = k.small[:, 11:12]
    NP = NT // 2

    def slot(s, i):
        return acc[s][i // 3][:, i % 3 * XW:i % 3 * XW + XW]

    names = ("sign_done", "edge_done", "mask_done", "mask_free", "acc_done", "part_done", "acc_free", "aT_ps",
             "aT_done", "aT_last", "y_loaded", "y_final", "y_stored", "sum_done", "den_done", "stat_done", "mv_done",
             "std_done", "inv_done")
    s = {n: sem("a0_" + n) for n in names}
    passed = [sem(f"a0_passed{i}") for i in range(3)]
    stage_in = [sem(f"a0_stage_in{i}") for i in range(2)]
    f2_in = [sem(f"a0_f2_in{h}") for h in range(2)]
    SIGN0, EDGE0, MASK0, FREE0, APS0, AT0 = 17, 2, 3, 4, 3, 1

    adj_r = adj.rearrange("(c i p) n -> p c i n", i=IT, p=P)
    y0_r = y0_dram.rearrange("(c i p) d -> p c i d", i=IT, p=P)
    x1_r = x1_dram.rearrange("(c i p) d -> p c i d", i=IT, p=P)
    f2_r = f2_dram.rearrange("(h c i) p -> h c (i p)", h=H, i=IT)

    with nc.Block() as block:

        @block.sync
        def _(sp):
            def load_adj(c):
                with sp.Fori(0, NP // 2) as q:
                    for u in range(2):
                        wait_apart(sp, s["aT_ps"], (c * NP + q * 2 + u) * 2 - 2 + APS0, passed[0])
                        sp.dma_start(stage[:, u, :, :],
                                     adj_r[:, bass.ds(c, 1), :, bass.ds(q * 512 + u * 256, 256)].rearrange(
                                         "p c i n -> p (c i) n")).then_inc(stage_in[u], 16)

            def load_f2(c, h):
                wait_apart(sp, s["sign_done"], (c * H + h - 1) * NP + SIGN0, passed[0])
                sp.dma_start(f2b[:, h % 2, :],
                             f2_r[h, bass.ds(c, 1), :].rearrange("a n -> (a n)").partition_broadcast(P)
                             ).then_inc(f2_in[h % 2], 16)

            def store_y(c):
                wait_apart(sp, s["y_final"], c + 1, passed[0])
                sp.dma_start(x1_r[:, bass.ds(c, 1), :, :].rearrange("p c i d -> p (c i) d"), y[:]
                             ).then_inc(s["y_stored"], 16)
                wait_apart(sp, s["y_stored"], c * 16 + 16, passed[0])

            def load_y(c):
                sp.dma_start(y[:], y0_r[:, bass.ds(c, 1), :, :].rearrange("p c i d -> p (c i) d")
                             ).then_inc(s["y_loaded"], 16)

            load_f2(0, 0)
            load_adj(0)
            load_f2(0, 1)
            load_y(0)

            def chunk(c):
                load_f2(c, 2)
                load_f2(c, 3)
                load_f2(c + 1, 0)
                load_adj(c + 1)
                load_f2(c + 1, 1)

            chunk(0)
            with sp.Fori(1, NIC - 1) as c:
                store_y(c - 1)
                load_y(c)
                chunk(c)
            store_y(NIC - 2)
            load_y(NIC - 1)
            load_f2(NIC - 1, 2)
            load_f2(NIC - 1, 3)
            store_y(NIC - 1)

        def transpose_pair(pe, c, q, u):
            pe.wait_ge(stage_in[u], (c * (NP // 2) + q) * 16 + 16)
            quad = c * NQ + q
            for j in range(2):
                if (u, j) == (0, 1):
                    pe.wait_ge(s["aT_last"], quad + AT0)
                else:
                    pe.wait_ge(s["aT_done"], quad * 3 + u + (u and j) + AT0)
                for i in range(IT):
                    last = nc.tensor.transpose(bank[6 + j][:, i * P:(i + 1) * P],
                                               stage[:, u, i, j * P:(j + 1) * P], ident[:])
                last.then_inc(s["aT_ps"], 1)

        @block.tensor
        def _(pe):
            pe.sem_inc(s["aT_ps"], APS0)

            def products(c, h, q, first=False, last_quad=False, tr=None):
                hh = c * H + h
                for t4 in range(4):
                    if tr is not None and t4 % 2 == 0:
                        transpose_pair(pe, tr, q, t4 // 2)
                    pe.wait_ge(s["mask_done"], hh * NT + q * 4 + t4 + 1 + MASK0)
                    for i in range(2 * IT):
                        br, it = i // IT, i % IT
                        for pt in range(2):
                            begin = first and t4 == 0 and pt == 0 and i % 3 == 0
                            end = last_quad and t4 == 3 and pt == 1
                            op = nc.tensor.matmul(slot(h % 2, i), mask[:, t4, br, it * P:(it + 1) * P],
                                                  xs[:, h, bass.ds(q * 4 + t4, 1), br, pt, 0:XW].rearrange(
                                                      "p a n -> p (a n)"),
                                                  start=begin, stop=end, skip_group_check=True)
                    op.then_inc(s["mask_free"], 1)

            def chunk(c, tr):
                for h in range(H):
                    pe.wait_ge(s["acc_free"], c * H + h + 1)
                    t = tr if h == H - 1 else None
                    products(c, h, 0, first=True, tr=t)
                    with pe.Fori(1, NQ - 1) as q:
                        products(c, h, q, tr=t)
                    products(c, h, NQ - 1, last_quad=True, tr=t)

            with pe.Fori(0, NP // 2) as q:
                for u in range(2):
                    transpose_pair(pe, 0, q, u)
            chunk(0, 1)
            with pe.Fori(1, NIC - 1) as c:
                chunk(c, c + 1)
            chunk(NIC - 1, None)

        @block.scalar
        def _(act):
            act.sem_inc(s["sign_done"], SIGN0)
            act.sem_inc(s["aT_done"], AT0)

            def copy(c, q, u):
                for t4 in ((0, 1), (2,))[u]:
                    act.wait_ge(s["aT_ps"], c * NT + q * 4 + t4 + 1 + APS0)
                    nc.scalar.activation(flat(aT[:, bass.ds(q * 4 + t4, 1), :]), bank[6 + t4 % 2][:],
                                         ACT.Copy).then_inc(s["aT_done"], 1)

            def signs(c, h, q, tr=None, tr_q=None):
                for u in range(2):
                    act.wait_ge(s["edge_done"], (c * H + h) * NP + q * 2 + u - 1 + EDGE0)
                    for j in range(2):
                        last = nc.scalar.activation(sign[:, u, j, :], f2b[:, h % 2, :], ACT.Sign,
                                                    bias=k.f12[:, h, bass.ds(q * 4 + 2 * u + j, 1)])
                    last.then_inc(s["sign_done"], 1)
                    if tr is not None:
                        copy(tr, tr_q, u)

            def read_out(c, h, st):
                hh = c * H + h
                act.wait_ge(s["mask_free"], hh * NT + NT + 4)
                act.wait_ge(s["acc_free"], hh + 2)
                for i in range(IT):
                    last = nc.scalar.activation(part[:, i, :], slot(st, i), ACT.Copy,
                                                scale=k.expo[:, 2, h, bass.ds(c * IT + i, 1)])
                last.then_inc(s["part_done"], 1)

            def deviation(c):
                act.wait_ge(s["mv_done"], c * 2 + 2)
                nc.scalar.activation(rstd[:], mv[:, :, 1], ACT.Sqrt).then_inc(s["std_done"], 1)

            def chunk(c, tr, prev):
                for h in range(H):
                    t = tr if h == H - 1 else None
                    act.wait_ge(f2_in[h % 2], (c * 2 + h // 2) * 16 + 16)
                    if h == 0 and prev is not None:
                        signs(c, h, 0, c, NQ - 1)
                        read_out(prev, H - 1, 1)
                    else:
                        signs(c, h, 0)
                        if h:
                            read_out(c, h - 1, (h - 1) % 2)
                    start = 1
                    if h == 0 and prev is not None:
                        for q in range(1, 5):
                            signs(c, h, q)
                        deviation(prev)
                        start = 5
                    with act.Fori(start, NQ) as q:
                        signs(c, h, q, t, q - 1)

            with act.Fori(0, NP // 2) as q:
                for u in range(2):
                    copy(0, q, u)
            chunk(0, 1, None)
            with act.Fori(1, NIC - 1) as c:
                chunk(c, c + 1, c - 1)
            chunk(NIC - 1, None, NIC - 2)
            read_out(NIC - 1, H - 1, 1)
            deviation(NIC - 1)

        @block.vector
        def _(dve):
            dve.sem_inc(s["edge_done"], EDGE0)
            dve.sem_inc(s["aT_last"], AT0)
            dve.sem_inc(s["mask_done"], MASK0)
            dve.sem_inc(s["mask_free"], FREE0)
            dve.sem_inc(s["acc_free"], 2)

            def edges(c, h, q, u):
                pair = (c * H + h) * NP + q * 2 + u
                if h == 0:
                    dve.wait_ge(s["aT_done"], (c * NQ + q) * 3 + 2 + u + AT0)
                    if u:
                        dve.wait_ge(s["aT_last"], c * NQ + q + 1 + AT0)
                dve.wait_ge(s["mask_done"], pair * 2 - 2 + MASK0)
                dve.wait_ge(s["sign_done"], pair + 1 + SIGN0)
                nc.vector.tensor_tensor(out=signed[:, u, :, :].rearrange("p j n -> p (j n)"),
                                        in0=sign[:, u, :, :].rearrange("p j n -> p (j n)"),
                                        in1=aT[:, bass.ds(q * 4 + 2 * u, 2), :].rearrange("p j n -> p (j n)"),
                                        op=ALU.mult).then_inc(s["edge_done"], 1)

            def branches(c, h, q, u, j):
                t4 = 2 * u + j
                dve.wait_ge(s["mask_free"], (c * H + h) * NT + q * 4 + t4 - 3 + FREE0)
                for br, op in ((0, ALU.max), (1, ALU.min)):
                    last = nc.vector.tensor_scalar(mask[:, t4, br, :], signed[:, u, j, :], 0.0,
                                                   k.qm[:, br, h, bass.ds(q * 4 + t4, 1)], op, ALU.mult)
                last.then_inc(s["mask_done"], 1)

            def copy_last(c, q):
                dve.wait_ge(s["edge_done"], edges_before(c, q))
                dve.wait_ge(s["aT_ps"], c * NT + q * 4 + 4 + APS0)
                nc.vector.tensor_copy(flat(aT[:, bass.ds(q * 4 + 3, 1), :]), bank[7][:]).then_inc(s["aT_last"], 1)

            def edges_before(c, q):
                return ((c - 1) * H + H - 1) * NP + q * 2 + 2 + EDGE0

            def masks(c, h, q, following, tr=None, tr_q=None):
                for u in range(2):
                    dve.wait_ge(s["edge_done"], (c * H + h) * NP + q * 2 + u + 1 + EDGE0)
                    branches(c, h, q, u, 0)
                    if u == 0:
                        edges(c, h, q, 1)
                    elif following is not None:
                        edges(*following, 0)
                    branches(c, h, q, u, 1)
                    if u == 0 and tr is not None:
                        copy_last(tr, tr_q)

            def read_out(c, h, st):
                hh = c * H + h
                dve.wait_ge(s["part_done"], hh + 1)
                for i in range(IT):
                    nc.vector.scalar_tensor_tensor(
                        out=part[:, i, :], in0=slot(st, IT + i), scalar=k.expo[:, 3, h, bass.ds(c * IT + i, 1)],
                        in1=part[:, i, :], op0=ALU.mult, op1=ALU.add).then_inc(s["sum_done"], 1)

            def divide(c, h):
                hh = c * H + h
                dve.wait_ge(s["sum_done"], (hh + 1) * IT)
                dve.wait_ge(s["acc_free"], hh + 2)
                nc.vector.tensor_scalar(dinv[:], part[:, :, DH], 1e-30, ratio, ALU.max, ALU.mult
                                        ).then_inc(s["den_done"], 1)
                dve.wait_ge(s["den_done"], hh * 2 + 1)
                nc.vector.reciprocal(dinv[:], dinv[:]).then_inc(s["den_done"], 1)
                dve.wait_ge(s["den_done"], hh * 2 + 2)
                if h == 0:
                    dve.wait_ge(s["y_loaded"], c * 16 + 16)
                for i in range(IT):
                    ys = y[:, i, h * DH:(h + 1) * DH]
                    last = nc.vector.scalar_tensor_tensor(out=ys, in0=part[:, i, 0:DH], scalar=dinv[:, i:i + 1],
                                                          in1=ys, op0=ALU.mult, op1=ALU.add)
                last.then_inc(s["acc_free"], 1)

            def moments(c):
                dve.wait_ge(s["acc_free"], c * H + H + 2)
                for i in range(IT):
                    last = nc.vector.bn_stats(stats[:, i, :], y[:, i, :])
                last.then_inc(s["stat_done"], 1)
                wait_apart(dve, s["stat_done"], c + 1, passed[2])
                for i in range(IT):
                    last = nc.vector.bn_aggr(mv[:, i, :], stats[:, i, :])
                last.then_inc(s["mv_done"], 1)
                dve.wait_ge(s["mv_done"], c * 2 + 1)
                nc.vector.tensor_scalar(mv[:, :, 1], mv[:, :, 1], EPS, None, ALU.add).then_inc(s["mv_done"], 1)

            def normalize(c):
                dve.wait_ge(s["std_done"], c + 1)
                nc.vector.reciprocal(rstd[:], rstd[:]).then_inc(s["inv_done"], 1)
                dve.wait_ge(s["inv_done"], c + 1)
                for i in range(IT):
                    last = nc.vector.tensor_scalar(y[:, i, :], y[:, i, :], mv[:, i, 0:1], rstd[:, i:i + 1],
                                                   ALU.subtract, ALU.mult)
                last.then_inc(s["y_final"], 1)

            def chunk(c, prev, last=False):
                for h in range(H):
                    tr = c + 1 if h == H - 1 and not last else None
                    ph = (c, h - 1) if h else (prev, H - 1)
                    ended = prev is not None and h == 0
                    masks(c, h, 0, (c, h, 1), c if ended else None, NQ - 1)
                    masks(c, h, 1, (c, h, 2), tr, 0)
                    if ph[0] is not None:
                        read_out(*ph, ph[1] % 2)
                    masks(c, h, 2, (c, h, 3), tr, 1)
                    if ph[0] is not None:
                        divide(*ph)
                    start = 3
                    if ended:
                        masks(c, h, 3, (c, h, 4))
                        moments(prev)
                        masks(c, h, 4, (c, h, 5))
                        normalize(prev)
                        start = 5
                    with dve.Fori(start, NQ - 1) as q:
                        masks(c, h, q, (c, h, q + 1), tr, q - 1)
                    masks(c, h, NQ - 1, (c, h + 1, 0) if h < H - 1 else None if last else (c + 1, 0, 0),
                          tr, NQ - 2)

            with dve.Fori(0, NQ) as q:
                dve.wait_ge(s["aT_ps"], q * 4 + 4 + APS0)
                nc.vector.tensor_copy(flat(aT[:, bass.ds(q * 4 + 3, 1), :]), bank[7][:]).then_inc(s["aT_last"], 1)
            edges(0, 0, 0, 0)
            chunk(0, None)
            with dve.Fori(1, NIC - 1) as c:
                chunk(c, c - 1)
            chunk(NIC - 1, NIC - 2, last=True)
            read_out(NIC - 1, H - 1, 1)
            divide(NIC - 1, H - 1)
            moments(NIC - 1)
            normalize(NIC - 1)


def project1(nc, sem, k, w1, nw, ew, x1_dram):
    m = Map(nc, k.at)
    k.hT = m("hT", [P, 2, KT, N], F16, 2)
    k.v = m("v", [P, 2, NT, D], F16, 2)
    k.free = m.at
    w_sb = m("w1_sb", [P, KT, D], FP32, 4)
    e_sb = m("e1_sb", [P, KT, D], FP32, 4)
    x_in = m("x1_in", [P, 2, IT, D], FP32, 4)
    xT = m("x1T", [P, 2, KT, IC], FP32, 4)
    n_bc = m("n_bc", [P, D], FP32, 4)
    prod = m("prod1", [P, IT, D], FP32, 4)
    assert m.at <= nc.sbuf_usable_end, m.at
    bank, ident, small = k.bank, k.ident, k.small
    peak, gmax = small[:, 12:14], small[:, 14:16]
    s_e, s_w, k.inv_e2, k.inv_w = small[:, 16:17], small[:, 17:18], small[:, 18:19], small[:, 19:20]

    steps, w_in, n_in, g_in, g_out, scale_done, xT_ps, xT_done, mm, hi, lo, prod_done, score_done, node_max, \
        node_exp, node_sum = (sem("p2_" + n) for n in (
            "steps", "w_in", "n_in", "g_in", "g_out", "scale_done", "xT_ps", "xT_done", "mm", "hi", "lo",
            "prod_done", "score_done", "node_max", "node_exp", "node_sum"))
    passed = [sem(f"p2_passed{i}") for i in range(3)]
    x_loaded = [sem(f"p2_x_loaded{i}") for i in range(2)]
    x1_r = x1_dram.rearrange("(c i p) d -> p c i d", i=IT, p=P)
    NJ = KT + IT

    with nc.Block() as block:

        @block.sync
        def _(sp):
            sp.dma_start(w_sb[:], w1.rearrange("(k p) d -> p k d", p=P)).then_inc(w_in, 16)
            sp.dma_start(e_sb[:], ew.rearrange("(k p) d -> p k d", p=P)).then_inc(w_in, 16)
            sp.dma_start(n_bc[:], nw.rearrange("d o -> (d o)").partition_broadcast(P)).then_inc(n_in, 16)
            with sp.Fori(0, NIC // 2) as c2:
                for u in range(2):
                    wait_apart(sp, score_done, c2 * 2 + u + 1, passed[0])
                    sp.dma_start(x_in[:, u, :, :], x1_r[:, bass.ds(c2 * 2 + u, 1), :, :].rearrange(
                        "p c i d -> p (c i) d")).then_inc(x_loaded[u], 16)

        @block.gpsimd
        def _(pool):
            pool.wait_ge(g_in, 1)
            nc.gpsimd.partition_all_reduce(gmax, peak, P, RMAX).then_inc(g_out, 1)
            pool.wait_ge(node_max, 1)
            nc.gpsimd.partition_all_reduce(small[:, 21:22], small[:, 20:21], P, RMAX).then_inc(node_max, 1)
            pool.wait_ge(node_exp, 2)
            nc.gpsimd.partition_all_reduce(small[:, 24:25], small[:, 23:24], P, RADD).then_inc(node_sum, 1)

        @block.tensor
        def _(pe):
            def transposes(c2, u):
                c = c2 * 2 + u
                pe.wait_ge(x_loaded[u], c2 * 16 + 16)
                for j in range(KT):
                    pe.wait_ge(xT_done, c * KT + j + 1)
                    for i in range(IT):
                        last = nc.tensor.transpose(bank[j % 2][:, i * P:(i + 1) * P],
                                                   x_in[:, u, i, j * P:(j + 1) * P], ident[:])
                    last.then_inc(xT_ps, 1)

            def product(c2, u, j):
                c = c2 * 2 + u
                pe.wait_ge(lo, c * NJ + j + 1)
                for i in range(KT):
                    if j < KT:
                        left, right = e_sb[:, i, j * P:(j + 1) * P], xT[:, u, i, :]
                    else:
                        left, right = xT[:, u, i, (j - KT) * P:(j - KT + 1) * P], w_sb[:, i, :]
                    last = nc.tensor.matmul(bank[2 + j % 4][:], left, right, start=(i == 0), stop=(i == KT - 1))
                last.then_inc(mm, 1)

            def chunk(c2, u, following):
                pe.wait_ge(xT_done, (c2 * 2 + u) * KT + KT + 2)
                for j in range(NJ):
                    product(c2, u, j)
                    if j == 3 and following is not None:
                        transposes(*following)

            pe.wait_ge(w_in, 32)
            transposes(0, 0)
            with pe.Fori(0, NIC // 2 - 1) as c2:
                chunk(c2, 0, (c2, 1))
                chunk(c2, 1, (c2 + 1, 0))
            chunk(NIC // 2 - 1, 0, (NIC // 2 - 1, 1))
            chunk(NIC // 2 - 1, 1, None)

        def place(c2, u, j, part):
            c = c2 * 2 + u
            if j < KT:
                return k.hT[:, part, j, bass.ds(c * IC, IC)]
            return flat(k.v[:, part, bass.ds(c * IT + (j - KT), 1), :])

        @block.scalar
        def _(act):
            act.sem_inc(xT_done, 2)

            def copies(c2, u):
                c = c2 * 2 + u
                for j in range(KT):
                    act.wait_ge(xT_ps, c * KT + j + 1)
                    nc.scalar.activation(xT[:, u, j, :], bank[j % 2][:], ACT.Copy).then_inc(xT_done, 1)

            def split(c2, u, following):
                for j in range(NJ):
                    act.wait_ge(mm, (c2 * 2 + u) * NJ + j + 1)
                    nc.scalar.activation(place(c2, u, j, 0), bank[2 + j % 4][:], ACT.Copy,
                                         scale=(s_e if j < KT else s_w)).then_inc(hi, 1)
                    if j == 3 and following is not None:
                        copies(*following)

            copies(0, 0)
            act.wait_ge(scale_done, 1)
            with act.Fori(0, NIC // 2 - 1) as c2:
                split(c2, 0, (c2, 1))
                split(c2, 1, (c2 + 1, 0))
            split(NIC // 2 - 1, 0, (NIC // 2 - 1, 1))
            split(NIC // 2 - 1, 1, None)
            act.wait_ge(node_max, 3)
            nc.scalar.activation(k.score[:], k.score[:], ACT.Exp, bias=small[:, 22:23],
                                 accum_out=small[:, 23:24]).then_inc(node_exp, 2)

        @block.vector
        def _(dve):
            dve.sem_inc(lo, 4)
            dve.sem_inc(score_done, 2)
            link = linker(nc, dve, steps)
            dve.wait_ge(w_in, 32)
            for i, w in enumerate((e_sb, w_sb)):
                link(lambda v: v.tensor_reduce(out=peak[:, i:i + 1], in_=w[:].rearrange("p k d -> p (k d)"),
                                               axis=AX.X, op=ALU.max, apply_absolute_value=True))
            dve.sem_inc(g_in, 1)
            dve.wait_ge(g_out, 1)
            power_of_two(link, small[:, 16:18], gmax, 64.0)
            link(lambda v: v.reciprocal(small[:, 18:20], small[:, 16:18]))
            link(lambda v: v.tensor_scalar(k.inv_e2, k.inv_e2, k.inv_e2, None, ALU.mult))
            dve.sem_inc(scale_done, 1)
            dve.wait_ge(n_in, 16)

            def chunk(c2, u):
                c = c2 * 2 + u
                dve.wait_ge(x_loaded[u], c2 * 16 + 16)
                for i in range(IT):
                    last = nc.vector.tensor_tensor(out=prod[:, i, :], in0=x_in[:, u, i, :], in1=n_bc[:], op=ALU.mult)
                last.then_inc(prod_done, 1)
                for j in range(NJ):
                    dve.wait_ge(hi, c * NJ + j + 1)
                    nc.vector.scalar_tensor_tensor(out=place(c2, u, j, 1), in0=bank[2 + j % 4][:],
                                                   scalar=(s_e if j < KT else s_w), in1=place(c2, u, j, 0),
                                                   op0=ALU.mult, op1=ALU.subtract).then_inc(lo, 1)
                    if j == 0:
                        dve.wait_ge(prod_done, c + 1)
                        nc.vector.tensor_reduce(out=k.score[:, bass.ds(c * IT, IT)], in_=prod[:], axis=AX.X,
                                                op=ALU.add).then_inc(score_done, 1)

            with dve.Fori(0, NIC // 2) as c2:
                for u in range(2):
                    chunk(c2, u)
            dve.wait_ge(score_done, NIC + 2)
            link(lambda v: v.tensor_reduce(out=small[:, 20:21], in_=k.score[:], axis=AX.X, op=ALU.max))
            dve.sem_inc(node_max, 1)
            dve.wait_ge(node_max, 2)
            link(lambda v: v.tensor_scalar(small[:, 22:23], small[:, 21:22], -1.0, None, ALU.mult))
            dve.sem_inc(node_max, 1)
            dve.wait_ge(node_sum, 1)
            link(lambda v: v.reciprocal(small[:, 25:26], small[:, 24:25]))
            link(lambda v: v.tensor_scalar(k.score[:], k.score[:], small[:, 25:26], k.inv_w, ALU.mult, ALU.mult))


def attend1(nc, sem, k, adj, b1, x1_dram, out):
    m = Map(nc, k.free)
    pr = m("pr", [P, 2, N], FP32, 4)
    NM = 4
    QW = N // NM
    neg = m("neg", [P, NM, QW], FP32, 4)
    pT = m("pT", [P, 2, 2, IC], F16, 2)
    xr = m("xr", [P, 2, D], FP32, 4)
    bias = m("bias1", [P, D], FP32, 4)
    cmax = m("cmax", [P, 2, 8], FP32, 4)
    st = m("st1", [P, 2, 16], FP32, 4)
    assert m.at <= nc.sbuf_usable_end, m.at
    bank, ident, hT, v = k.bank, k.ident, k.hT, k.v
    NC = N // IC
    names = ("neg_done", "qk", "s_done", "max_done", "bias_done", "exp_done", "coef_done",
             "pT_ps", "hi", "lo", "pv", "x_biased", "sum_done", "stat_done", "mv_done", "std_done", "inv_done",
             "norm_done", "b_in")
    s = {n: sem("a1_" + n) for n in names}
    passed = [sem(f"a1_passed{i}") for i in range(3)]
    neg_in = [sem(f"a1_neg_in{i}") for i in range(NM)]
    x_in = [sem(f"a1_x_in{i}") for i in range(2)]
    o_out = [sem(f"a1_o_out{i}") for i in range(2)]
    S0 = 8
    adj_r = adj.rearrange("(t p) n -> p t n", p=P)
    x1_r = x1_dram.rearrange("(t p) d -> p t d", p=P)
    out_r = out.rearrange("(t p) d -> p t d", p=P)

    with nc.Block() as block:

        @block.sync
        def _(sp):
            sp.dma_start(bias[:], b1.partition_broadcast(P)).then_inc(s["b_in"], 16)

            def tile(t, u, first=False):
                for i in range(NM):
                    wait_apart(sp, s["s_done"], (t - 1) * NC + 2 * i + 2 + S0, passed[0])
                    sp.dma_start(neg[:, i:i + 1, :], adj_r[:, bass.ds(t, 1), i * QW:(i + 1) * QW]
                                 ).then_inc(neg_in[i], 16)
                    if i == 1:
                        if not first:
                            wait_apart(sp, s["norm_done"], t + 1, passed[0])
                            sp.dma_start(out_r[:, bass.ds(t - 2, 1), :], xr[:, u:u + 1, :]).then_inc(o_out[u], 16)
                            wait_apart(sp, o_out[u], (t - u) * 8, passed[0])
                        sp.dma_start(xr[:, u:u + 1, :], x1_r[:, bass.ds(t, 1), :]).then_inc(x_in[u], 16)

            tile(0, 0, True)
            tile(1, 1, True)
            with sp.Fori(1, NT // 2) as i2:
                for u in range(2):
                    tile(i2 * 2 + u, u)
            for u in range(2):
                sp.wait_ge(s["norm_done"], NT + u + 1)
                sp.dma_start(out_r[:, NT - 2 + u, :], xr[:, u, :]).then_inc(o_out[u], 16)
            for u in range(2):
                sp.wait_ge(o_out[u], NT // 2 * 16)

        @block.gpsimd
        def _(pool):
            pool.wait_ge(s["b_in"], 16)
            with pool.Fori(0, NT // 2) as i2:
                for u in range(2):
                    t = i2 * 2 + u
                    for i in range(NM):
                        wait_apart(pool, neg_in[i], t * 16 + 16, passed[1])
                        nc.gpsimd.tensor_scalar(neg[:, i, :], neg[:, i, :], -1.0, BIG, ALU.add, ALU.mult
                                                ).then_inc(s["neg_done"], 1)
                    pool.wait_ge(x_in[u], i2 * 16 + 16)
                    nc.gpsimd.tensor_tensor(out=xr[:, u, :], in0=xr[:, u, :], in1=bias[:], op=ALU.add
                                            ).then_inc(s["x_biased"], 1)

        @block.tensor
        def _(pe):
            def logits(t, c):
                pe.wait_ge(s["s_done"], t * NC + c - 3 + S0)
                n = 0
                for a, b in ((0, 0), (0, 1), (1, 0)):
                    for j in range(KT):
                        last = nc.tensor.matmul(bank[c % 4][:], hT[:, a, j, bass.ds(t * P, P)],
                                                hT[:, b, j, c * IC:(c + 1) * IC], start=(n == 0), stop=(n == 11))
                        n += 1
                last.then_inc(s["qk"], 1)

            def transposes(t, u, g):
                pe.wait_ge(s["exp_done"], t + 1)
                pe.wait_ge(s["lo"], t * NC + g + 1)
                for j in range(4):
                    last = nc.tensor.transpose(bank[4 + g % 2][:, j * P:(j + 1) * P],
                                               pr[:, u, (g * 4 + j) * P:(g * 4 + j + 1) * P], ident[:])
                last.then_inc(s["pT_ps"], 1)

            def values(t, u, g):
                pe.wait_ge(s["lo"], t * NC + g + 3)
                if g == 0:
                    pe.wait_ge(s["sum_done"], t + 1)
                for j in range(4):
                    for a, b in ((0, 0), (0, 1), (1, 0)):
                        last = nc.tensor.matmul(bank[6 + u][:], pT[:, g % 2, a, j * P:(j + 1) * P],
                                                v[:, b, g * 4 + j, :], start=(g == 0 and j == 0 and a == b),
                                                stop=(g == NC - 1 and j == 3 and a == 1))
                last.then_inc(s["pv"], 1)

            def step(t, u, rows=True, prev=True):
                for c in range(NC):
                    if rows:
                        logits(t, c)
                    if prev and c >= 2:
                        transposes(t - 1, 1 - u, c - 2)
                        if c >= 3:
                            values(t - 1, 1 - u, c - 3)
                if prev:
                    transposes(t - 1, 1 - u, NC - 2)
                    values(t - 1, 1 - u, NC - 3)
                    transposes(t - 1, 1 - u, NC - 1)
                    values(t - 1, 1 - u, NC - 2)
                    values(t - 1, 1 - u, NC - 1)

            step(0, 0, prev=False)
            with pe.Fori(0, NT // 2 - 1) as i2:
                step(i2 * 2 + 1, 1)
                step(i2 * 2 + 2, 0)
            step(NT - 1, 1)
            step(NT, 0, rows=False)

        @block.scalar
        def _(act):
            def exps(t, u):
                act.wait_ge(s["bias_done"], t + 1)
                nc.scalar.activation(pr[:, u, :], pr[:, u, :], ACT.Exp, bias=st[:, u, 1:2], scale=k.inv_e2,
                                     accum_out=st[:, u, 2:3]).then_inc(s["exp_done"], 1)

            def high(t, u, g):
                act.wait_ge(s["pT_ps"], t * NC + g + 1)
                act.wait_ge(s["pv"], t * NC + g + 1)
                nc.scalar.activation(pT[:, g % 2, 0, :], bank[4 + g % 2][:], ACT.Copy).then_inc(s["hi"], 1)

            def deviation(t, u):
                act.wait_ge(s["mv_done"], t * 2 + 2)
                nc.scalar.activation(st[:, u, 13:14], st[:, u, 12:13], ACT.Sqrt).then_inc(s["std_done"], 1)

            def step(t, u, prev=True):
                exps(t, u)
                if prev:
                    deviation(t - 1, 1 - u)
                for g in range(NC):
                    high(t, u, g)

            act.sem_inc(s["pv"], 2)
            step(0, 0, prev=False)
            with act.Fori(0, NT // 2 - 1) as i2:
                step(i2 * 2 + 1, 1)
                step(i2 * 2 + 2, 0)
            step(NT - 1, 1)
            deviation(NT - 1, 1)

        @block.vector
        def _(dve):
            dve.sem_inc(s["s_done"], S0)
            dve.sem_inc(s["lo"], 2)
            dve.sem_inc(s["norm_done"], 2)
            dve.sem_inc(s["sum_done"], 2)

            def mask_chunk(t, u, c):
                if c % 2 == 0:
                    dve.wait_ge(s["neg_done"], t * NM + c // 2 + 1)
                wait_apart(dve, s["qk"], t * NC + c + 1, passed[2])
                nc.vector.tensor_tensor_reduce(out=pr[:, u, c * IC:(c + 1) * IC], in0=bank[c % 4][:],
                                               in1=neg[:, c // 2, c % 2 * IC:(c % 2 + 1) * IC], scale=1.0,
                                               scalar=-3.3e38, op0=ALU.add, op1=ALU.max,
                                               accum_out=cmax[:, u, c:c + 1]).then_inc(s["s_done"], 1)

            def row_max(t, u):
                dve.wait_ge(s["s_done"], t * NC + NC + S0)
                nc.vector.tensor_reduce(out=st[:, u, 0:1], in_=cmax[:, u, :], axis=AX.X, op=ALU.max
                                        ).then_inc(s["max_done"], 1)
                dve.wait_ge(s["max_done"], t * 3 + 1)
                nc.vector.tensor_scalar(st[:, u, 3:4], st[:, u, 0:1], k.inv_e2, -1.0, ALU.mult, ALU.mult
                                        ).then_inc(s["max_done"], 1)
                dve.wait_ge(s["max_done"], t * 3 + 2)
                nc.vector.tensor_scalar(st[:, u, 1:2], st[:, u, 3:4], PSCALE, None, ALU.add
                                        ).then_inc(s["bias_done"], 1)
                nc.vector.tensor_scalar(st[:, u, 4:5], st[:, u, 0:1], -1.0e38, k.score[:, bass.ds(t, 1)],
                                        ALU.is_gt, ALU.mult).then_inc(s["max_done"], 1)

            def low(t, u, g):
                dve.wait_ge(s["hi"], t * NC + g + 1)
                nc.vector.tensor_tensor(out=pT[:, g % 2, 1, :], in0=bank[4 + g % 2][:], in1=pT[:, g % 2, 0, :],
                                        op=ALU.subtract).then_inc(s["lo"], 1)

            def coef(t, u):
                dve.wait_ge(s["exp_done"], t + 1)
                dve.wait_ge(s["max_done"], t * 3 + 3)
                nc.vector.reciprocal(st[:, u, 5:6], st[:, u, 2:3]).then_inc(s["coef_done"], 1)
                dve.wait_ge(s["coef_done"], t * 2 + 1)
                nc.vector.tensor_scalar(st[:, u, 5:6], st[:, u, 5:6], st[:, u, 4:5], None, ALU.mult
                                        ).then_inc(s["coef_done"], 1)

            def total(t, u):
                dve.wait_ge(s["pv"], t * NC + NC + 2)
                dve.wait_ge(s["coef_done"], t * 2 + 2)
                dve.wait_ge(s["x_biased"], t + 1)
                nc.vector.scalar_tensor_tensor(out=xr[:, u, :], in0=bank[6 + u][:], scalar=st[:, u, 5:6],
                                               in1=xr[:, u, :], op0=ALU.mult, op1=ALU.add).then_inc(s["sum_done"], 1)
                dve.wait_ge(s["sum_done"], t + 3)
                nc.vector.bn_stats(st[:, u, 6:12], xr[:, u, :]).then_inc(s["stat_done"], 1)
                wait_apart(dve, s["stat_done"], t + 1, passed[2])
                nc.vector.bn_aggr(st[:, u, 14:16], st[:, u, 6:12]).then_inc(s["mv_done"], 1)
                dve.wait_ge(s["mv_done"], t * 2 + 1)
                nc.vector.tensor_scalar(st[:, u, 12:13], st[:, u, 15:16], EPS, None, ALU.add
                                        ).then_inc(s["mv_done"], 1)

            def normalize(t, u):
                dve.wait_ge(s["std_done"], t + 1)
                nc.vector.reciprocal(st[:, u, 13:14], st[:, u, 13:14]).then_inc(s["inv_done"], 1)
                dve.wait_ge(s["inv_done"], t + 1)
                nc.vector.tensor_scalar(xr[:, u, :], xr[:, u, :], st[:, u, 14:15], st[:, u, 13:14],
                                        ALU.subtract, ALU.mult).then_inc(s["norm_done"], 1)

            def step(t, u, rows=True, prev=True, prev2=True):
                w = 1 - u
                for c in range(NC):
                    if rows:
                        mask_chunk(t, u, c)
                    if c == 0:
                        if prev:
                            coef(t - 1, w)
                        if prev2:
                            total(t - 2, u)
                    if c == 2 and prev2:
                        normalize(t - 2, u)
                    if prev and c >= 2:
                        low(t - 1, w, c - 2)
                if rows:
                    row_max(t, u)
                if prev:
                    low(t - 1, w, NC - 2)
                    low(t - 1, w, NC - 1)

            step(0, 0, prev=False, prev2=False)
            step(1, 1, prev2=False)
            with dve.Fori(1, NT // 2) as i2:
                step(i2 * 2, 0)
                step(i2 * 2 + 1, 1)
            step(NT, 0, rows=False)
            total(NT - 1, 1)
            normalize(NT - 1, 1)


_INS = ["x", "adj", "L0_gnn_weight", "L0_gnn_weight_u", "L0_gnn_weight_v", "L0_gnn_bias", "L0_gnn_proj_w",
        "L0_gnn_proj_b", "L1_gnn_weight", "L1_gnn_bias", "L1_gnn_node_w", "L1_gnn_edge_w"]


def kernel(**inputs):
    import numpy as _np
    import concourse.bacc as _bacc
    from concourse import mybir as _mybir
    from concourse.bass_utils import run_bass_kernel_spmd as _run

    nc = _bacc.Bacc("TRN2", target_bir_lowering=False, num_devices=1)
    arrays, args = {}, []
    for name in _INS:
        a = _np.ascontiguousarray(inputs[name])
        arrays[f"in_{name}_dram"] = a
        args.append(nc.dram_tensor(f"in_{name}_dram", a.shape, _mybir.dt.from_np(a.dtype), kind="ExternalInput").ap())
    args.append(nc.dram_tensor("out_0_dram", (N, D), FP32, kind="ExternalOutput").ap())
    build(nc, *args)
    r = _run(nc, [arrays], core_ids=[0])
    return r.results[0]["out_0_dram"]
```

```python
import numpy as np
import concourse.bass as bass
from concourse import mybir
from contextlib import ExitStack

FP32 = mybir.dt.float32
F16 = mybir.dt.float16
BF16 = mybir.dt.bfloat16
U32 = mybir.dt.uint32
ALU = mybir.AluOpType
ACT = mybir.ActivationFunctionType
AX = mybir.AxisListType
RMAX = bass.bass_isa.ReduceOp.max
RADD = bass.bass_isa.ReduceOp.add

P = 128
N = 4096
D = 512
H = 4
DH = D // H
NT = N // P
KT = D // P
IC = 512
NIC = N // IC
IT = IC // P
XW = DH + 1
XP = DH + 2
NQ = NT // 4
EPS = 1e-5
SHIFT = 40.0
DEN = 1024.0
SLOPE = 0.2
BIG = 3.0e38
PEAK = 64.0
X1S = 1024.0
PSCALE = 8.317766166719343


class Map:

    def __init__(self, nc, at):
        self.nc, self.at = nc, at

    def __call__(self, name, shape, dt, width):
        size = int(np.prod(shape[1:])) * width
        t = self.nc.alloc_sbuf_tensor_at(name, shape, dt, offset=self.at)
        self.at += (size + 31) // 32 * 32
        return t


def build(nc, x, adj, w0, wu, wv, b0, pw, pb, w1, b1, nw, ew, out):
    ctx = ExitStack()
    with ctx:
        def sem(name):
            return ctx.enter_context(nc.semaphore(name))

        y0_dram = nc.dram_tensor("y0_scratch", [N, D], FP32).ap()
        x1_dram = nc.dram_tensor("x1_scratch", [N, D], FP32).ap()
        e_dram = nc.dram_tensor("e_scratch", [N, N], FP32).ap()
        f2_dram = nc.dram_tensor("f2_scratch", [H * NT, P], FP32).ap()

        keep = Map(nc, (nc.sbuf_base + 31) // 32 * 32)
        k = Kept()
        k.ident = keep("ident", [P, P], FP32, 4)
        ident_bf_at = keep.at
        k.ident_bf = keep("ident_bf", [P, P], BF16, 2)
        k.f12 = keep("f12", [P, 2 * H, NT], FP32, 4)
        k.expo = keep("expo", [P, 4, H, NT], FP32, 4)
        k.qm = keep("qm", [P, 2, H, NT], FP32, 4)
        k.score = nc.alloc_sbuf_tensor_at("score", [P, NT], FP32, offset=ident_bf_at)
        k.small = keep("small", [P, 20], FP32, 4)
        k.at = keep.at
        k.bank = [ctx.enter_context(nc.psum_tensor(f"bank{i}", [P, 512], FP32)) for i in range(8)]

        project0(nc, sem, k, x, w0, wu, wv, b0, pw, pb, w1, ew, y0_dram)
        scale_support(nc, sem, k, adj, f2_dram)
        attend0(nc, sem, k, adj, y0_dram, f2_dram, x1_dram, w1, ew)
        project1(nc, sem, k, nw, x1_dram)
        attend1(nc, sem, k, adj, b1, x1_dram, e_dram, out)


class Kept:
    pass


def wait_apart(eng, done, value, passed):
    eng.wait_ge(done, value)
    eng.sem_inc(passed, 1)


def adjacency_block(ap):
    return ap.bitcast(BF16).rearrange("p (n half) -> p n half", half=2)[:, :, 1]


def key_tile(bank, i=None):
    if i is None:
        return bank[:, 0:IC // 2].bitcast(BF16)
    return bank[:, i * P // 2:(i + 1) * P // 2].bitcast(BF16)


def flat(ap):
    return ap.rearrange("p a n -> p (a n)")


X_BYTES = H * NT * 2 * 2 * XP * 2


def project0(nc, sem, k, x, w0, wu, wv, b0, pw, pb, w1, ew, y0_dram):
    k.sup = nc.alloc_sbuf_tensor_at("sup", [P, NT, D], FP32, offset=k.at + (X_BYTES + 31) // 32 * 32)
    m = Map(nc, k.at)
    w_sb = m("w_sb", [P, 2, KT * D], FP32, 4)
    w_parts = m("w_parts", [P, 2, 2, KT * D], F16, 2)
    u_bc = m("u_bc", [P, 2, D], FP32, 4)
    bias = m("bias", [P, 2, D], FP32, 4)
    x_in = m("x_in", [P, NT, D], FP32, 4)
    x_s = m("x_s", [P, 2, D], FP32, 4)
    xT = m("xT", [P, 2, 2, KT * P], F16, 2)
    prod = m("prod", [P, 2, 2 * H, DH], FP32, 4)
    y_sb = m("y_sb", [P, 4, D], FP32, 4)
    w_peak = m("w_peak", [P, 4], FP32, 4)
    w_scale = m("w_scale", [P, 4], FP32, 4)
    row_max = m("row_max", [P, NT], FP32, 4)
    scale = m("scale", [P, NT], FP32, 4)
    tmp = m("tmp", [P, 2, 4], FP32, 4)
    back = m("back", [P, 2, NT], FP32, 4)
    assert m.at <= k.at + X_BYTES, m.at
    ident, bank = k.ident, k.bank
    peak, gmax = k.small[:, 12:14], k.small[:, 14:16]
    k.s_e, k.s_w = k.small[:, 16:17], k.small[:, 17:18]
    k.inv_e2, k.inv_w = k.small[:, 18:19], k.small[:, 19:20]
    PASSES = ((0, 0), (0, 1), (1, 0))
    NG = NT // 4
    CHAIN, SC0 = 8, 1

    w_in, c_in, id_done, bias_done = sem("p0_w_in"), sem("p0_c_in"), sem("p0_id_done"), sem("p0_bias_done")
    l1_in, l1_peak, l1_max, steps = sem("p0_l1_in"), sem("p0_l1_peak"), sem("p0_l1_max"), sem("p0_steps")
    w_peaked, w_maxed, w_high, w_low = (sem("p0_" + n) for n in ("w_peaked", "w_maxed", "w_high", "w_low"))
    x_loaded = [sem(f"p0_x_loaded{i}") for i in range(2)]
    y_stored = [sem(f"p0_y_stored{i}") for i in range(4)]
    passed = sem("p0_passed")
    x_ready, peaked, scaled, xs_done, xb_done, xT_ps, xT_high, xT_low, mm_s, mm_y = (sem("p0_" + n) for n in (
        "x_ready", "peaked", "scaled", "xs_done", "xb_done", "xT_ps", "xT_high", "xT_low", "mm_s", "mm_y"))
    s_done, y_done, prod_done, f_done = (sem("p0_" + n) for n in ("s_done", "y_done", "prod_done", "f_done"))

    x_t = x.rearrange("(t p) d -> p t d", p=P)
    y_t = y0_dram.rearrange("(t p) d -> p t d", p=P)

    with nc.Block() as block:

        @block.sync
        def _(sp):
            def load_x(g):
                if g >= 2:
                    sp.wait_ge(x_loaded[g % 2], g // 2 * 16)
                    sp.sem_inc(x_ready, 1)
                sp.dma_start(x_in[:, g * 4:g * 4 + 4, :], x_t[:, g * 4:g * 4 + 4, :]).then_inc(x_loaded[g % 2], 16)

            sp.dma_start(w_sb[:, 0, :].rearrange("p (k d) -> p k d", k=KT),
                         w0.rearrange("(k p) d -> p k d", p=P)).then_inc(w_in, 16)
            sp.dma_start(w_sb[:, 1, :].rearrange("p (k d) -> p k d", k=KT),
                         pw.rearrange("(k p) d -> p k d", p=P)).then_inc(w_in, 16)
            load_x(0)
            sp.dma_start(u_bc[:, 0, :], wu.rearrange("h d o -> (h d o)").partition_broadcast(P)).then_inc(c_in, 16)
            sp.dma_start(u_bc[:, 1, :], wv.rearrange("h d o -> (h d o)").partition_broadcast(P)).then_inc(c_in, 16)
            sp.dma_start(bias[:, 0, :], b0.rearrange("a d -> (a d)").partition_broadcast(P)).then_inc(c_in, 16)
            sp.dma_start(bias[:, 1, :], pb.partition_broadcast(P)).then_inc(c_in, 16)
            for g in range(1, NG):
                load_x(g)
            for g in range(NG - 2, NG):
                sp.wait_ge(x_loaded[g % 2], NG // 2 * 16)
                sp.sem_inc(x_ready, 1)
            sp.wait_ge(w_low, 2)
            for i, w in enumerate((ew, w1)):
                sp.dma_start(w_sb[:, i, :].rearrange("p (k d) -> p k d", k=KT),
                             w.rearrange("(k p) d -> p k d", p=P)).then_inc(l1_in, 16)
            with sp.Fori(0, NG) as q:
                for u in range(4):
                    wait_apart(sp, y_done, q * 4 + u + 5, passed)
                    sp.dma_start(y_t[:, bass.ds(q * 4 + u, 1), :], y_sb[:, u:u + 1, :]).then_inc(y_stored[u], 16)
            for u in range(4):
                sp.wait_ge(y_stored[u], NG * 16)

        @block.gpsimd
        def _(pool):
            nc.gpsimd.memset(ident[:], 0.0).then_inc(id_done, 1)
            pool.wait_ge(id_done, 1)
            nc.gpsimd.affine_select(out=ident[:], in_=ident[:], compare_op=ALU.not_equal, fill=1.0, base=0,
                                    pattern=[[-1, P]], channel_multiplier=1).then_inc(id_done, 1)
            pool.wait_ge(w_peaked, 2)
            nc.gpsimd.partition_all_reduce(w_peak[:, 2:4], w_peak[:, 0:2], P, RMAX).then_inc(w_maxed, 1)
            pool.wait_ge(c_in, 64)
            nc.gpsimd.tensor_tensor(out=bias[:, 0, :], in0=bias[:, 0, :], in1=bias[:, 1, :],
                                    op=ALU.add).then_inc(bias_done, 1)
            pool.wait_ge(bias_done, 1)
            with pool.Fori(0, NG) as q:
                for u in range(4):
                    pool.wait_ge(xs_done, q * 4 + u + 1)
                    xt = flat(x_in[:, bass.ds(q * 4 + u, 1), :])
                    nc.gpsimd.tensor_tensor(out=xt, in0=xt, in1=bias[:, 0, :], op=ALU.add).then_inc(xb_done, 1)
            pool.wait_ge(l1_peak, 2)
            nc.gpsimd.partition_all_reduce(gmax, peak, P, RMAX).then_inc(l1_max, 1)

        def transpose_tile(pe, q, u):
            pe.wait_ge(xs_done, q * 4 + u + 1)
            pe.wait_ge(xT_low, q * 4 + u + 1)
            for j in range(KT):
                last = nc.tensor.transpose(bank[u % 2][:, j * P:(j + 1) * P], x_s[:, u % 2, j * P:(j + 1) * P],
                                           ident[:])
            last.then_inc(xT_ps, 1)

        def project_tile(pe, q, u):
            pe.wait_ge(xT_low, q * 4 + u + 3)
            for out_bank, i, free, credit, done in ((2, 0, s_done, 1, mm_s), (4, 1, y_done, 3, mm_y)):
                pe.wait_ge(free, q * 4 + u + credit)
                n = 0
                for a, b in PASSES:
                    for j in range(KT):
                        last = nc.tensor.matmul(bank[out_bank + u % 2][:], xT[:, u % 2, a, j * P:(j + 1) * P],
                                                w_parts[:, i, b, j * D:(j + 1) * D], start=(n == 0), stop=(n == 11))
                        n += 1
                last.then_inc(done, 1)

        @block.tensor
        def _(pe):
            pe.sem_inc(xT_ps, 2)
            pe.wait_ge(id_done, 2)
            transpose_tile(pe, 0, 0)
            pe.wait_ge(w_low, 2)
            with pe.Fori(0, NG - 1) as q:
                for u in range(4):
                    transpose_tile(pe, q + (u + 1) // 4, (u + 1) % 4)
                    project_tile(pe, q, u)
            for u in range(4):
                if u < 3:
                    transpose_tile(pe, NG - 1, u + 1)
                project_tile(pe, NG - 1, u)

        @block.scalar
        def _(act):
            act.sem_inc(s_done, 2)
            act.sem_inc(mm_y, 2)

            def scale_x(q, u):
                t = q * 4 + u
                act.wait_ge(scaled, q * CHAIN + CHAIN + SC0)
                act.wait_ge(xT_ps, t + 1)
                nc.scalar.activation(x_s[:, u % 2, :], flat(x_in[:, bass.ds(t, 1), :]), ACT.Copy,
                                     scale=scale[:, bass.ds(t, 1)]).then_inc(xs_done, 1)

            def high_x(q, u):
                act.wait_ge(xT_ps, q * 4 + u + 3)
                act.wait_ge(mm_y, q * 4 + u + 1)
                nc.scalar.activation(xT[:, u % 2, 0, :], bank[u % 2][:], ACT.Copy).then_inc(xT_high, 1)

            def copy_s(q, u):
                act.wait_ge(mm_s, q * 4 + u + 1)
                nc.scalar.activation(flat(k.sup[:, bass.ds(q * 4 + u, 1), :]), bank[2 + u % 2][:],
                                     ACT.Copy, scale=back[:, 0, bass.ds(q * 4 + u, 1)]).then_inc(s_done, 1)

            def tile(q, u, left):
                if left > 1:
                    high_x(q + (u + 1) // 4, (u + 1) % 4)
                if left > 2:
                    scale_x(q + (u + 2) // 4, (u + 2) % 4)
                copy_s(q, u)

            act.wait_ge(w_maxed, 2)
            for i in range(2):
                nc.scalar.activation(w_parts[:, i, 0, :], w_sb[:, i, :], ACT.Copy, scale=w_scale[:, i:i + 1]
                                     ).then_inc(w_high, 1)
            scale_x(0, 0)
            scale_x(0, 1)
            high_x(0, 0)
            with act.Fori(0, NG - 1) as q:
                for u in range(4):
                    tile(q, u, NT)
            for u in range(4):
                tile(NG - 1, u, 4 - u)

        @block.vector
        def _(dve):
            dve.sem_inc(y_done, 4)
            dve.sem_inc(xT_low, 2)
            dve.sem_inc(scaled, SC0)
            link = linker(nc, dve, steps)

            def peaks(q, half):
                dve.wait_ge(x_ready, q + 1)
                nc.vector.tensor_reduce(out=row_max[:, bass.ds(q * 4 + 2 * half, 2)],
                                        in_=x_in[:, bass.ds(q * 4 + 2 * half, 2), :], axis=AX.X, op=ALU.max,
                                        apply_absolute_value=True).then_inc(peaked, 1)

            def scales(q):
                g = bass.ds(q * 4, 4)
                sc, inv = tmp[:, 0, :], tmp[:, 1, :]
                dve.wait_ge(peaked, q * 2 + 2)
                dve.wait_ge(scaled, q * CHAIN + SC0)
                nc.vector.tensor_scalar(sc, row_max[:, g], 1e-30, None, ALU.max).then_inc(scaled, 1)
                dve.wait_ge(scaled, q * CHAIN + 1 + SC0)
                nc.vector.reciprocal(sc, sc).then_inc(scaled, 1)
                dve.wait_ge(scaled, q * CHAIN + 2 + SC0)
                nc.vector.tensor_scalar(sc, sc, PEAK, None, ALU.mult).then_inc(scaled, 1)
                dve.wait_ge(scaled, q * CHAIN + 3 + SC0)
                nc.vector.tensor_scalar(sc.bitcast(U32), sc.bitcast(U32), 0x7F800000, None, ALU.bitwise_and
                                        ).then_inc(scaled, 1)
                dve.wait_ge(scaled, q * CHAIN + 4 + SC0)
                nc.vector.reciprocal(inv, sc).then_inc(scaled, 1)
                nc.vector.tensor_scalar(scale[:, g], sc, 1.0, None, ALU.mult).then_inc(scaled, 1)
                dve.wait_ge(scaled, q * CHAIN + 6 + SC0)
                for i in range(2):
                    nc.vector.tensor_scalar(back[:, i, g], inv, w_scale[:, 2 + i:3 + i], None, ALU.mult
                                            ).then_inc(scaled, 1)

            def low_x(q, u):
                dve.wait_ge(xT_high, q * 4 + u + 1)
                nc.vector.tensor_tensor(out=xT[:, u % 2, 1, :], in0=bank[u % 2][:], in1=xT[:, u % 2, 0, :],
                                        op=ALU.subtract).then_inc(xT_low, 1)

            def tile(q, u, first=False, last_group=False):
                t = q * 4 + u
                if not (last_group and u == 3):
                    low_x(q + (u + 1) // 4, (u + 1) % 4)
                if u < 2 and not last_group:
                    peaks(q + 1, u)
                dve.wait_ge(s_done, t + 3)
                st = flat(k.sup[:, bass.ds(t, 1), :])
                for i in range(2):
                    last = nc.vector.tensor_tensor(
                        out=prod[:, u % 2, i * H:(i + 1) * H, :].rearrange("p h d -> p (h d)"), in0=st,
                        in1=u_bc[:, i, :], op=ALU.mult)
                last.then_inc(prod_done, 1)
                if u == 1 and not last_group:
                    scales(q + 1)
                dve.wait_ge(prod_done, t + 1)
                nc.vector.tensor_reduce(out=k.f12[:, :, bass.ds(t, 1)], in_=prod[:, u % 2, :, :], axis=AX.X,
                                        op=ALU.add).then_inc(f_done, 1)
                dve.wait_ge(mm_y, t + 3)
                dve.wait_ge(xb_done, t + 1)
                if not first:
                    dve.wait_ge(y_stored[u], q * 16)
                nc.vector.scalar_tensor_tensor(out=y_sb[:, u, :], in0=bank[4 + u % 2][:],
                                               scalar=back[:, 1, bass.ds(t, 1)], in1=flat(x_in[:, bass.ds(t, 1), :]),
                                               op0=ALU.mult, op1=ALU.add).then_inc(y_done, 1)

            dve.wait_ge(w_in, 32)
            for i in range(2):
                nc.vector.tensor_reduce(out=w_peak[:, i:i + 1], in_=w_sb[:, i, :], axis=AX.X, op=ALU.max,
                                        apply_absolute_value=True).then_inc(w_peaked, 1)
            peaks(0, 0)
            peaks(0, 1)
            dve.wait_ge(w_maxed, 1)
            power_of_two(link, w_scale[:, 0:2], w_peak[:, 2:4], PEAK)
            link(lambda v: v.reciprocal(w_scale[:, 2:4], w_scale[:, 0:2]))
            dve.sem_inc(w_maxed, 1)
            scales(0)
            for i in range(2):
                dve.wait_ge(w_high, i + 1)
                nc.vector.scalar_tensor_tensor(out=w_parts[:, i, 1, :], in0=w_sb[:, i, :], scalar=w_scale[:, i:i + 1],
                                               in1=w_parts[:, i, 0, :], op0=ALU.mult, op1=ALU.subtract
                                               ).then_inc(w_low, 1)
            low_x(0, 0)
            dve.wait_ge(c_in, 64)
            for u in range(4):
                tile(0, u, first=True)
            with dve.Fori(1, NG - 2) as q:
                for u in range(4):
                    tile(q, u)
            for u in range(4):
                tile(NG - 2, u)
                if u % 2:
                    dve.wait_ge(l1_in, 32)
                    nc.vector.tensor_reduce(out=peak[:, u // 2:u // 2 + 1], in_=w_sb[:, u // 2, :], axis=AX.X,
                                            op=ALU.max, apply_absolute_value=True).then_inc(l1_peak, 1)
            for u in range(4):
                tile(NG - 1, u, last_group=True)
            link(lambda v: v.tensor_reduce(out=k.small[:, 4:5], in_=row_max[:], axis=AX.X, op=ALU.max))
            link(lambda v: v.tensor_scalar(k.small[:, 4:5], k.small[:, 4:5], w_peak[:, 2:3], float(D),
                                           ALU.mult, ALU.mult))
            dve.wait_ge(l1_max, 1)
            power_of_two(link, k.small[:, 16:18], gmax, PEAK)
            link(lambda v: v.reciprocal(k.small[:, 18:20], k.small[:, 16:18]))
            link(lambda v: v.tensor_scalar(k.inv_e2, k.inv_e2, k.inv_e2, None, ALU.mult))
            dve.wait_ge(f_done, NT)


def power_of_two(link, out, peak, room):
    link(lambda v: v.tensor_scalar(out, peak, 1e-30, None, ALU.max))
    link(lambda v: v.reciprocal(out, out))
    link(lambda v: v.tensor_scalar(out, out, room, None, ALU.mult))
    link(lambda v: v.tensor_scalar(out.bitcast(U32), out.bitcast(U32), 0x7F800000, None, ALU.bitwise_and))


def linker(nc, dve, done):
    count = [0]

    def link(step):
        step(nc.vector).then_inc(done, 1)
        count[0] += 1
        dve.wait_ge(done, count[0])
    return link


def scale_support(nc, sem, k, adj, f2_dram):
    k.xs = nc.alloc_sbuf_tensor_at("xs", [P, H, NT, 2, 2, XP], F16, offset=k.at)
    over = Map(nc, k.at + (X_BYTES + 31) // 32 * 32)
    k.stage = over("stage", [P, 2, IT, 2 * P], FP32, 4)
    k.aT = over("aT", [P, NT, IC], BF16, 2)
    k.attend_at = over.at
    STAGE_TILES, BEHIND = 4, 6
    m = Map(nc, k.at + (X_BYTES + 31) // 32 * 32 + NT * D * 4)
    t1 = m("t1", [P, 2, 2, D], FP32, 4)
    arg = m("arg", [P, 2, H, NT], FP32, 4)
    f2r = k.expo[:, 3].rearrange("p h t -> p (h t)")
    qb = k.expo[:, 2].rearrange("p h t -> p (h t)").bitcast(BF16).rearrange("p (a h t) -> p a h t", a=2, h=H)
    small, bank, ident, f12 = k.small, k.bank, k.ident, k.f12
    peak, gmax, scale, ratio = small[:, 0:5], small[:, 5:10], small[:, 10:11], small[:, 11:12]

    steps, g_out, e_done, f2_ps, f2_sb, f2_out = (sem("p1_" + n) for n in
                                                  ("steps", "g_out", "e_done", "f2_ps", "f2_sb", "f2_out"))
    aT_ps, aT_done = sem("p1_aT_ps"), sem("p1_aT_done")
    stage_in = [sem(f"p1_stage_in{i}") for i in range(2)]
    passed = sem("p1_passed")
    adj_r = adj.rearrange("(c i p) n -> p c i n", i=IT, p=P)
    local_done, arg_done, cs_done, t1_dve, t1_pool, hi_done, lo_done = (sem("p1_" + n) for n in (
        "local_done", "arg_done", "cs_done", "t1_dve", "t1_pool", "hi_done", "lo_done"))

    def fac(mm, t):
        return arg[:, mm, :, bass.ds(t, 1)].broadcast_to([P, H, DH])

    def half(t, mm, part):
        return k.xs[:, :, bass.ds(t, 1), mm, part, 0:DH].rearrange("p h a d -> p (h a) d")

    def sup(t):
        return flat(k.sup[:, bass.ds(t, 1), :]).rearrange("p (h d) -> p h d", h=H)

    with nc.Block() as block:

        @block.tensor
        def _(pe):
            nc.tensor.transpose(bank[0][:, 0:P], f12[:, H:2 * H, :].rearrange("p h t -> p (h t)"),
                                ident[:]).then_inc(f2_ps, 1)
            pe.sem_inc(aT_ps, 3)
            pe.wait_ge(f2_sb, 1)
            with pe.Fori(0, NT // 4) as q:
                for u in range(2):
                    pe.wait_ge(stage_in[u], q * 16 + 16)
                    for j in range(2):
                        pe.wait_ge(aT_done, q * 4 + 2 * u + j + 1)
                        for i in range(IT):
                            last = nc.tensor.transpose(key_tile(bank[6 + j], i),
                                                       adjacency_block(k.stage[:, u, i, j * P:(j + 1) * P]),
                                                       k.ident_bf[:])
                        last.then_inc(aT_ps, 1)

        @block.sync
        def _(sp):
            sp.wait_ge(f2_sb, 1)
            sp.dma_start(f2_dram, f2r).then_inc(f2_out, 16)
            sp.wait_ge(f2_out, 16)
            sp.wait_ge(t1_dve, STAGE_TILES)
            sp.wait_ge(t1_pool, STAGE_TILES)
            with sp.Fori(0, NT // 4) as q:
                for u in range(2):
                    wait_apart(sp, aT_ps, (q * 2 + u) * 2 + 1, passed)
                    sp.dma_start(k.stage[:, u, :, :], adj_r[:, 0, :, bass.ds(q * 512 + u * 256, 256)]
                                 ).then_inc(stage_in[u], 16)

        @block.gpsimd
        def _(pool):
            pool.wait_ge(local_done, 1)
            nc.gpsimd.partition_all_reduce(gmax, peak, P, RMAX).then_inc(g_out, 1)
            pool.wait_ge(cs_done, 1)
            with pool.Fori(0, NT // 2) as i:
                for u in range(2):
                    pool.wait_ge(lo_done, i * 4 + 2 * u + 2)
                    nc.gpsimd.tensor_tensor(out=t1[:, u, 1, :].rearrange("p (h d) -> p h d", h=H),
                                            in0=sup(i * 2 + u), in1=fac(1, i * 2 + u), op=ALU.mult
                                            ).then_inc(t1_pool, 1)

        @block.scalar
        def _(act):
            nc.scalar.activation(k.ident_bf[:], ident[:], ACT.Copy)
            act.wait_ge(f2_ps, 1)
            nc.scalar.activation(f2r, bank[0][:, 0:P], ACT.Copy).then_inc(f2_sb, 1)
            act.wait_ge(arg_done, 1)
            nc.scalar.activation(k.expo[:, 0:2].rearrange("p a h t -> p (a h t)"),
                                 arg[:].rearrange("p a h t -> p (a h t)"), ACT.Exp).then_inc(e_done, 1)
            act.wait_ge(arg_done, 2)
            act.wait_ge(f2_out, 16)
            nc.scalar.activation(k.expo[:, 2:4].rearrange("p a h t -> p (a h t)"),
                                 arg[:].rearrange("p a h t -> p (a h t)"), ACT.Exp).then_inc(e_done, 1)
            act.sem_inc(aT_done, 2)

            def high(t, u):
                for mm, ready in ((0, t1_dve), (1, t1_pool)):
                    act.wait_ge(ready, t + 1)
                    nc.scalar.activation(half(t, mm, 0), t1[:, u, mm, :].rearrange("p (h d) -> p h d", h=H),
                                         ACT.Copy).then_inc(hi_done, 1)

            def copy(j, u):
                act.wait_ge(aT_ps, j + 4)
                nc.scalar.activation(flat(k.aT[:, bass.ds(j, 1), :]), key_tile(bank[6 + u]), ACT.Copy).then_inc(aT_done, 1)

            for t in range(BEHIND):
                high(t, t % 2)
            with act.Fori(BEHIND // 2, NT // 2) as i:
                for u in range(2):
                    high(i * 2 + u, u)
                    copy(i * 2 + (u - BEHIND), u)
            for j in range(NT - BEHIND, NT):
                copy(j, j % 2)

        @block.vector
        def _(dve):
            link = linker(nc, dve, steps)
            link(lambda v: v.tensor_reduce(out=peak[:, 0:4], in_=f12[:, 0:H, :], axis=AX.X, op=ALU.max))
            dve.sem_inc(local_done, 1)
            dve.sem_inc(lo_done, 4)
            dve.wait_ge(g_out, 1)
            for h in range(H):
                c = gmax[:, h:h + 1]
                nc.vector.tensor_scalar(arg[:, 0, h, :], f12[:, h, :], c, SHIFT, ALU.subtract, ALU.add)
                link(lambda v: v.tensor_scalar(arg[:, 1, h, :], f12[:, h, :], c, SLOPE, ALU.subtract, ALU.mult))
            link(lambda v: v.tensor_scalar(arg[:, 1], arg[:, 1], SHIFT, None, ALU.add))
            dve.sem_inc(arg_done, 1)
            power_of_two(link, scale, gmax[:, 4:5], 16384.0)
            link(lambda v: v.tensor_scalar(ratio, scale, 1.0 / DEN, None, ALU.mult))
            dve.wait_ge(e_done, 1)
            key = k.expo[:, 0:2]
            link(lambda v: v.tensor_copy(qb, key))
            link(lambda v: v.tensor_copy(k.qm[:], qb))
            link(lambda v: v.tensor_scalar(arg[:], k.qm[:], 1e-37, None, ALU.max))
            link(lambda v: v.reciprocal(arg[:], arg[:]))
            link(lambda v: v.tensor_tensor(out=key, in0=key, in1=arg[:], op=ALU.mult))
            link(lambda v: v.tensor_scalar(k.qm[:, 1], k.qm[:, 1], -1.0, None, ALU.mult))
            for h in range(H):
                link(lambda v: v.tensor_scalar(arg[:, 0, h, :], f12[:, H + h, :], gmax[:, h:h + 1], 1.0 - SLOPE,
                                               ALU.add, ALU.mult))
            link(lambda v: v.tensor_scalar(arg[:, 1], arg[:, 0], -1.0, 0.0, ALU.mult, ALU.min))
            link(lambda v: v.tensor_scalar(arg[:, 0], arg[:, 0], 0.0, None, ALU.min))
            dve.sem_inc(arg_done, 1)
            dve.wait_ge(e_done, 2)
            link(lambda v: v.tensor_scalar(arg[:], key, DEN, None, ALU.mult))
            for mm in range(2):
                link(lambda v: v.tensor_copy(k.xs[:, :, :, mm, 0, DH], arg[:, mm]))
                link(lambda v: v.tensor_tensor(out=k.xs[:, :, :, mm, 1, DH], in0=arg[:, mm],
                                               in1=k.xs[:, :, :, mm, 0, DH], op=ALU.subtract))
            link(lambda v: v.tensor_scalar(arg[:], key, scale, None, ALU.mult))
            dve.sem_inc(cs_done, 1)

            def scaled(t, u):
                dve.wait_ge(lo_done, t * 2 + 1)
                nc.vector.tensor_tensor(out=t1[:, u, 0, :].rearrange("p (h d) -> p h d", h=H), in0=sup(t),
                                        in1=fac(0, t), op=ALU.mult).then_inc(t1_dve, 1)

            def low(t, u):
                for mm in range(2):
                    dve.wait_ge(hi_done, t * 2 + mm + 1)
                    nc.vector.tensor_tensor(out=half(t, mm, 1), in0=t1[:, u, mm, :].rearrange("p (h d) -> p h d", h=H),
                                            in1=half(t, mm, 0), op=ALU.subtract).then_inc(lo_done, 1)

            scaled(0, 0)
            with dve.Fori(0, NT // 2 - 1) as i:
                for u in range(2):
                    scaled(i * 2 + u + 1, (u + 1) % 2)
                    low(i * 2 + u, u)
            scaled(NT - 1, 1)
            low(NT - 2, 0)
            low(NT - 1, 1)


def attend0(nc, sem, k, adj, y0_dram, f2_dram, x1_dram, w1, ew):
    head_bytes = X_BYTES // H
    ahead = Map(nc, k.at)
    w_sb = ahead("w1_sb", [P, 2, KT * D], FP32, 4)
    k.w_parts = ahead("w1_parts", [P, 2, 2, KT * D], F16, 2)
    assert ahead.at <= k.at + head_bytes, ahead.at
    ahead.at = k.at + head_bytes
    k.x1_in = ahead("x1_in", [P, 2, IT, D], FP32, 4)
    assert ahead.at <= k.at + 2 * head_bytes, ahead.at
    k.project_at = ahead.at
    m = Map(nc, k.attend_at)
    stage, aT = k.stage, k.aT
    f2b = m("f2b", [P, 2, IC], FP32, 4)
    sign = m("sign", [P, 2, 2, IC], BF16, 2)
    signed = m("signed", [P, 2, 2, IC], BF16, 2)
    mask = m("mask", [P, 4, 2, IC], BF16, 2)
    y = m("y", [P, IT, D], FP32, 4)
    part = m("part", [P, IT, XW], FP32, 4)
    part2 = m("part2", [P, IT, XW], FP32, 4)
    dinv = m("dinv", [P, IT], FP32, 4)
    stats = m("stats", [P, IT, 6], FP32, 4)
    mv = m("mv", [P, IT, 2], FP32, 4)
    rstd = m("rstd", [P, IT], FP32, 4)
    assert m.at <= nc.sbuf_usable_end, m.at
    bank, xs = k.bank, k.xs
    acc = [bank[0:3], bank[3:6]]
    ratio = k.small[:, 11:12]
    NP = NT // 2

    def slot(s, i):
        return acc[s][i // 3][:, i % 3 * XW:i % 3 * XW + XW]

    names = ("sign_done", "edge_done", "mask_done", "mask_free", "part_done", "y_added", "aT_ps", "aT_done",
             "aT_last", "y_loaded", "y_final", "y_stored", "sum_done", "den_done", "stat_done", "mv_done",
             "std_done", "inv_done", "pool_step")
    s = {n: sem("a0_" + n) for n in names}
    passed = [sem(f"a0_passed{i}") for i in range(2)]
    stage_in = [sem(f"a0_stage_in{i}") for i in range(2)]
    f2_in = [sem(f"a0_f2_in{h}") for h in range(2)]
    w_in = [sem(f"a0_w_in{i}") for i in range(2)]
    w_high, w_low, x1_loaded = sem("a0_w_high"), sem("a0_w_low"), sem("a0_x1_loaded")
    SIGN0, EDGE0, MASK0, FREE0, APS0, AT0, PART0, Y0 = 17, 2, 3, 4, 3, 1, 4, 1

    adj_r = adj.rearrange("(c i p) n -> p c i n", i=IT, p=P)
    y0_r = y0_dram.rearrange("(c i p) d -> p c i d", i=IT, p=P)
    x1_r = x1_dram.rearrange("(c i p) d -> p c i d", i=IT, p=P)
    f2_r = f2_dram.rearrange("(h c i) p -> h c (i p)", h=H, i=IT)

    with nc.Block() as block:

        @block.sync
        def _(sp):
            def load_quad(c, q):
                for u in range(2):
                    wait_apart(sp, s["aT_ps"], (c * NP + q * 2 + u) * 2 - 2 + APS0, passed[0])
                    sp.dma_start(stage[:, u, :, :],
                                 adj_r[:, bass.ds(c, 1), :, bass.ds(q * 512 + u * 256, 256)].rearrange(
                                     "p c i n -> p (c i) n")).then_inc(stage_in[u], 16)

            def load_adj(c):
                with sp.Fori(1, NQ) as q:
                    load_quad(c, q)

            def load_f2(c, h):
                wait_apart(sp, s["sign_done"], (c * H + h - 1) * NP + SIGN0, passed[0])
                sp.dma_start(f2b[:, h % 2, :],
                             f2_r[h, bass.ds(c, 1), :].rearrange("a n -> (a n)").partition_broadcast(P)
                             ).then_inc(f2_in[h % 2], 16)

            def store_y(c):
                wait_apart(sp, s["y_final"], c + 1, passed[0])
                sp.dma_start(x1_r[:, bass.ds(c, 1), :, :].rearrange("p c i d -> p (c i) d"), y[:]
                             ).then_inc(s["y_stored"], 16)
                wait_apart(sp, s["y_stored"], c * 16 + 16, passed[0])

            def load_y(c):
                sp.dma_start(y[:], y0_r[:, bass.ds(c, 1), :, :].rearrange("p c i d -> p (c i) d")
                             ).then_inc(s["y_loaded"], 16)

            load_f2(0, 0)
            load_f2(0, 1)
            load_y(0)

            def chunk(c):
                load_f2(c, 2)
                load_f2(c, 3)
                load_quad(c + 1, 0)
                load_f2(c + 1, 0)
                load_adj(c + 1)
                load_f2(c + 1, 1)

            chunk(0)
            with sp.Fori(1, NIC - 1) as c:
                store_y(c - 1)
                load_y(c)
                chunk(c)
            store_y(NIC - 2)
            load_y(NIC - 1)
            load_f2(NIC - 1, 2)
            load_f2(NIC - 1, 3)
            sp.wait_ge(s["mask_free"], ((NIC - 1) * H + 1) * NT + FREE0)
            for i, w in enumerate((ew, w1)):
                sp.dma_start(w_sb[:, i, :].rearrange("p (k d) -> p k d", k=KT),
                             w.rearrange("(k p) d -> p k d", p=P)).then_inc(w_in[i], 16)
            sp.wait_ge(s["mask_free"], ((NIC - 1) * H + 2) * NT + FREE0)
            for c in range(2):
                sp.dma_start(k.x1_in[:, c, :, :], x1_r[:, c, :, :]).then_inc(x1_loaded, 16)
            store_y(NIC - 1)
            sp.wait_ge(x1_loaded, 32)

        def transpose_pair(pe, c, q, u):
            pe.wait_ge(stage_in[u], ((c - 1) * (NP // 2) + q) * 16 + 16)
            quad = c * NQ + q
            for j in range(2):
                if (u, j) == (0, 1):
                    pe.wait_ge(s["aT_last"], quad + AT0)
                else:
                    pe.wait_ge(s["aT_done"], quad * 3 + u + (u and j) + AT0)
                for i in range(IT):
                    last = nc.tensor.transpose(key_tile(bank[6 + j], i),
                                               adjacency_block(stage[:, u, i, j * P:(j + 1) * P]), k.ident_bf[:])
                last.then_inc(s["aT_ps"], 1)

        @block.tensor
        def _(pe):
            pe.sem_inc(s["aT_ps"], APS0 + NT)

            def products(c, h, q, first=False, last_quad=False, tr=None):
                hh = c * H + h
                for t4 in range(4):
                    if tr is not None and t4 % 2 == 0:
                        transpose_pair(pe, tr, q, t4 // 2)
                    pe.wait_ge(s["mask_done"], hh * NT + q * 4 + t4 + 1 + MASK0)
                    for i in range(2 * IT):
                        br, it = i // IT, i % IT
                        for pt in range(2):
                            begin = first and t4 == 0 and pt == 0 and i % 3 == 0
                            end = last_quad and t4 == 3 and pt == 1
                            op = nc.tensor.matmul(slot(h % 2, i), mask[:, t4, br, it * P:(it + 1) * P],
                                                  xs[:, h, bass.ds(q * 4 + t4, 1), br, pt, 0:XW].rearrange(
                                                      "p a n -> p (a n)"),
                                                  start=begin, stop=end, skip_group_check=True)
                    op.then_inc(s["mask_free"], 1)

            def chunk(c, tr):
                for h in range(H):
                    pe.wait_ge(s["part_done"], (c * H + h) * 2 - 2 + PART0)
                    t = tr if h == H - 1 else None
                    products(c, h, 0, first=True, tr=t)
                    with pe.Fori(1, NQ - 1) as q:
                        products(c, h, q, tr=t)
                    products(c, h, NQ - 1, last_quad=True, tr=t)

            chunk(0, 1)
            with pe.Fori(1, NIC - 1) as c:
                chunk(c, c + 1)
            chunk(NIC - 1, None)

        @block.scalar
        def _(act):
            act.sem_inc(s["sign_done"], SIGN0)
            act.sem_inc(s["aT_done"], AT0 + 3 * NQ)
            act.sem_inc(s["part_done"], PART0)

            def copy(c, q, u):
                for t4 in ((0, 1), (2,))[u]:
                    act.wait_ge(s["aT_ps"], c * NT + q * 4 + t4 + 1 + APS0)
                    nc.scalar.activation(flat(aT[:, bass.ds(q * 4 + t4, 1), :]), key_tile(bank[6 + t4 % 2]),
                                         ACT.Copy).then_inc(s["aT_done"], 1)

            def signs(c, h, q, tr=None, tr_q=None):
                for u in range(2):
                    act.wait_ge(s["edge_done"], (c * H + h) * NP + q * 2 + u - 1 + EDGE0)
                    for j in range(2):
                        last = nc.scalar.activation(sign[:, u, j, :], f2b[:, h % 2, :], ACT.Sign,
                                                    bias=k.f12[:, h, bass.ds(q * 4 + 2 * u + j, 1)])
                    last.then_inc(s["sign_done"], 1)
                    if tr is not None:
                        copy(tr, tr_q, u)

            def read_out(c, h, br):
                hh = c * H + h
                if br == 0:
                    act.wait_ge(s["mask_free"], hh * NT + NT + FREE0)
                    act.wait_ge(s["y_added"], hh + Y0)
                for i in range(IT):
                    last = nc.scalar.activation((part, part2)[br][:, i, :], slot(h % 2, br * IT + i), ACT.Copy,
                                                scale=k.expo[:, 2 + br, h, bass.ds(c * IT + i, 1)])
                last.then_inc(s["part_done"], 1)

            def deviation(c):
                act.wait_ge(s["mv_done"], c * 2 + 2)
                nc.scalar.activation(rstd[:], mv[:, :, 1], ACT.Sqrt).then_inc(s["std_done"], 1)

            def normalize(c):
                act.wait_ge(s["inv_done"], c * 2 + 2)
                for i in range(IT):
                    last = nc.scalar.activation(y[:, i, :], y[:, i, :], ACT.Identity, bias=mv[:, i, 0:1],
                                                scale=rstd[:, i:i + 1])
                last.then_inc(s["y_final"], 1)

            def chunk(c, tr, prev):
                for h in range(H):
                    t = tr if h == H - 1 else None
                    pc, ph = (c, h - 1) if h else (prev, H - 1)
                    act.wait_ge(f2_in[h % 2], (c * 2 + h // 2) * 16 + 16)
                    if h == 0 and prev is not None:
                        signs(c, h, 0, c, NQ - 1)
                    else:
                        signs(c, h, 0)
                    for q in (1, 2):
                        signs(c, h, q, t, q - 1)
                        if pc is not None:
                            read_out(pc, ph, q - 1)
                    if h == 1 and prev is not None:
                        normalize(prev)
                    with act.Fori(3, NQ) as q:
                        signs(c, h, q, t, q - 1)
                    if h == 0 and prev is not None:
                        deviation(prev)

            chunk(0, 1, None)
            with act.Fori(1, NIC - 1) as c:
                chunk(c, c + 1, c - 1)
            chunk(NIC - 1, None, NIC - 2)
            read_out(NIC - 1, H - 1, 0)
            read_out(NIC - 1, H - 1, 1)
            for i, scale in enumerate((k.s_e, k.s_w)):
                act.wait_ge(w_in[i], 16)
                nc.scalar.activation(k.w_parts[:, i, 0, :], w_sb[:, i, :], ACT.Copy, scale=scale
                                     ).then_inc(w_high, 1)
            deviation(NIC - 1)
            normalize(NIC - 1)

        @block.vector
        def _(dve):
            dve.sem_inc(s["edge_done"], EDGE0)
            dve.sem_inc(s["aT_last"], AT0 + NQ)
            dve.sem_inc(s["mask_done"], MASK0)
            dve.sem_inc(s["mask_free"], FREE0)

            def edges(c, h, q, u):
                pair = (c * H + h) * NP + q * 2 + u
                if h == 0:
                    dve.wait_ge(s["aT_done"], (c * NQ + q) * 3 + 2 + u + AT0)
                    if u:
                        dve.wait_ge(s["aT_last"], c * NQ + q + 1 + AT0)
                dve.wait_ge(s["mask_done"], pair * 2 - 2 + MASK0)
                dve.wait_ge(s["sign_done"], pair + 1 + SIGN0)
                nc.vector.tensor_tensor(out=signed[:, u, :, :].rearrange("p j n -> p (j n)"),
                                        in0=sign[:, u, :, :].rearrange("p j n -> p (j n)"),
                                        in1=aT[:, bass.ds(q * 4 + 2 * u, 2), :].rearrange("p j n -> p (j n)"),
                                        op=ALU.mult).then_inc(s["edge_done"], 1)

            def branches(c, h, q, u, j):
                t4 = 2 * u + j
                dve.wait_ge(s["mask_free"], (c * H + h) * NT + q * 4 + t4 - 3 + FREE0)
                for br, op in ((0, ALU.max), (1, ALU.min)):
                    last = nc.vector.tensor_scalar(mask[:, t4, br, :], signed[:, u, j, :], 0.0,
                                                   k.qm[:, br, h, bass.ds(q * 4 + t4, 1)], op, ALU.mult)
                last.then_inc(s["mask_done"], 1)

            def copy_last(c, q):
                dve.wait_ge(s["edge_done"], edges_before(c, q))
                dve.wait_ge(s["aT_ps"], c * NT + q * 4 + 4 + APS0)
                nc.vector.tensor_copy(flat(aT[:, bass.ds(q * 4 + 3, 1), :]), key_tile(bank[7])).then_inc(s["aT_last"], 1)

            def edges_before(c, q):
                return ((c - 1) * H + H - 1) * NP + q * 2 + 2 + EDGE0

            def masks(c, h, q, following, tr=None, tr_q=None):
                for u in range(2):
                    dve.wait_ge(s["edge_done"], (c * H + h) * NP + q * 2 + u + 1 + EDGE0)
                    branches(c, h, q, u, 0)
                    if u == 0:
                        edges(c, h, q, 1)
                    elif following is not None:
                        edges(*following, 0)
                    branches(c, h, q, u, 1)
                    if u == 0 and tr is not None:
                        copy_last(tr, tr_q)

            def denominator(c, h):
                hh = c * H + h
                dve.wait_ge(s["sum_done"], hh + 1)
                dve.wait_ge(s["y_added"], hh + Y0)
                nc.vector.tensor_scalar(dinv[:], part[:, :, DH], 1e-30, ratio, ALU.max, ALU.mult
                                        ).then_inc(s["den_done"], 1)

            def inverse(c, h):
                dve.wait_ge(s["den_done"], (c * H + h) * 2 + 1)
                nc.vector.reciprocal(dinv[:], dinv[:]).then_inc(s["den_done"], 1)

            def moments(c, rows):
                dve.wait_ge(s["y_added"], c * H + H + Y0)
                for i in rows:
                    nc.vector.bn_stats(stats[:, i, :], y[:, i, :]).then_inc(s["stat_done"], 1)

            def variance(c):
                wait_apart(dve, s["stat_done"], c * IT + IT, passed[1])
                for i in range(IT):
                    last = nc.vector.bn_aggr(mv[:, i, :], stats[:, i, :])
                last.then_inc(s["mv_done"], 1)
                dve.wait_ge(s["mv_done"], c * 2 + 1)
                nc.vector.tensor_scalar(mv[:, :, 1], mv[:, :, 1], EPS, None, ALU.add).then_inc(s["mv_done"], 1)

            def inverse_deviation(c):
                dve.wait_ge(s["std_done"], c + 1)
                nc.vector.reciprocal(rstd[:], rstd[:]).then_inc(s["inv_done"], 1)

            def shift_of(c):
                dve.wait_ge(s["inv_done"], c * 2 + 1)
                nc.vector.scalar_tensor_tensor(out=mv[:, :, 0], in0=mv[:, :, 0], scalar=-1.0, in1=rstd[:],
                                               op0=ALU.mult, op1=ALU.mult).then_inc(s["inv_done"], 1)

            def chunk(c, prev, last=False):
                for h in range(H):
                    tr = c + 1 if h == H - 1 and not last else None
                    pc, ph = (c, h - 1) if h else (prev, H - 1)
                    ended = prev is not None and h == 0
                    masks(c, h, 0, (c, h, 1), c if ended else None, NQ - 1)
                    if h == 1 and prev is not None:
                        inverse_deviation(prev)
                    masks(c, h, 1, (c, h, 2), tr, 0)
                    if h == 1 and prev is not None:
                        shift_of(prev)
                    masks(c, h, 2, (c, h, 3), tr, 1)
                    if pc is not None:
                        denominator(pc, ph)
                    masks(c, h, 3, (c, h, 4), tr, 2)
                    if pc is not None:
                        inverse(pc, ph)
                    if ended:
                        masks(c, h, 4, (c, h, 5))
                        moments(prev, (0, 1))
                        masks(c, h, 5, (c, h, 6))
                        moments(prev, (2, 3))
                        masks(c, h, 6, (c, h, 7))
                        variance(prev)
                    else:
                        with dve.Fori(4, NQ - 1) as q:
                            masks(c, h, q, (c, h, q + 1), tr, q - 1)
                    masks(c, h, NQ - 1, (c, h + 1, 0) if h < H - 1 else None if last else (c + 1, 0, 0),
                          tr, NQ - 2)

            edges(0, 0, 0, 0)
            chunk(0, None)
            with dve.Fori(1, NIC - 1) as c:
                chunk(c, c - 1)
            chunk(NIC - 1, NIC - 2, last=True)
            denominator(NIC - 1, H - 1)
            inverse(NIC - 1, H - 1)

            def low_weight(i, scale):
                dve.wait_ge(w_high, i + 1)
                nc.vector.scalar_tensor_tensor(out=k.w_parts[:, i, 1, :], in0=w_sb[:, i, :], scalar=scale,
                                               in1=k.w_parts[:, i, 0, :], op0=ALU.mult, op1=ALU.subtract
                                               ).then_inc(w_low, 1)

            low_weight(0, k.s_e)
            moments(NIC - 1, range(IT))
            variance(NIC - 1)
            low_weight(1, k.s_w)
            inverse_deviation(NIC - 1)
            shift_of(NIC - 1)

        @block.gpsimd
        def _(pool):
            pool.sem_inc(s["y_added"], Y0)

            def add_head(c, h):
                hh = c * H + h
                pool.wait_ge(s["part_done"], hh * 2 + 2 + PART0)
                nc.gpsimd.tensor_tensor(out=part[:], in0=part[:], in1=part2[:], op=ALU.add).then_inc(s["sum_done"], 1)
                pool.wait_ge(s["sum_done"], hh + 1)
                pool.wait_ge(s["den_done"], hh * 2 + 2)
                nc.gpsimd.tensor_tensor(out=part[:, :, 0:DH], in0=part[:, :, 0:DH],
                                        in1=dinv[:, :, None].broadcast_to([P, IT, DH]), op=ALU.mult
                                        ).then_inc(s["pool_step"], 1)
                pool.wait_ge(s["pool_step"], hh + 1)
                if h == 0:
                    pool.wait_ge(s["y_loaded"], c * 16 + 16)
                ys = y[:, :, h * DH:(h + 1) * DH]
                nc.gpsimd.tensor_tensor(out=ys, in0=ys, in1=part[:, :, 0:DH], op=ALU.add).then_inc(s["y_added"], 1)

            with pool.Fori(0, NIC) as c:
                for h in range(H):
                    add_head(c, h)


def project1(nc, sem, k, nw, x1_dram):
    m = Map(nc, k.project_at)
    k.hT = m("hT", [P, 2, KT, N], F16, 2)
    k.v = m("v", [P, 2, NT, D], F16, 2)
    k.free = m.at
    w_parts, x_in = k.w_parts, k.x1_in
    xT = m("x1T", [P, 2, 2, KT, IC], F16, 2)
    n_bc = m("n_bc", [P, D], FP32, 4)
    prod = m("prod1", [P, IT, D], FP32, 4)
    assert m.at <= nc.sbuf_usable_end, m.at
    bank, ident, small = k.bank, k.ident, k.small
    PASSES = ((0, 0), (0, 1), (1, 0))

    steps, n_in, xT_ps, xT_high, xT_low, mm, hi, lo, prod_done, score_done, node_max, \
        node_exp, node_sum = (sem("p2_" + n) for n in (
            "steps", "n_in", "xT_ps", "xT_high", "xT_low", "mm", "hi", "lo",
            "prod_done", "score_done", "node_max", "node_exp", "node_sum"))
    passed = sem("p2_passed")
    x_loaded = [sem(f"p2_x_loaded{i}") for i in range(2)]
    x1_r = x1_dram.rearrange("(c i p) d -> p c i d", i=IT, p=P)
    NJ = KT + IT

    with nc.Block() as block:

        @block.sync
        def _(sp):
            def load_x(c2, u):
                wait_apart(sp, score_done, c2 * 2 + u + 1, passed)
                wait_apart(sp, xT_low, (c2 * 2 + u - 1) * KT + 2, passed)
                sp.dma_start(x_in[:, u, :, :], x1_r[:, bass.ds(c2 * 2 + u, 1), :, :].rearrange(
                    "p c i d -> p (c i) d")).then_inc(x_loaded[u], 16)

            sp.sem_inc(x_loaded[0], 16)
            sp.sem_inc(x_loaded[1], 16)
            sp.dma_start(n_bc[:], nw.rearrange("d o -> (d o)").partition_broadcast(P)).then_inc(n_in, 16)
            with sp.Fori(1, NIC // 2) as c2:
                for u in range(2):
                    load_x(c2, u)

        @block.gpsimd
        def _(pool):
            pool.wait_ge(node_max, 1)
            nc.gpsimd.partition_all_reduce(small[:, 1:2], small[:, 0:1], P, RMAX).then_inc(node_max, 1)
            pool.wait_ge(node_exp, 2)
            nc.gpsimd.partition_all_reduce(small[:, 4:5], small[:, 3:4], P, RADD).then_inc(node_sum, 1)

        @block.tensor
        def _(pe):
            def transposes(c2, u):
                c = c2 * 2 + u
                pe.wait_ge(x_loaded[u], c2 * 16 + 16)
                for j in range(KT):
                    pe.wait_ge(xT_low, c * KT + j + 1)
                    for i in range(IT):
                        last = nc.tensor.transpose(bank[j % 2][:, i * P:(i + 1) * P],
                                                   x_in[:, u, i, j * P:(j + 1) * P], ident[:])
                    last.then_inc(xT_ps, 1)

            def product(c2, u, j):
                c = c2 * 2 + u
                pe.wait_ge(lo, c * NJ + j + 1)
                n = 0
                for a, b in PASSES:
                    for i in range(KT):
                        if j < KT:
                            left = w_parts[:, 0, b, i * D + j * P:i * D + (j + 1) * P]
                            right = xT[:, u, a, i, :]
                        else:
                            left = xT[:, u, a, i, (j - KT) * P:(j - KT + 1) * P]
                            right = w_parts[:, 1, b, i * D:(i + 1) * D]
                        last = nc.tensor.matmul(bank[2 + j % 4][:], left, right, start=(n == 0), stop=(n == 11))
                        n += 1
                last.then_inc(mm, 1)

            def chunk(c2, u, following):
                pe.wait_ge(xT_low, (c2 * 2 + u) * KT + KT + 2)
                for j in range(NJ):
                    product(c2, u, j)
                    if j == 3 and following is not None:
                        transposes(*following)

            transposes(0, 0)
            chunk(0, 0, (0, 1))
            with pe.Fori(0, NIC // 2 - 1) as c2:
                chunk(c2, 1, (c2 + 1, 0))
                chunk(c2 + 1, 0, (c2 + 1, 1))
            chunk(NIC // 2 - 1, 1, None)

        def place(c2, u, j, part):
            c = c2 * 2 + u
            if j < KT:
                return k.hT[:, part, j, bass.ds(c * IC, IC)]
            return flat(k.v[:, part, bass.ds(c * IT + (j - KT), 1), :])

        @block.scalar
        def _(act):
            def high_x(c2, u):
                c = c2 * 2 + u
                for j in range(KT):
                    act.wait_ge(xT_ps, c * KT + j + 1)
                    nc.scalar.activation(xT[:, u, 0, j, :], bank[j % 2][:], ACT.Copy, scale=X1S
                                         ).then_inc(xT_high, 1)

            def high(c2, u, following):
                for j in range(NJ):
                    act.wait_ge(mm, (c2 * 2 + u) * NJ + j + 1)
                    nc.scalar.activation(place(c2, u, j, 0), bank[2 + j % 4][:], ACT.Copy, scale=1.0 / X1S
                                         ).then_inc(hi, 1)
                    if j == 3 and following is not None:
                        high_x(*following)

            high_x(0, 0)
            high(0, 0, (0, 1))
            with act.Fori(0, NIC // 2 - 1) as c2:
                high(c2, 1, (c2 + 1, 0))
                high(c2 + 1, 0, (c2 + 1, 1))
            high(NIC // 2 - 1, 1, None)
            act.wait_ge(node_max, 3)
            nc.scalar.activation(k.score[:], k.score[:], ACT.Exp, bias=small[:, 2:3],
                                 accum_out=small[:, 3:4]).then_inc(node_exp, 2)

        @block.vector
        def _(dve):
            dve.sem_inc(lo, 4)
            dve.sem_inc(score_done, 2)
            dve.sem_inc(xT_low, 2)
            link = linker(nc, dve, steps)

            def low_x(c2, u):
                c = c2 * 2 + u
                for j in range(KT):
                    dve.wait_ge(xT_high, c * KT + j + 1)
                    nc.vector.scalar_tensor_tensor(out=xT[:, u, 1, j, :], in0=bank[j % 2][:], scalar=X1S,
                                                   in1=xT[:, u, 0, j, :], op0=ALU.mult, op1=ALU.subtract
                                                   ).then_inc(xT_low, 1)

            def chunk(c2, u, following):
                c = c2 * 2 + u
                dve.wait_ge(x_loaded[u], c2 * 16 + 16)
                for i in range(IT):
                    last = nc.vector.tensor_tensor(out=prod[:, i, :], in0=x_in[:, u, i, :], in1=n_bc[:], op=ALU.mult)
                last.then_inc(prod_done, 1)
                for j in range(NJ):
                    dve.wait_ge(hi, c * NJ + j + 1)
                    nc.vector.scalar_tensor_tensor(out=place(c2, u, j, 1), in0=bank[2 + j % 4][:],
                                                   scalar=1.0 / X1S, in1=place(c2, u, j, 0),
                                                   op0=ALU.mult, op1=ALU.subtract).then_inc(lo, 1)
                    if j == 1:
                        dve.wait_ge(prod_done, c + 1)
                        nc.vector.tensor_reduce(out=k.score[:, bass.ds(c * IT, IT)], in_=prod[:], axis=AX.X,
                                                op=ALU.add).then_inc(score_done, 1)
                    if j == 3 and following is not None:
                        low_x(*following)

            low_x(0, 0)
            dve.wait_ge(n_in, 16)
            chunk(0, 0, (0, 1))
            with dve.Fori(0, NIC // 2 - 1) as c2:
                chunk(c2, 1, (c2 + 1, 0))
                chunk(c2 + 1, 0, (c2 + 1, 1))
            chunk(NIC // 2 - 1, 1, None)
            dve.wait_ge(score_done, NIC + 2)
            link(lambda v: v.tensor_reduce(out=small[:, 0:1], in_=k.score[:], axis=AX.X, op=ALU.max))
            dve.sem_inc(node_max, 1)
            dve.wait_ge(node_max, 2)
            link(lambda v: v.tensor_scalar(small[:, 2:3], small[:, 1:2], -1.0, None, ALU.mult))
            dve.sem_inc(node_max, 1)
            dve.wait_ge(node_sum, 1)
            link(lambda v: v.reciprocal(small[:, 5:6], small[:, 4:5]))
            link(lambda v: v.tensor_scalar(k.score[:], k.score[:], small[:, 5:6], k.inv_w, ALU.mult, ALU.mult))


def attend1(nc, sem, k, adj, b1, x1_dram, e_dram, out):
    m = Map(nc, k.at)
    pr = m("pr", [P, 2, N], FP32, 4)
    neg = m("neg", [P, N // IC, IC], FP32, 4)
    assert m.at <= k.project_at, m.at
    m = Map(nc, k.free)
    pT = m("pT", [P, 2, 2, IC], F16, 2)
    e_row = m("e_row", [P, 2, IC], FP32, 4)
    e_col = m("e_col", [P, 2, IT, P], FP32, 4)
    xr = m("xr", [P, 2, D], FP32, 4)
    bias = m("bias1", [P, D], FP32, 4)
    cmax = m("cmax", [P, 2, 8], FP32, 4)
    st = m("st1", [P, 2, 17], FP32, 4)
    assert m.at <= nc.sbuf_usable_end, m.at
    bank, ident, hT, v = k.bank, k.ident, k.hT, k.v
    NC = N // IC
    names = ("qk", "s_done", "max_done", "bias_done", "exp_done", "coef_done",
             "pT_ps", "hi", "lo", "pv", "x_biased", "sum_done", "stat_done", "mv_done", "std_done", "inv_done",
             "norm_done", "b_in", "e_saved", "eT_ps", "eT_out")
    s = {n: sem("a1_" + n) for n in names}
    passed = [sem(f"a1_passed{i}") for i in range(3)]
    neg_in = [sem(f"a1_neg_in{i}") for i in range(NC)]
    neg_done = [sem(f"a1_neg_done{i}") for i in range(NC)]
    e_stored = [sem(f"a1_e_stored{i}") for i in range(2)]
    e_in = [sem(f"a1_e_in{i}") for i in range(2)]
    x_in = [sem(f"a1_x_in{i}") for i in range(2)]
    o_out = [sem(f"a1_o_out{i}") for i in range(2)]
    S0, ET0, OUT0 = 1, 1, 1
    adj_r = adj.rearrange("(t p) n -> p t n", p=P)
    x1_r = x1_dram.rearrange("(t p) d -> p t d", p=P)
    out_r = out.rearrange("(t p) d -> p t d", p=P)
    e_r = e_dram.rearrange("(t p) n -> p t n", p=P)
    eT_r = e_dram.rearrange("(c i p) n -> p c i n", i=IT, p=P)

    def total_before(t, R, per):
        return (t * per(R)) + (IT * sum(per(r) for r in range(R)) - IT * R * per(R))

    def computed(R):
        return NC - R

    def turned(R):
        return NC - 1 - R

    def stored_in(j):
        return lambda R: (NC - R - j) // 2

    def lag(n):
        return min(2, n)

    def run_groups(engine, step):
        for t in range(IT):
            step(t, t % 2, 0)
        for R in range(1, NC):
            with engine.Fori(2 * R, 2 * R + 2) as i2:
                for u in range(2):
                    step(i2 * 2 + u, u, R)

    with nc.Block() as block:

        @block.sync
        def _(sp):
            sp.dma_start(bias[:], b1.partition_broadcast(P)).then_inc(s["b_in"], 16)

            def load_neg(t, c):
                sp.dma_start(neg[:, c:c + 1, :], adj_r[:, bass.ds(t, 1), c * IC:(c + 1) * IC]
                             ).then_inc(neg_in[c], 16)

            for c in range(NC):
                load_neg(0, c)

            def rows(t, u):
                if not isinstance(t, int) or t >= 2:
                    wait_apart(sp, s["norm_done"], t + 1, passed[0])
                    sp.dma_start(out_r[:, bass.ds(t - 2, 1), :], xr[:, u:u + 1, :]).then_inc(o_out[u], 16)
                    wait_apart(sp, o_out[u], (t - u) * 8, passed[0])
                sp.dma_start(xr[:, u:u + 1, :], x1_r[:, bass.ds(t, 1), :]).then_inc(x_in[u], 16)

            def step(t, u, R, last=False):
                n = computed(R)
                if R:
                    for j in range(2):
                        sp.wait_ge(e_stored[j], 16 * total_before(IT * R, R, stored_in(j)))
                    wait_apart(sp, s["pT_ps"], (t - 1) * NC, passed[0])
                    sp.dma_start(pr[:, u:u + 1, 0:R * IC], e_r[:, bass.ds(t, 1), 0:R * IC]).then_inc(e_in[u], 16)
                for i in range(NC + 1):
                    if i < NC:
                        c = (R + i) % NC
                        if i == 6:
                            rows(t, u)
                        if not last:
                            wait_apart(sp, s["s_done"], t * NC + i + 1 + S0, passed[0])
                            load_neg(t + 1, c)
                    if 2 <= i <= n:
                        wait_apart(sp, s["eT_out"], total_before(t, R, turned) + i - 1 + OUT0, passed[0])
                        sp.dma_start(eT_r[:, R + i - 1, :, bass.ds(t * P, P)], e_col[:, i % 2, :, :]
                                     ).then_inc(e_stored[i % 2], 16)

            for t in range(IT):
                step(t, t % 2, 0)
            for R in range(1, NC - 1):
                with sp.Fori(2 * R, 2 * R + 2) as i2:
                    for u in range(2):
                        step(i2 * 2 + u, u, R)
            for t in range(NT - IT, NT):
                step(t, t % 2, NC - 1, last=(t == NT - 1))
            for u in range(2):
                sp.wait_ge(s["norm_done"], NT + u + 1)
                sp.dma_start(out_r[:, NT - 2 + u, :], xr[:, u, :]).then_inc(o_out[u], 16)
            for u in range(2):
                sp.wait_ge(o_out[u], NT // 2 * 16)
                sp.wait_ge(e_stored[u], 16 * total_before(NT, NC, stored_in(u)))

        @block.gpsimd
        def _(pool):
            pool.wait_ge(s["b_in"], 16)

            def to_mask(t, c):
                wait_apart(pool, neg_in[c], t * 16 + 16, passed[1])
                nc.gpsimd.tensor_scalar(neg[:, c, :], neg[:, c, :], -1.0, BIG, ALU.add, ALU.mult
                                        ).then_inc(neg_done[c], 1)

            def step(t, u, R, last=False):
                if not last:
                    for i in range(NC):
                        to_mask(t + 1, (R + i) % NC)
                pool.wait_ge(x_in[u], (t - u) * 8 + 16)
                nc.gpsimd.tensor_tensor(out=xr[:, u, :], in0=xr[:, u, :], in1=bias[:], op=ALU.add
                                        ).then_inc(s["x_biased"], 1)

            for c in range(NC):
                to_mask(0, c)
            for t in range(IT):
                step(t, t % 2, 0)
            for R in range(1, NC - 1):
                with pool.Fori(2 * R, 2 * R + 2) as i2:
                    for u in range(2):
                        step(i2 * 2 + u, u, R)
            for t in range(NT - IT, NT):
                step(t, t % 2, NC - 1, last=(t == NT - 1))

        @block.tensor
        def _(pe):
            pe.sem_inc(s["eT_ps"], ET0)

            def logits(t, R, i):
                pe.wait_ge(s["s_done"], t * NC + max(i - 2, 0) + S0)
                c, n = R + i, 0
                for a, b in ((0, 0), (0, 1), (1, 0)):
                    for j in range(KT):
                        last = nc.tensor.matmul(bank[i % 3][:], hT[:, a, j, bass.ds(t * P, P)],
                                                hT[:, b, j, c * IC:(c + 1) * IC], start=(n == 0), stop=(n == 11))
                        n += 1
                last.then_inc(s["qk"], 1)

            def turn(t, R, i):
                before = total_before(t, R, turned) + i - 1
                pe.wait_ge(s["e_saved"], before + 1)
                pe.wait_ge(s["eT_out"], before + OUT0)
                for j in range(IT):
                    last = nc.tensor.transpose(bank[3][:, j * P:(j + 1) * P], e_row[:, i % 2, j * P:(j + 1) * P],
                                               ident[:])
                last.then_inc(s["eT_ps"], 1)

            def transposes(t, u, g):
                pe.wait_ge(s["exp_done"], t * 2 + 1 + g // (NC // 2))
                pe.wait_ge(s["lo"], t * NC + g + 1)
                for j in range(4):
                    last = nc.tensor.transpose(bank[4 + g % 2][:, j * P:(j + 1) * P],
                                               pr[:, u, (g * 4 + j) * P:(g * 4 + j + 1) * P], ident[:])
                last.then_inc(s["pT_ps"], 1)

            def values(t, u, g):
                pe.wait_ge(s["lo"], t * NC + g + 3)
                if g == 0:
                    pe.wait_ge(s["sum_done"], t + 1)
                for j in range(4):
                    for a, b in ((0, 0), (0, 1), (1, 0)):
                        last = nc.tensor.matmul(bank[6 + u][:], pT[:, g % 2, a, j * P:(j + 1) * P],
                                                v[:, b, g * 4 + j, :], start=(g == 0 and j == 0 and a == b),
                                                stop=(g == NC - 1 and j == 3 and a == 1))
                last.then_inc(s["pv"], 1)

            def step(t, u, R):
                n = computed(R)
                for i in range(NC + lag(n) + 1):
                    if i < n:
                        logits(t, R, i)
                    if 2 <= i <= n:
                        turn(t, R, i - 1)
                    if isinstance(t, int) and t == 0:
                        continue
                    g = i - lag(n)
                    if 0 <= g < NC:
                        transposes(t - 1, 1 - u, g)
                    if 1 <= g:
                        values(t - 1, 1 - u, g - 1)

            run_groups(pe, step)
            step(NT, 0, NC)

        @block.scalar
        def _(act):
            act.sem_inc(s["pv"], 2)
            act.sem_inc(s["eT_out"], OUT0)

            def exps(t, u, half):
                if half == 0:
                    act.wait_ge(s["bias_done"], t + 1)
                e, col = pr[:, u, half * (N // 2):(half + 1) * (N // 2)], (2, 16)[half]
                nc.scalar.activation(e, e, ACT.Exp, bias=st[:, u, 1:2], scale=k.inv_e2,
                                     accum_out=st[:, u, col:col + 1]).then_inc(s["exp_done"], 1)

            def save(t, R, i):
                act.wait_ge(s["s_done"], t * NC + i + 1 + S0)
                act.wait_ge(s["eT_ps"], total_before(t, R, turned) + max(i - 2, 0) + ET0)
                nc.scalar.activation(e_row[:, i % 2, :], bank[i % 3][:], ACT.Copy).then_inc(s["e_saved"], 1)

            def unload(t, R, i):
                act.wait_ge(s["eT_ps"], total_before(t, R, turned) + i + ET0)
                j = (i + 1) % 2
                if not isinstance(t, int) or t > 0 or i > 2:
                    act.wait_ge(e_stored[j], 16 * (total_before(t, R, stored_in(j)) + (i - 1) // 2))
                nc.scalar.activation(e_col[:, j, :, :].rearrange("p i n -> p (i n)"), bank[3][:], ACT.Copy
                                     ).then_inc(s["eT_out"], 1)

            def high(t, u, g):
                act.wait_ge(s["pT_ps"], t * NC + g + 1)
                act.wait_ge(s["pv"], t * NC + g + 1)
                nc.scalar.activation(pT[:, g % 2, 0, :], bank[4 + g % 2][:], ACT.Copy).then_inc(s["hi"], 1)

            def deviation(t, u):
                act.wait_ge(s["mv_done"], t * 2 + 2)
                nc.scalar.activation(st[:, u, 13:14], st[:, u, 12:13], ACT.Sqrt).then_inc(s["std_done"], 1)

            def step(t, u, R):
                n = computed(R)
                after_first, after_second = (not isinstance(t, int) or t >= i for i in (1, 2))
                if after_first:
                    exps(t - 1, 1 - u, 0)
                for i in range(NC + lag(n)):
                    if 1 <= i < n:
                        save(t, R, i)
                    if 2 <= i <= n:
                        unload(t, R, i - 1)
                    g = i - lag(n)
                    if 0 <= g and after_first:
                        high(t - 1, 1 - u, g)
                        if g == 1:
                            exps(t - 1, 1 - u, 1)
                    if g == 1 and after_second:
                        deviation(t - 2, u)

            run_groups(act, step)
            step(NT, 0, NC)
            deviation(NT - 1, 1)

        @block.vector
        def _(dve):
            dve.sem_inc(s["s_done"], S0)
            dve.sem_inc(s["lo"], 2)
            dve.sem_inc(s["norm_done"], 2)
            dve.sem_inc(s["sum_done"], 2)

            def mask_chunk(t, u, R, i):
                c = (R + i) % NC
                dve.wait_ge(neg_done[c], t + 1)
                if i < computed(R):
                    wait_apart(dve, s["qk"], total_before(t, R, computed) + i + 1, passed[2])
                    e = bank[i % 3][:]
                else:
                    wait_apart(dve, e_in[u], (t - u) * 8 - 16, passed[2])
                    e = pr[:, u, c * IC:(c + 1) * IC]
                nc.vector.tensor_tensor_reduce(out=pr[:, u, c * IC:(c + 1) * IC], in0=e, in1=neg[:, c, :], scale=1.0,
                                               scalar=-3.3e38, op0=ALU.add, op1=ALU.max,
                                               accum_out=cmax[:, u, c:c + 1]).then_inc(s["s_done"], 1)

            def row_max(t, u):
                dve.wait_ge(s["s_done"], t * NC + NC + S0)
                nc.vector.tensor_reduce(out=st[:, u, 0:1], in_=cmax[:, u, :], axis=AX.X, op=ALU.max
                                        ).then_inc(s["max_done"], 1)
                dve.wait_ge(s["max_done"], t * 3 + 1)
                nc.vector.tensor_scalar(st[:, u, 3:4], st[:, u, 0:1], k.inv_e2, -1.0, ALU.mult, ALU.mult
                                        ).then_inc(s["max_done"], 1)
                dve.wait_ge(s["max_done"], t * 3 + 2)
                nc.vector.tensor_scalar(st[:, u, 1:2], st[:, u, 3:4], PSCALE, None, ALU.add
                                        ).then_inc(s["bias_done"], 1)
                nc.vector.tensor_scalar(st[:, u, 4:5], st[:, u, 0:1], -1.0e38, k.score[:, bass.ds(t, 1)],
                                        ALU.is_gt, ALU.mult).then_inc(s["max_done"], 1)

            def low(t, u, g):
                dve.wait_ge(s["hi"], t * NC + g + 1)
                nc.vector.tensor_tensor(out=pT[:, g % 2, 1, :], in0=bank[4 + g % 2][:], in1=pT[:, g % 2, 0, :],
                                        op=ALU.subtract).then_inc(s["lo"], 1)

            def coef(t, u):
                dve.wait_ge(s["exp_done"], t * 2 + 2)
                dve.wait_ge(s["max_done"], t * 3 + 3)
                nc.vector.tensor_tensor(out=st[:, u, 5:6], in0=st[:, u, 2:3], in1=st[:, u, 16:17], op=ALU.add
                                        ).then_inc(s["coef_done"], 1)
                dve.wait_ge(s["coef_done"], t * 3 + 1)
                nc.vector.reciprocal(st[:, u, 5:6], st[:, u, 5:6]).then_inc(s["coef_done"], 1)
                dve.wait_ge(s["coef_done"], t * 3 + 2)
                nc.vector.tensor_scalar(st[:, u, 5:6], st[:, u, 5:6], st[:, u, 4:5], None, ALU.mult
                                        ).then_inc(s["coef_done"], 1)

            def total(t, u):
                dve.wait_ge(s["pv"], t * NC + NC + 2)
                dve.wait_ge(s["coef_done"], t * 3 + 3)
                dve.wait_ge(s["x_biased"], t + 1)
                nc.vector.scalar_tensor_tensor(out=xr[:, u, :], in0=bank[6 + u][:], scalar=st[:, u, 5:6],
                                               in1=xr[:, u, :], op0=ALU.mult, op1=ALU.add).then_inc(s["sum_done"], 1)
                dve.wait_ge(s["sum_done"], t + 3)
                nc.vector.bn_stats(st[:, u, 6:12], xr[:, u, :]).then_inc(s["stat_done"], 1)
                wait_apart(dve, s["stat_done"], t + 1, passed[2])
                nc.vector.bn_aggr(st[:, u, 14:16], st[:, u, 6:12]).then_inc(s["mv_done"], 1)
                dve.wait_ge(s["mv_done"], t * 2 + 1)
                nc.vector.tensor_scalar(st[:, u, 12:13], st[:, u, 15:16], EPS, None, ALU.add
                                        ).then_inc(s["mv_done"], 1)

            def normalize(t, u):
                dve.wait_ge(s["std_done"], t + 1)
                nc.vector.reciprocal(st[:, u, 13:14], st[:, u, 13:14]).then_inc(s["inv_done"], 1)
                dve.wait_ge(s["inv_done"], t + 1)
                nc.vector.tensor_scalar(xr[:, u, :], xr[:, u, :], st[:, u, 14:15], st[:, u, 13:14],
                                        ALU.subtract, ALU.mult).then_inc(s["norm_done"], 1)

            def step(t, u, R):
                n = computed(R)
                after_first, after_second = (not isinstance(t, int) or t >= i for i in (1, 2))
                masked = 0
                for i in range(NC + lag(n)):
                    if i < n:
                        mask_chunk(t, u, R, i)
                        masked += 1
                    elif i >= 4 and R < NC:
                        for _ in range(min(1 if R < 5 else 2, NC - masked)):
                            mask_chunk(t, u, R, masked)
                            masked += 1
                    if i == 0 and after_second:
                        total(t - 2, u)
                    if i == lag(n) + 3:
                        if after_first:
                            coef(t - 1, 1 - u)
                        if after_second:
                            normalize(t - 2, u)
                    g = i - lag(n)
                    if 0 <= g and after_first:
                        low(t - 1, 1 - u, g)
                    if masked == NC:
                        row_max(t, u)
                        masked += 1

            run_groups(dve, step)
            step(NT, 0, NC)
            total(NT - 1, 1)
            normalize(NT - 1, 1)


_INS = ["x", "adj", "L0_gnn_weight", "L0_gnn_weight_u", "L0_gnn_weight_v", "L0_gnn_bias", "L0_gnn_proj_w",
        "L0_gnn_proj_b", "L1_gnn_weight", "L1_gnn_bias", "L1_gnn_node_w", "L1_gnn_edge_w"]


def kernel(**inputs):
    import numpy as _np
    import concourse.bacc as _bacc
    from concourse import mybir as _mybir
    from concourse.bass_utils import run_bass_kernel_spmd as _run

    nc = _bacc.Bacc("TRN2", target_bir_lowering=False, num_devices=1)
    arrays, args = {}, []
    for name in _INS:
        a = _np.ascontiguousarray(inputs[name])
        arrays[f"in_{name}_dram"] = a
        args.append(nc.dram_tensor(f"in_{name}_dram", a.shape, _mybir.dt.from_np(a.dtype), kind="ExternalInput").ap())
    args.append(nc.dram_tensor("out_0_dram", (N, D), FP32, kind="ExternalOutput").ap())
    build(nc, *args)
    r = _run(nc, [arrays], core_ids=[0])
    return r.results[0]["out_0_dram"]
```
